# Optimizing a Trainium2 kernel written in Bass

```python
import numpy as np
import jax
import jax.numpy as jnp

def _softmax(x, axis=-1):
    return jax.nn.softmax(x, axis=axis)

def _gelu(x):
    return jax.nn.gelu(x, approximate=True)

def _silu(x):
    return jax.nn.silu(x)

def _sigmoid(x):
    return jax.nn.sigmoid(x)

def _layernorm(x, axis=-1, eps=1e-05):
    m = jnp.mean(x, axis=axis, keepdims=True)
    v = jnp.var(x, axis=axis, keepdims=True)
    return (x - m) / jnp.sqrt(v + eps)

def _scatter_add(tgt, idx, src, axis=0):
    return tgt.at[idx].add(src)

def _segment_sum(src, seg, n):
    return jax.ops.segment_sum(src, seg, n)
kernel_name = 'mk_seq_preln_d1_jaxref_r8_9f6566'

def setup_inputs(seed: int=0):
    np.random.seed(seed)
    _w = jnp.asarray

    def _L0_attn_setup():
        import jax, jax.numpy as jnp
        import numpy as np
        DIM = 128
        HEADS = 16
        HEAD_DIM = DIM // HEADS
        B, S = (4, 512)
        key = jax.random.key(seed)
        ks = jax.random.split(key, 8)
        sc = 1.0 / np.sqrt(DIM)
        return {'x': jax.random.normal(ks[0], (B, S, DIM), dtype=jnp.float32), 'Wq': jax.random.normal(ks[1], (DIM, DIM), dtype=jnp.float32) * sc, 'Wk': jax.random.normal(ks[2], (DIM, DIM), dtype=jnp.float32) * sc, 'Wv': jax.random.normal(ks[3], (DIM, DIM), dtype=jnp.float32) * sc, 'Wp': jax.random.normal(ks[4], (DIM, DIM), dtype=jnp.float32) * sc, 'bp': jnp.zeros((DIM,), dtype=jnp.float32), 'conv_w': jax.random.normal(ks[5], (DIM, 3), dtype=jnp.float32) * (1.0 / np.sqrt(3.0)), 'conv_b': jnp.zeros((DIM,), dtype=jnp.float32)}
    _L0_attn_in = _L0_attn_setup()

    def _L0_ffn_setup():
        import jax, jax.numpy as jnp
        import numpy as np
        B, L, D = (1, 256, 128)
        E, H, G, K = (64, 32, 64, 16)

        def _grouped_routing_scores(router_scores):
            T, En = router_scores.shape
            Tq = T // G
            budget = Tq * K
            order = jnp.argsort(-router_scores, axis=0)
            sorted_vals = jnp.take_along_axis(router_scores, order, axis=0)
            group_score = sorted_vals.reshape(Tq, G, En).sum(axis=1)
            _, top_flat = jax.lax.top_k(group_score.reshape(-1), budget)
            gmask = jnp.zeros((Tq * En,), bool).at[top_flat].set(True).reshape(Tq, En)
            mask_sorted = jnp.broadcast_to(gmask[:, None, :], (Tq, G, En)).reshape(T, En)
            mask = jnp.zeros((T, En), bool).at[order, jnp.arange(En)[None, :]].set(mask_sorted)
            fs = jnp.where(mask, router_scores, 0.0)
            return fs / (fs.sum(axis=-1, keepdims=True) + 1e-06)
        key = jax.random.key(seed)
        ks = jax.random.split(key, 6)
        s = lambda k, shape, scale: jax.random.normal(k, shape, jnp.float32) * scale
        return {'x': jax.random.normal(ks[0], (B, L, D), jnp.float32), 'Wr': s(ks[1], (D, E), D ** (-0.5)), 'br': jnp.zeros((E,), jnp.float32), 'Wup': s(ks[2], (E, D, H), D ** (-0.5)), 'bup': jnp.zeros((E, H), jnp.float32), 'Wgate': s(ks[3], (E, D, H), D ** (-0.5)), 'bgate': jnp.zeros((E, H), jnp.float32), 'Wdown': s(ks[4], (E, H, D), H ** (-0.5)), 'bdown': jnp.zeros((E, D), jnp.float32)}
    _L0_ffn_in = _L0_ffn_setup()
    _d = {'L0_attn_x': _L0_attn_in['x'], 'L0_attn_Wq': _L0_attn_in['Wq'], 'L0_attn_Wk': _L0_attn_in['Wk'], 'L0_attn_Wv': _L0_attn_in['Wv'], 'L0_attn_Wp': _L0_attn_in['Wp'], 'L0_attn_bp': _L0_attn_in['bp'], 'L0_attn_conv_w': _L0_attn_in['conv_w'], 'L0_attn_conv_b': _L0_attn_in['conv_b'], 'L0_ffn_Wr': _L0_ffn_in['Wr'], 'L0_ffn_br': _L0_ffn_in['br'], 'L0_ffn_Wup': _L0_ffn_in['Wup'], 'L0_ffn_bup': _L0_ffn_in['bup'], 'L0_ffn_Wgate': _L0_ffn_in['Wgate'], 'L0_ffn_bgate': _L0_ffn_in['bgate'], 'L0_ffn_Wdown': _L0_ffn_in['Wdown'], 'L0_ffn_bdown': _L0_ffn_in['bdown']}
    _x0 = _d['L0_attn_x']
    _d['L0_attn_x'] = jax.random.normal(jax.random.fold_in(jax.random.key(seed), 1), (16, 512, 128), dtype=_x0.dtype)
    del _x0
    return _d

def reference(L0_attn_x, L0_attn_Wq, L0_attn_Wk, L0_attn_Wv, L0_attn_Wp, L0_attn_bp, L0_attn_conv_w, L0_attn_conv_b, L0_ffn_Wr, L0_ffn_br, L0_ffn_Wup, L0_ffn_bup, L0_ffn_Wgate, L0_ffn_bgate, L0_ffn_Wdown, L0_ffn_bdown):

    def _L0_attn_ref(x, Wq, Wk, Wv, Wp, bp, conv_w, conv_b):
        import jax, jax.numpy as jnp
        import numpy as np
        DIM = 128
        HEADS = 16
        HEAD_DIM = DIM // HEADS
        B, S = (4, 512)
        b, s, d = x.shape

        def split_heads(t):
            return t.reshape(b, s, HEADS, HEAD_DIM).transpose(0, 2, 1, 3)
        q = split_heads(x @ Wq.T)
        k = split_heads(x @ Wk.T)
        v = split_heads(x @ Wv.T)
        q = jax.nn.elu(q) + 1.0
        k = jax.nn.elu(k) + 1.0
        kv_state = jnp.einsum('bhnd,bhne->bhde', k, v)
        k_state = k.sum(axis=2)
        attn_out = jnp.einsum('bhnd,bhde->bhne', q, kv_state)
        denom = jnp.maximum(jnp.einsum('bhnd,bhd->bhn', q, k_state), 1e-06)[..., None]
        attn_out = (attn_out / denom).transpose(0, 2, 1, 3).reshape(b, s, d)
        xp = jnp.pad(x, ((0, 0), (1, 1), (0, 0)))
        local = xp[:, :-2, :] * conv_w[:, 0] + xp[:, 1:-1, :] * conv_w[:, 1] + xp[:, 2:, :] * conv_w[:, 2] + conv_b
        return (attn_out + local) @ Wp.T + bp

    def _L0_ffn_ref(x, Wr, br, Wup, bup, Wgate, bgate, Wdown, bdown):
        import jax, jax.numpy as jnp
        import numpy as np
        B, L, D = (1, 256, 128)
        E, H, G, K = (64, 32, 64, 16)

        def _grouped_routing_scores(router_scores):
            T, En = router_scores.shape
            Tq = T // G
            budget = Tq * K
            order = jnp.argsort(-router_scores, axis=0)
            sorted_vals = jnp.take_along_axis(router_scores, order, axis=0)
            group_score = sorted_vals.reshape(Tq, G, En).sum(axis=1)
            _, top_flat = jax.lax.top_k(group_score.reshape(-1), budget)
            gmask = jnp.zeros((Tq * En,), bool).at[top_flat].set(True).reshape(Tq, En)
            mask_sorted = jnp.broadcast_to(gmask[:, None, :], (Tq, G, En)).reshape(T, En)
            mask = jnp.zeros((T, En), bool).at[order, jnp.arange(En)[None, :]].set(mask_sorted)
            fs = jnp.where(mask, router_scores, 0.0)
            return fs / (fs.sum(axis=-1, keepdims=True) + 1e-06)
        Bx, Lx, Dx = x.shape
        xt = x.reshape(-1, Dx)
        router_scores = jax.nn.softmax(xt @ Wr + br, axis=-1)
        fs = _grouped_routing_scores(router_scores)
        up = jnp.einsum('td,edh->teh', xt, Wup) + bup
        gate = jnp.einsum('td,edh->teh', xt, Wgate) + bgate
        h = jax.nn.silu(up) * gate * fs[:, :, None]
        out = jnp.einsum('teh,ehd->td', h, Wdown) + fs @ bdown
        return out.reshape(Bx, Lx, Dx)
    x = L0_attn_x
    x = x + _L0_attn_ref(_layernorm(x, axis=-1), L0_attn_Wq, L0_attn_Wk, L0_attn_Wv, L0_attn_Wp, L0_attn_bp, L0_attn_conv_w, L0_attn_conv_b)
    x = x + _L0_ffn_ref(_layernorm(x, axis=-1), L0_ffn_Wr, L0_ffn_br, L0_ffn_Wup, L0_ffn_bup, L0_ffn_Wgate, L0_ffn_bgate, L0_ffn_Wdown, L0_ffn_bdown)
    return x

_drawn_inputs = setup_inputs


def setup_inputs(seed=0):
    import zlib

    import numpy as np

    out = dict(_drawn_inputs(seed))
    spreads = {'L0_attn_bp': (0.0, 0.1),
     'L0_attn_conv_b': (0.0, 0.1),
     'L0_ffn_br': (0.0, 0.368),
     'L0_ffn_bup': (0.0, 0.652),
     'L0_ffn_bgate': (0.0, 0.659),
     'L0_ffn_bdown': (0.0, 0.395)}
    factors = {'L0_attn_Wq': 5.029, 'L0_attn_Wk': 2.685}
    for name, (base, spread) in spreads.items():
        noise = np.random.default_rng([zlib.crc32(name.encode()), seed]).standard_normal(out[name].shape)
        drawn = base * np.exp(spread * noise) if base else spread * noise
        out[name] = jnp.asarray(drawn.astype(out[name].dtype))
    for name, factor in factors.items():
        out[name] = (out[name] * factor).astype(out[name].dtype)
    return out
```

```python
from contextlib import ExitStack

import concourse.bass as bass
from concourse import mybir

F32 = mybir.dt.float32
F32R = mybir.dt.float32r
I32 = mybir.dt.int32
ALU = mybir.AluOpType
ACT = mybir.ActivationFunctionType
AX_X = mybir.AxisListType.X

P = 128
BATCH, SEQ = 16, 512
TOK = BATCH * SEQ
TT = SEQ // P
NT = TOK // P
HEADS, HD = 16, 8
E, H = 64, 32
CH = E * H // P
EPC = P // H
GROUP, KEEP = 64, 16
NG = TOK // GROUP
BUDGET = NG * KEEP
HALF = TOK // 2
HB = BATCH // 2
LN_EPS = 1e-5
DEN_EPS = 1e-6

C_ID, C_BLOCK, C_ONES, C_PAIR, C_FIRST, C_TRI, C_HEAD, C_SEL = 0, 128, 256, 384, 512, 640, 704, 720
C_END = C_SEL + CH * P
V_CONV, V_CONVB, V_BUP, V_BGATE = 0, 3, 4, 4 + CH
V_END = 4 + 2 * CH


ONE = 1


def start_semaphores(nc, sems, zeros=()):
    with nc.Block() as block:
        @block.vector
        def _(dve):
            for s in zeros:
                dve.sem_clear(s)

        @block.sync
        def _(sp):
            for s in sems[0::3]:
                sp.sem_clear(s)
                sp.sem_inc(s, ONE)

        @block.scalar
        def _(act):
            for s in sems[1::3]:
                act.sem_clear(s)
                act.sem_inc(s, ONE)

        @block.tensor
        def _(pe):
            for s in sems[2::3]:
                pe.sem_clear(s)
                pe.sem_inc(s, ONE)


def fold_statistics(dve, st, tmp, mean, chain):
    dve.tensor_tensor(tmp[:, 0, :], st[:, :, 1], st[:, :, 4], ALU.add).then_inc(chain, 1)
    dve.tensor_tensor(tmp[:, 1, :], st[:, :, 1], st[:, :, 4], ALU.subtract).then_inc(chain, 1)
    dve.tensor_tensor(tmp[:, 2, :], st[:, :, 2], st[:, :, 5], ALU.add).then_inc(chain, 1)
    dve.wait_ge(chain, ONE + 3)
    dve.tensor_scalar(mean[:, :], tmp[:, 0, :], 0.5, None, ALU.mult).then_inc(chain, 1)
    dve.tensor_tensor(tmp[:, 3, :], tmp[:, 1, :], tmp[:, 1, :], ALU.mult).then_inc(chain, 1)
    dve.wait_ge(chain, ONE + 5)
    dve.scalar_tensor_tensor(tmp[:, 4, :], tmp[:, 3, :], P / 4.0, tmp[:, 2, :], ALU.mult, ALU.add).then_inc(chain, 1)


def attention_phase(nc, x, wqT, wkvT, wpT, bp, cst, par, xres, st):
    sems = []
    with ExitStack() as ctx:
        def sb(name, shape, dt=F32):
            return ctx.enter_context(nc.sbuf_tensor(name, shape, dt))

        def sb2(name, shape, dt=F32):
            return [sb(f"{name}{u}", shape, dt) for u in range(2)]

        def ps2(name, shape):
            return [ctx.enter_context(nc.psum_tensor(f"{name}{u}", shape, F32)) for u in range(2)]

        def sem(name):
            sems.append(ctx.enter_context(nc.semaphore(name)))
            return sems[-1]

        def sem2(name):
            return [sem(f"{name}{u}") for u in range(2)]

        wq_sb = sb("wq_sb", [P, P])
        wkv_sb = sb("wkv_sb", [P, 2 * P])
        wp_sb = sb("wp_sb", [P, P])
        bp_sb = sb("bp_sb", [1, P])
        rstd = sb("rstd", [P, NT])
        std = sb("std", [P, NT])
        tmp = sb("tmp", [P, 5, NT])
        mean = sb("mean", [P, NT])
        x2s = sb2("x2s", [P, TT, P])
        bst = sb2("bst", [P, TT, 6])
        stat = sb2("stat", [P, 2, TT])
        xn = sb2("xn", [P, TT, P])
        xnT = sb2("xnT", [P, SEQ + 2])
        eq = sb2("eq", [P, SEQ])
        rq = sb2("rq", [P, SEQ])
        ek = sb2("ek", [P, TT, P])
        rk = sb2("rk", [P, TT, P])
        qT = sb2("qT", [P, SEQ])
        kk = sb2("kk", [P, TT, P])
        v1 = sb2("v1", [P, TT, P + 1])
        loc0 = sb2("loc0", [P, SEQ])
        loc1 = sb2("loc1", [P, SEQ])
        loc2 = sb2("loc2", [P, SEQ])
        kvs = sb2("kvs", [P, P + HEADS])
        den = sb2("den", [P, TT, HEADS])
        rden = sb2("rden", [P, TT, HEADS])
        att = sb2("att", [P, TT, P])
        yT = sb2("yT", [P, SEQ])
        psT = ps2("psT", [P, SEQ])
        psQ = ps2("psQ", [P, SEQ])
        psKV = ps2("psKV", [P, TT, 2 * P])

        x_in = [sem(f"x_in{k}") for k in range(4)]
        w_in = sem("w_in")
        staged = sem2("staged")
        bn1_done = sem2("bn1_done")
        st1_done = sem2("st1_done")
        st2_done = sem2("st2_done")
        var_done = sem("var_done")
        x2_kept = sem2("x2_kept")
        std_done = sem("std_done")
        rstd_done = sem("rstd_done")
        pads_done = sem("pads_done")
        stat_done = sem2("stat_done")
        xn_ready = sem2("xn_ready")
        xT_ps = sem2("xT_ps")
        xnT_ready = sem2("xnT_ready")
        q_ps = sem2("q_ps")
        kv_ps = sem2("kv_ps")
        q_act = sem2("q_act")
        kv_act = sem2("kv_act")
        loc0_ready = sem2("loc0_ready")
        loc1_ready = sem2("loc1_ready")
        loc2_ready = sem2("loc2_ready")
        q_ready = sem2("q_ready")
        k_ready = sem2("k_ready")
        kvs_ps = sem2("kvs_ps")
        kvs_ready = sem2("kvs_ready")
        at_ps = sem2("at_ps")
        den_done = sem2("den_done")
        rden_done = sem2("rden_done")
        at_ready = sem2("at_ready")
        aT_ps = sem2("aT_ps")
        y_ready = sem2("y_ready")
        o_ps = sem2("o_ps")
        x2_ready = sem2("x2_ready")
        bn2_done = sem2("bn2_done")

        NX = 4
        start_semaphores(nc, sems)
        block = ctx.enter_context(nc.Block())

        @block.sync
        def _(sp):
            xt = x.rearrange("b (j p) d -> p (b j) d", p=P)
            for k in range(NX):
                n = NT // NX
                sp.dma_start(xres[:, k * n:(k + 1) * n, :], xt[:, k * n:(k + 1) * n, :]).then_inc(x_in[k], 16)

        @block.gpsimd
        def _(pool):
            for u in range(2):
                pool.memset(xnT[u][:, 0:1], 0.0).then_inc(pads_done, 1)
                pool.memset(xnT[u][:, SEQ + 1:SEQ + 2], 0.0).then_inc(pads_done, 1)
                pool.memset(v1[u][:, :, P:P + 1], 1.0).then_inc(pads_done, 1)
            for k in range(NX):
                pool.wait_ge(x_in[k], ONE + 16)
                with pool.Fori(k * BATCH // NX // 2, (k + 1) * BATCH // NX // 2) as i:
                    for u in range(2):
                        pool.wait_ge(bn1_done[u], ONE + TT * i)
                        pool.tensor_copy(x2s[u][:, :, :], xres[:, bass.ds((2 * i + u) * TT, TT), :]).then_inc(staged[u], 1)
            with pool.Fori(0, BATCH // 2) as i:
                for u in range(2):
                    pool.wait_ge(x2_ready[u], ONE + i + 1)
                    pool.tensor_copy(xres[:, bass.ds((2 * i + u) * TT, TT), :], x2s[u][:, :, :]).then_inc(x2_kept[u], 1)

        @block.scalar
        def _(act):
            for dst, src in ((wq_sb[:, :], wqT), (wkv_sb[:, :], wkvT), (wp_sb[:, :], wpT), (bp_sb[:, :], bp)):
                act.dma_start(dst, src).then_inc(w_in, 16)
            act.wait_ge(var_done, ONE + 6)
            act.activation(std[:, :], tmp[:, 4, :], ACT.Sqrt, bias=par[:, V_END:V_END + 1],
                           scale=1.0 / P).then_inc(std_done, 1)
            act.wait_ge(pads_done, ONE + 6)
            with act.Fori(0, BATCH // 2) as i:
                for u in range(2):
                    act.wait_ge(xT_ps[u], ONE + i + 1)
                    act.wait_ge(y_ready[u], ONE + i)
                    act.activation(xnT[u][:, 1:SEQ + 1], psT[u][:, :], ACT.Copy).then_inc(xnT_ready[u], 1)
                for u in range(2):
                    act.wait_ge(q_ps[u], ONE + i + 1)
                    act.wait_ge(q_ready[u], ONE + i)
                    act.activation(eq[u][:, :], psQ[u][:, :], ACT.Exp).then_inc(q_act[u], 1)
                    act.activation(rq[u][:, :], psQ[u][:, :], ACT.Relu).then_inc(q_act[u], 1)
                for u in range(2):
                    act.wait_ge(kv_ps[u], ONE + i + 1)
                    act.wait_ge(k_ready[u], ONE + i)
                    act.wait_ge(kvs_ps[u], ONE + i)
                    act.activation(ek[u][:, :, :], psKV[u][:, :, 0:P], ACT.Exp).then_inc(kv_act[u], 1)
                    act.activation(rk[u][:, :, :], psKV[u][:, :, 0:P], ACT.Relu).then_inc(kv_act[u], 1)
                    act.activation(v1[u][:, :, 0:P], psKV[u][:, :, P:2 * P], ACT.Copy).then_inc(kv_act[u], 1)
                for u in range(2):
                    act.wait_ge(xnT_ready[u], ONE + i + 1)
                    act.wait_ge(loc1_ready[u], ONE + i)
                    act.activation(loc0[u][:, :], xnT[u][:, 1:SEQ + 1], ACT.Identity,
                                   bias=par[:, V_CONVB:V_CONVB + 1],
                                   scale=par[:, V_CONV + 1:V_CONV + 2]).then_inc(loc0_ready[u], 1)

        @block.tensor
        def _(pe):
            pe.wait_ge(w_in, ONE + 64)
            with pe.Fori(0, BATCH // 2) as i:
                for u in range(2):
                    pe.wait_ge(xn_ready[u], ONE + TT * i + TT)
                    pe.wait_ge(y_ready[u], ONE + i)
                    for j in range(TT):
                        mm = pe.transpose(psT[u][:, j * P:(j + 1) * P], xn[u][:, j, :], cst[:, C_ID:C_ID + P])
                    mm.then_inc(xT_ps[u], 1)
                for u in range(2):
                    pe.wait_ge(xnT_ready[u], ONE + i + 1)
                    pe.wait_ge(x2_ready[u], ONE + i)
                    pe.matmul(psQ[u][:, :], wq_sb[:, :], xnT[u][:, 1:SEQ + 1],
                              start=True, stop=True).then_inc(q_ps[u], 1)
                    pe.wait_ge(at_ready[u], ONE + i)
                    for j in range(TT):
                        mm = pe.matmul(psKV[u][:, j, :], xnT[u][:, 1 + j * P:1 + (j + 1) * P], wkv_sb[:, :],
                                       start=True, stop=True)
                    mm.then_inc(kv_ps[u], 1)
                for u in range(2):
                    pe.wait_ge(k_ready[u], ONE + i + 1)
                    pe.wait_ge(kv_act[u], ONE + 3 * i + 3)
                    for j in range(TT):
                        mm = pe.matmul(psKV[u][:, 0, 0:P + 1], kk[u][:, j, :], v1[u][:, j, :],
                                       start=(j == 0), stop=(j == TT - 1))
                    mm.then_inc(kvs_ps[u], 1)
                for u in range(2):
                    pe.wait_ge(kvs_ready[u], ONE + 2 * i + 2)
                    pe.wait_ge(q_ready[u], ONE + i + 1)
                    for j in range(TT):
                        mm = pe.matmul(psKV[u][:, j, 0:P + HEADS], qT[u][:, j * P:(j + 1) * P], kvs[u][:, :],
                                       start=True, stop=True)
                    mm.then_inc(at_ps[u], 1)
                for u in range(2):
                    pe.wait_ge(at_ready[u], ONE + i + 1)
                    for j in range(TT):
                        mm = pe.transpose(psT[u][:, j * P:(j + 1) * P], att[u][:, j, :], cst[:, C_ID:C_ID + P])
                    mm.then_inc(aT_ps[u], 1)
                for u in range(2):
                    pe.wait_ge(y_ready[u], ONE + i + 1)
                    pe.wait_ge(q_act[u], ONE + 2 * i + 2)
                    for j in range(TT):
                        o = psQ[u][:, j * P:(j + 1) * P]
                        pe.matmul(o, yT[u][:, j * P:(j + 1) * P], wp_sb[:, :], start=True, stop=False)
                        mm = pe.matmul(o, cst[0:1, C_ONES:C_ONES + P], bp_sb[:, :], start=False, stop=True)
                    mm.then_inc(o_ps[u], 1)

        @block.vector
        def _(dve):
            with dve.Fori(0, BATCH // 2) as i:
                for u in range(2):
                    dve.wait_ge(staged[u], ONE + i + 1)
                    dve.wait_ge(st1_done[u], ONE + i)
                    for j in range(TT):
                        dve.bn_stats(bst[u][:, j, :], x2s[u][:, j, :]).then_inc(bn1_done[u], 1)
                for u in range(2):
                    dve.wait_ge(bn1_done[u], ONE + TT * i + TT)
                    dve.tensor_scalar(st[:, bass.ds((2 * i + u) * TT, TT), :], bst[u][:, :, :], 1.0, None,
                                      ALU.mult).then_inc(st1_done[u], 1)
            for u in range(2):
                dve.wait_ge(st1_done[u], ONE + BATCH // 2)
            fold_statistics(dve, st, tmp, mean, var_done)
            dve.wait_ge(std_done, ONE + 1)
            dve.reciprocal(rstd[:, :], std[:, :]).then_inc(rstd_done, 1)
            dve.wait_ge(rstd_done, ONE + 1)
            with dve.Fori(0, BATCH // 2) as i:
                for u in range(2):
                    t0 = (2 * i + u) * TT
                    dve.wait_ge(xn_ready[u], ONE + TT * i)
                    dve.tensor_scalar(stat[u][:, 0, :], mean[:, bass.ds(t0, TT)], 1.0, None,
                                      ALU.mult).then_inc(stat_done[u], 1)
                    dve.tensor_scalar(stat[u][:, 1, :], rstd[:, bass.ds(t0, TT)], 1.0, None,
                                      ALU.mult).then_inc(stat_done[u], 1)
                for u in range(2):
                    t0 = (2 * i + u) * TT
                    dve.wait_ge(stat_done[u], ONE + 2 * i + 2)
                    dve.wait_ge(xT_ps[u], ONE + i)
                    for j in range(TT):
                        dve.tensor_scalar(xn[u][:, j, :], xres[:, bass.ds(t0 + j, 1), :], stat[u][:, 0, j:j + 1],
                                          stat[u][:, 1, j:j + 1], ALU.subtract, ALU.mult).then_inc(xn_ready[u], 1)
                for u in range(2):
                    dve.wait_ge(q_act[u], ONE + 2 * i + 2)
                    dve.wait_ge(at_ps[u], ONE + i)
                    dve.scalar_tensor_tensor(qT[u][:, :], eq[u][:, :], 1.0, rq[u][:, :],
                                             ALU.min, ALU.add).then_inc(q_ready[u], 1)
                for u in range(2):
                    dve.wait_ge(kv_act[u], ONE + 3 * i + 3)
                    dve.wait_ge(kvs_ps[u], ONE + i)
                    dve.scalar_tensor_tensor(kk[u][:, :, :], ek[u][:, :, :], 1.0, rk[u][:, :, :],
                                             ALU.min, ALU.add).then_inc(k_ready[u], 1)
                for u in range(2):
                    dve.wait_ge(loc0_ready[u], ONE + i + 1)
                    dve.wait_ge(loc2_ready[u], ONE + i)
                    dve.scalar_tensor_tensor(loc1[u][:, :], xnT[u][:, 0:SEQ], par[:, V_CONV:V_CONV + 1],
                                             loc0[u][:, :], ALU.mult, ALU.add).then_inc(loc1_ready[u], 1)
                for u in range(2):
                    dve.wait_ge(kvs_ps[u], ONE + i + 1)
                    dve.wait_ge(at_ps[u], ONE + i)
                    dve.tensor_tensor(kvs[u][:, 0:P], psKV[u][:, 0, 0:P], cst[:, C_BLOCK:C_BLOCK + P],
                                      ALU.mult).then_inc(kvs_ready[u], 1)
                    dve.tensor_scalar(kvs[u][:, P:P + HEADS], cst[:, C_HEAD:C_HEAD + HEADS],
                                      psKV[u][:, 0, P:P + 1], None, ALU.mult).then_inc(kvs_ready[u], 1)
                for u in range(2):
                    dve.wait_ge(loc1_ready[u], ONE + i + 1)
                    dve.wait_ge(y_ready[u], ONE + i)
                    dve.scalar_tensor_tensor(loc2[u][:, :], xnT[u][:, 2:SEQ + 2], par[:, V_CONV + 2:V_CONV + 3],
                                             loc1[u][:, :], ALU.mult, ALU.add).then_inc(loc2_ready[u], 1)
                for u in range(2):
                    dve.wait_ge(at_ps[u], ONE + i + 1)
                    dve.wait_ge(rden_done[u], ONE + i)
                    dve.tensor_scalar(den[u][:, :, :], psKV[u][:, :, P:P + HEADS], 1e-6, None,
                                      ALU.max).then_inc(den_done[u], 1)
                    dve.wait_ge(den_done[u], ONE + i + 1)
                    dve.wait_ge(at_ready[u], ONE + i)
                    dve.reciprocal(rden[u][:, :, :], den[u][:, :, :]).then_inc(rden_done[u], 1)
                    dve.wait_ge(rden_done[u], ONE + i + 1)
                    dve.wait_ge(aT_ps[u], ONE + i)
                    dve.tensor_tensor(att[u][:, :, :].rearrange("p j (h e) -> p j h e", e=HD),
                                      psKV[u][:, :, 0:P].rearrange("p j (h e) -> p j h e", e=HD),
                                      rden[u][:, :, :].unsqueeze(3).broadcast_to([P, TT, HEADS, HD]),
                                      ALU.mult).then_inc(at_ready[u], 1)
                for u in range(2):
                    dve.wait_ge(aT_ps[u], ONE + i + 1)
                    dve.wait_ge(loc2_ready[u], ONE + i + 1)
                    dve.wait_ge(o_ps[u], ONE + i)
                    dve.tensor_tensor(yT[u][:, :], psT[u][:, :], loc2[u][:, :], ALU.add).then_inc(y_ready[u], 1)
                for u in range(2):
                    t0 = (2 * i + u) * TT
                    dve.wait_ge(o_ps[u], ONE + i + 1)
                    dve.wait_ge(x2_kept[u], ONE + i)
                    dve.tensor_tensor(x2s[u][:, :, :], psQ[u][:, :].rearrange("p (j d) -> p j d", d=P),
                                      xres[:, bass.ds(t0, TT), :], ALU.add).then_inc(x2_ready[u], 1)
                for u in range(2):
                    dve.wait_ge(x2_ready[u], ONE + i + 1)
                    dve.wait_ge(st2_done[u], ONE + i)
                    for j in range(TT):
                        dve.bn_stats(bst[u][:, j, :], x2s[u][:, j, :]).then_inc(bn2_done[u], 1)
                for u in range(2):
                    dve.wait_ge(bn2_done[u], ONE + TT * i + TT)
                    dve.tensor_scalar(st[:, bass.ds((2 * i + u) * TT, TT), :], bst[u][:, :, :], 1.0, None,
                                      ALU.mult).then_inc(st2_done[u], 1)


def router_phase(nc, wr, br, cst, par, xres, st, xH, xL, score, xsave):
    sems = []
    with ExitStack() as ctx:
        def sb(name, shape, dt=F32):
            return ctx.enter_context(nc.sbuf_tensor(name, shape, dt))

        def sb2(name, shape, dt=F32):
            return [sb(f"{name}{u}", shape, dt) for u in range(2)]

        def ps2(name, shape):
            return [ctx.enter_context(nc.psum_tensor(f"{name}{u}", shape, F32)) for u in range(2)]

        def sem(name):
            sems.append(ctx.enter_context(nc.semaphore(name)))
            return sems[-1]

        def sem2(name):
            return [sem(f"{name}{u}") for u in range(2)]

        wr_sb = sb("wr_sb", [P, E])
        br_sb = sb("br_sb", [P, E])
        tmp = sb("r_tmp", [P, 5, NT])
        mean = sb("r_mean", [P, NT])
        std = sb("r_std", [P, NT])
        rstd = sb("r_rstd", [P, NT])
        stat = sb2("r_stat", [P, 2, TT])
        xn = sb2("r_xn", [P, TT, P])
        xT = sb2("r_xT", [P, SEQ])
        lg = sb2("r_lg", [P, TT, E])
        lc = sb2("r_lc", [P, TT, E])
        mx = sb2("r_mx", [P, TT])
        ex = sb2("r_ex", [P, TT, E])
        sm = sb2("r_sm", [P, TT])
        rs = sb2("r_rs", [P, TT])
        pr = sb2("r_pr", [P, TT, E])
        psT = ps2("r_psT", [P, SEQ])
        psR = ps2("r_psR", [P, TT, E])
        psS = ps2("r_psS", [P, TT // 2, P])

        w_in = sem("r_w_in")
        saved = sem("r_saved")
        var_done = sem("r_var_done")
        std_done = sem("r_std_done")
        rstd_done = sem("r_rstd_done")
        stat_done = sem2("r_stat_done")
        xn_ready = sem2("r_xn_ready")
        xT_ps = sem2("r_xT_ps")
        xT_ready = sem2("r_xT_ready")
        xH_ready = sem2("r_xH_ready")
        xL_ready = sem2("r_xL_ready")
        lg_ps = sem2("r_lg_ps")
        lg_done = sem2("r_lg_done")
        mx_done = sem2("r_mx_done")
        lc_done = sem2("r_lc_done")
        ex_done = sem2("r_ex_done")
        sm_done = sem2("r_sm_done")
        rs_done = sem2("r_rs_done")
        pr_done = sem2("r_pr_done")
        pT_ps = sem2("r_pT_ps")
        sc_done = sem2("r_sc_done")

        start_semaphores(nc, sems)
        block = ctx.enter_context(nc.Block())

        @block.sync
        def _(sp):
            sp.dma_start(wr_sb[:, :], wr).then_inc(w_in, 16)
            sp.dma_start(br_sb[:, :], br.partition_broadcast(P)).then_inc(w_in, 16)
            sp.dma_start(xsave, xres[:, :, :]).then_inc(saved, 16)
            sp.wait_ge(saved, ONE + 16)

        @block.scalar
        def _(act):
            act.wait_ge(var_done, ONE + 6)
            act.activation(std[:, :], tmp[:, 4, :], ACT.Sqrt, bias=par[:, V_END:V_END + 1],
                           scale=1.0 / P).then_inc(std_done, 1)
            with act.Fori(0, HB) as i:
                for u in range(2):
                    act.wait_ge(xT_ps[u], ONE + i + 1)
                    act.wait_ge(lg_ps[u], ONE + i)
                    act.wait_ge(xL_ready[u], ONE + i)
                    act.activation(xT[u][:, :], psT[u][:, :], ACT.Copy).then_inc(xT_ready[u], 1)
                    act.activation(xH[:, bass.ds((i + u * HB) * SEQ, SEQ)], psT[u][:, :],
                                   ACT.Copy).then_inc(xH_ready[u], 1)
                for u in range(2):
                    act.wait_ge(lc_done[u], ONE + i + 1)
                    act.wait_ge(pr_done[u], ONE + i)
                    act.activation(ex[u][:, :, :], lc[u][:, :, :], ACT.Exp).then_inc(ex_done[u], 1)
                for u in range(2):
                    act.wait_ge(pT_ps[u], ONE + i + 1)
                    dst = score[u * E:(u + 1) * E, bass.ds(i * SEQ, SEQ)].rearrange("e (a r t) -> e a r t", r=2, t=P)
                    for r in range(2):
                        act.activation(dst[:, :, r, :], psS[u][r * E:(r + 1) * E, :, :],
                                       ACT.Copy).then_inc(sc_done[u], 1)

        @block.gpsimd
        def _(pool):
            with pool.Fori(0, HB) as i:
                for u in range(2):
                    pool.wait_ge(xH_ready[u], ONE + i + 1)
                    at = bass.ds((i + u * HB) * SEQ, SEQ)
                    pool.tensor_tensor(xL[:, at], xT[u][:, :], xH[:, at].bitcast(F32),
                                       ALU.subtract).then_inc(xL_ready[u], 1)

        @block.tensor
        def _(pe):
            pe.wait_ge(w_in, ONE + 32)
            with pe.Fori(0, HB) as i:
                for u in range(2):
                    pe.wait_ge(xn_ready[u], ONE + TT * i + TT)
                    pe.wait_ge(xH_ready[u], ONE + i)
                    for j in range(TT):
                        mm = pe.transpose(psT[u][:, j * P:(j + 1) * P], xn[u][:, j, :], cst[:, C_ID:C_ID + P])
                    mm.then_inc(xT_ps[u], 1)
                for u in range(2):
                    pe.wait_ge(xT_ready[u], ONE + i + 1)
                    pe.wait_ge(lg_done[u], ONE + i)
                    for j in range(TT):
                        mm = pe.matmul(psR[u][:, j, :], xT[u][:, j * P:(j + 1) * P], wr_sb[:, :],
                                       start=True, stop=True)
                    mm.then_inc(lg_ps[u], 1)
                for u in range(2):
                    pe.wait_ge(pr_done[u], ONE + i + 1)
                    pe.wait_ge(sc_done[u], ONE + 2 * i)
                    for j in range(0, TT, 2):
                        mm = pe.transpose(psS[u][:, j // 2, :], pr[u][:, j:j + 2, :].rearrange("p a e -> p (a e)"),
                                          cst[:, C_ID:C_ID + P])
                    mm.then_inc(pT_ps[u], 1)

        @block.vector
        def _(dve):
            fold_statistics(dve, st, tmp, mean, var_done)
            dve.wait_ge(std_done, ONE + 1)
            dve.reciprocal(rstd[:, :], std[:, :]).then_inc(rstd_done, 1)
            dve.wait_ge(rstd_done, ONE + 1)
            dve.wait_ge(w_in, ONE + 32)
            with dve.Fori(0, HB) as i:
                for u in range(2):
                    t0 = (i + u * HB) * TT
                    dve.wait_ge(xn_ready[u], ONE + TT * i)
                    dve.tensor_scalar(stat[u][:, 0, :], mean[:, bass.ds(t0, TT)], 1.0, None,
                                      ALU.mult).then_inc(stat_done[u], 1)
                    dve.tensor_scalar(stat[u][:, 1, :], rstd[:, bass.ds(t0, TT)], 1.0, None,
                                      ALU.mult).then_inc(stat_done[u], 1)
                for u in range(2):
                    t0 = (i + u * HB) * TT
                    dve.wait_ge(stat_done[u], ONE + 2 * i + 2)
                    dve.wait_ge(xT_ps[u], ONE + i)
                    for j in range(TT):
                        dve.tensor_scalar(xn[u][:, j, :], xres[:, bass.ds(t0 + j, 1), :], stat[u][:, 0, j:j + 1],
                                          stat[u][:, 1, j:j + 1], ALU.subtract, ALU.mult).then_inc(xn_ready[u], 1)
                for u in range(2):
                    dve.wait_ge(lg_ps[u], ONE + i + 1)
                    dve.wait_ge(lc_done[u], ONE + i)
                    dve.tensor_tensor(lg[u][:, :, :], psR[u][:, :, :],
                                      br_sb[:, :].unsqueeze(1).broadcast_to([P, TT, E]),
                                      ALU.add).then_inc(lg_done[u], 1)
                for u in range(2):
                    dve.wait_ge(lg_done[u], ONE + i + 1)
                    dve.wait_ge(lc_done[u], ONE + i)
                    dve.tensor_reduce(mx[u][:, :], lg[u][:, :, :], AX_X, ALU.max).then_inc(mx_done[u], 1)
                for u in range(2):
                    dve.wait_ge(mx_done[u], ONE + i + 1)
                    dve.wait_ge(ex_done[u], ONE + i)
                    dve.tensor_tensor(lc[u][:, :, :], lg[u][:, :, :],
                                      mx[u][:, :].unsqueeze(2).broadcast_to([P, TT, E]),
                                      ALU.subtract).then_inc(lc_done[u], 1)
                for u in range(2):
                    dve.wait_ge(ex_done[u], ONE + i + 1)
                    dve.wait_ge(rs_done[u], ONE + i)
                    dve.tensor_reduce(sm[u][:, :], ex[u][:, :, :], AX_X, ALU.add).then_inc(sm_done[u], 1)
                for u in range(2):
                    dve.wait_ge(sm_done[u], ONE + i + 1)
                    dve.wait_ge(pr_done[u], ONE + i)
                    dve.reciprocal(rs[u][:, :], sm[u][:, :]).then_inc(rs_done[u], 1)
                for u in range(2):
                    dve.wait_ge(rs_done[u], ONE + i + 1)
                    dve.wait_ge(pT_ps[u], ONE + i)
                    dve.tensor_tensor(pr[u][:, :, :], ex[u][:, :, :],
                                      rs[u][:, :].unsqueeze(2).broadcast_to([P, TT, E]),
                                      ALU.mult).then_inc(pr_done[u], 1)


def merge_steps():
    steps = []
    block = 2
    while block <= HALF:
        steps.append((block, 0))
        d = block // 4
        while d >= 1:
            steps.append((2 * d, d))
            d //= 2
        block *= 2
    return steps


def routing_phase(nc, wupT, wgateT, wdn, bdn, sel, cst, score, wU, wG, wD, selR, bdR, onesR, w_stage, bd_stage):
    sems = []
    with ExitStack() as ctx:
        def sb(name, shape, dt=F32):
            return ctx.enter_context(nc.sbuf_tensor(name, shape, dt))

        def sem(name):
            sems.append(ctx.enter_context(nc.semaphore(name)))
            return sems[-1]

        bufs = [sb("sort0", [P, HALF]), sb("sort1", [P, HALF])]
        gsum = sb("gsum", [P, NG // 2])
        gmin = sb("gmin", [P, NG // 2])
        G = sb("G", [E, NG])
        M = sb("M", [E, NG])
        cand = sb("cand", [E, 1], I32)
        dec = sb("dec", [E, 1], I32)
        cnt = sb("cnt", [E, 1])
        junk = sb("junk", [E, NG])
        gt = sb("gt", [E, NG])
        eqg = sb("eqg", [E, NG])
        left = sb("left", [E, 1])
        cum = sb("cum", [E, NG])
        pos = sb("pos", [E, NG])
        tot = sb("tot", [E, NG])
        take = sb("take", [E, NG])
        kept = sb("kept", [E, NG])
        big = sb("big", [E, NG])
        mins = sb("mins", [E, NG])
        lim = sb("lim", [E, 2])
        lim2 = sb("lim2", [P, 2])
        cgt = sb("cgt", [P, 2])
        room = sb("room", [P, 2])
        psC = ctx.enter_context(nc.psum_tensor("psC", [E, 1], F32))
        psA = ctx.enter_context(nc.psum_tensor("psA", [E, NG], F32))
        psB = ctx.enter_context(nc.psum_tensor("psB", [E, NG], F32))
        psD = ctx.enter_context(nc.psum_tensor("psD", [P, 2], F32))

        sorted_ = sem("sorted_")
        swapped = sem("swapped")
        group_done = sem("group_done")
        moved = sem("moved")
        cand_ready = sem("cand_ready")
        cnt_ready = sem("cnt_ready")
        cnt_ps = sem("cnt_ps")
        dec_ready = sem("dec_ready")
        tie_in = sem("tie_in")
        tie_ps = sem("tie_ps")
        chain = sem("chain")
        lim_ready = sem("lim_ready")
        lim_moved = sem("lim_moved")
        cgt_ready = sem("cgt_ready")
        cgt_ps = sem("cgt_ps")
        w_in = [sem(f"w_in_{n}") for n in ("u", "g", "d", "s", "b")]
        w_high = sem("w_high")
        w_low = sem("w_low")
        bd_zero = sem("bd_zero")

        steps = merge_steps()
        last = [(2 * d, d) for d in (HALF // 2 >> s for s in range(12)) if d >= GROUP]
        n1, n2 = len(steps), len(last)
        A, B = bufs[(n1 - 1) % 2], bufs[n1 % 2]
        start_semaphores(nc, sems)
        block = ctx.enter_context(nc.Block())

        @block.sync
        def _(sp):
            sp.dma_start(w_stage[:, :], wupT).then_inc(w_in[0], 16)
            for r in range(0, P, E):
                sp.dma_start(bd_stage[r:r + E, :], bdn).then_inc(w_in[4], 16)
            sp.wait_ge(w_low, ONE + 1)
            sp.dma_start(w_stage[:, :], wgateT).then_inc(w_in[1], 16)
            sp.wait_ge(w_low, ONE + 2)
            sp.dma_start(w_stage[:, :], wdn).then_inc(w_in[2], 16)
            sp.wait_ge(w_low, ONE + 3)
            sp.dma_start(w_stage[:, :], sel).then_inc(w_in[3], 16)

        @block.gpsimd
        def _(pool):
            pool.memset(bdR[E:P, 1, :].bitcast(F32), 0.0).then_inc(bd_zero, 1)
            pool.wait_ge(bd_zero, ONE + 1)
            for n, w in enumerate((wU, wG, wD)):
                pool.wait_ge(w_high, ONE + n + 1)
                pool.tensor_tensor(w[:, 1, :], w_stage[:, :], w[:, 0, :].bitcast(F32),
                                   ALU.subtract).then_inc(w_low, 1)
            pool.wait_ge(w_high, ONE + 4)
            pool.wait_ge(w_low, ONE + 3)
            pool.tensor_tensor(bdR[0:E, 1, :], bd_stage[0:E, :], bdR[0:E, 0, :].bitcast(F32),
                               ALU.subtract).then_inc(w_low, 1)

        @block.scalar
        def _(act):
            for n, w in enumerate((wU, wG, wD)):
                act.wait_ge(w_in[n], ONE + 16)
                act.activation(w[:, 0, :], w_stage[:, :], ACT.Copy).then_inc(w_high, 1)
            act.wait_ge(w_in[4], ONE + 32)
            act.activation(bdR[:, 0, :], bd_stage[:, :], ACT.Copy).then_inc(w_high, 1)
            act.wait_ge(w_in[3], ONE + 16)
            act.activation(selR[:, :], w_stage[:, :], ACT.Copy).then_inc(w_high, 1)
            act.activation(onesR[:, :], cst[:, C_ONES:C_ONES + 2], ACT.Copy).then_inc(w_high, 1)
            act.wait_ge(sorted_, ONE + 2 * n1)
            act.activation(B[0:E, :], A[E:P, :], ACT.Copy).then_inc(swapped, 1)
            act.wait_ge(group_done, ONE + 2)
            act.activation(G[:, 0:NG // 2], gsum[0:E, :], ACT.Copy).then_inc(moved, 1)
            act.activation(G[:, NG // 2:NG], gsum[E:P, :], ACT.Copy).then_inc(moved, 1)
            act.activation(M[:, 0:NG // 2], gmin[0:E, :], ACT.Copy).then_inc(moved, 1)
            act.activation(M[:, NG // 2:NG], gmin[E:P, :], ACT.Copy).then_inc(moved, 1)
            act.wait_ge(lim_ready, ONE + 2)
            act.activation(lim2[0:E, :], lim[:, :], ACT.Copy).then_inc(lim_moved, 1)
            act.activation(lim2[E:P, :], lim[:, :], ACT.Copy).then_inc(lim_moved, 1)

        @block.tensor
        def _(pe):
            ones = cst[0:E, C_ONES:C_ONES + E]
            for b in range(31):
                pe.wait_ge(cnt_ready, ONE + b + 1)
                pe.matmul(psC[:, :], ones, cnt[:, :], start=True, stop=True).then_inc(cnt_ps, 1)
            pe.wait_ge(tie_in, ONE + 2)
            pe.matmul(psC[:, :], ones, cnt[:, :], start=True, stop=True).then_inc(tie_ps, 1)
            pe.matmul(psA[:, :], ones, eqg[:, :], start=True, stop=True).then_inc(tie_ps, 1)
            pe.matmul(psB[:, :], cst[0:E, C_TRI:C_TRI + E], eqg[:, :], start=True, stop=True).then_inc(tie_ps, 1)
            pe.wait_ge(cgt_ready, ONE + 2)
            pe.matmul(psD[:, 0:1], cst[:, C_PAIR:C_PAIR + P], cgt[:, 0:1], start=True, stop=True).then_inc(cgt_ps, 1)
            pe.matmul(psD[:, 1:2], cst[:, C_FIRST:C_FIRST + P], cgt[:, 1:2],
                      start=True, stop=True).then_inc(cgt_ps, 1)

        @block.vector
        def _(dve):
            src = score
            for s, (k, d) in enumerate(steps):
                dst = bufs[s % 2]
                if s:
                    dve.wait_ge(sorted_, ONE + 2 * s)
                if d:
                    a = src[:, :].rearrange("p (n t d) -> p n t d", t=2, d=d)
                    o = dst[:, :].rearrange("p (n t d) -> p n t d", t=2, d=d)
                    i0, i1, o0, o1 = a[:, :, 0], a[:, :, 1], o[:, :, 0], o[:, :, 1]
                else:
                    a = src[:, :].rearrange("p (n k) -> p n k", k=k)
                    o = dst[:, :].rearrange("p (n k) -> p n k", k=k)
                    i0, i1 = a[:, :, 0:k // 2], a[:, :, k - 1:k // 2 - 1:-1]
                    o0, o1 = o[:, :, 0:k // 2], o[:, :, k - 1:k // 2 - 1:-1]
                dve.tensor_tensor(o0, i0, i1, ALU.max).then_inc(sorted_, 1)
                dve.tensor_tensor(o1, i0, i1, ALU.min).then_inc(sorted_, 1)
                src = dst
            dve.wait_ge(sorted_, ONE + 2 * n1)
            dve.tensor_copy(B[E:P, :], A[0:E, :]).then_inc(swapped, 1)
            dve.wait_ge(swapped, ONE + 2)
            dve.tensor_tensor(A[0:E, :], A[0:E, :], B[0:E, ::-1], ALU.max).then_inc(sorted_, 1)
            dve.tensor_tensor(A[E:P, :], A[E:P, :], B[E:P, ::-1], ALU.min).then_inc(sorted_, 1)
            src, dst = A, B
            for s, (k, d) in enumerate(last):
                dve.wait_ge(sorted_, ONE + 2 * (n1 + 1 + s))
                a = src[:, :].rearrange("p (n t d) -> p n t d", t=2, d=d)
                o = dst[:, :].rearrange("p (n t d) -> p n t d", t=2, d=d)
                dve.tensor_tensor(o[:, :, 0], a[:, :, 0], a[:, :, 1], ALU.max).then_inc(sorted_, 1)
                dve.tensor_tensor(o[:, :, 1], a[:, :, 0], a[:, :, 1], ALU.min).then_inc(sorted_, 1)
                src, dst = dst, src
            dve.wait_ge(sorted_, ONE + 2 * (n1 + 1 + n2))
            g = src[:, :].rearrange("p (g r) -> p g r", r=GROUP)
            dve.tensor_reduce(gsum[:, :], g, AX_X, ALU.add).then_inc(group_done, 1)
            dve.tensor_reduce(gmin[:, :], g, AX_X, ALU.min).then_inc(group_done, 1)
            dve.memset(cand[:, :], 1 << 30).then_inc(cand_ready, 1)
            dve.wait_ge(moved, ONE + 4)
            for n, b in enumerate(range(30, -1, -1)):
                dve.wait_ge(cand_ready, ONE + n + 1)
                if n:
                    dve.wait_ge(cnt_ps, ONE + n)
                dve.tensor_scalar(junk[:, :], G[:, :], cand[:, :].bitcast(F32), 0.0, ALU.is_ge, ALU.add,
                                  accum_out=cnt[:, :]).then_inc(cnt_ready, 1)
                dve.wait_ge(cnt_ps, ONE + n + 1)
                dve.tensor_scalar(dec[:, :], psC[:, :], float(BUDGET), float(1 << b), ALU.is_lt,
                                  ALU.mult).then_inc(dec_ready, 1)
                dve.wait_ge(dec_ready, ONE + n + 1)
                dve.scalar_tensor_tensor(cand[:, :], dec[:, :], (1 << b) >> 1, cand[:, :], ALU.bitwise_or,
                                         ALU.bitwise_xor).then_inc(cand_ready, 1)
            dve.wait_ge(cand_ready, ONE + 32)
            lam = cand[:, :].bitcast(F32)
            dve.tensor_scalar(gt[:, :], G[:, :], lam, 0.0, ALU.is_gt, ALU.add,
                              accum_out=cnt[:, :]).then_inc(tie_in, 1)
            dve.tensor_scalar(eqg[:, :], G[:, :], lam, None, ALU.is_equal).then_inc(tie_in, 1)
            dve.wait_ge(tie_ps, ONE + 3)
            dve.tensor_scalar(left[:, :], psC[:, :], -1.0, float(BUDGET), ALU.mult, ALU.add).then_inc(chain, 1)
            dve.tensor_copy(tot[:, :], psA[:, :]).then_inc(chain, 1)
            dve.wait_ge(chain, ONE + 2)
            dve.tensor_tensor_scan(cum[:, :], tot[:, :], tot[:, :], 0.0, ALU.add, ALU.bypass).then_inc(chain, 1)
            dve.wait_ge(chain, ONE + 3)
            dve.tensor_tensor(pos[:, :], cum[:, :], tot[:, :], ALU.subtract).then_inc(chain, 1)
            dve.wait_ge(chain, ONE + 4)
            dve.tensor_tensor(cum[:, :], psB[:, :], pos[:, :], ALU.add).then_inc(chain, 1)
            dve.wait_ge(chain, ONE + 5)
            dve.scalar_tensor_tensor(take[:, :], cum[:, :], left[:, :], eqg[:, :], ALU.is_lt,
                                     ALU.mult).then_inc(chain, 1)
            dve.wait_ge(chain, ONE + 6)
            dve.tensor_tensor(kept[:, :], take[:, :], gt[:, :], ALU.add).then_inc(chain, 1)
            dve.wait_ge(chain, ONE + 7)
            dve.tensor_scalar(big[:, :], kept[:, :], -4.0, 4.0, ALU.mult, ALU.add).then_inc(chain, 1)
            dve.tensor_reduce(cnt[:, :], kept[:, :], AX_X, ALU.add).then_inc(chain, 1)
            dve.wait_ge(chain, ONE + 9)
            dve.tensor_tensor(mins[:, :], big[:, :], M[:, :], ALU.add).then_inc(chain, 1)
            dve.tensor_scalar(lim[:, 1:2], cnt[:, :], float(GROUP), None, ALU.mult).then_inc(lim_ready, 1)
            dve.wait_ge(chain, ONE + 10)
            dve.tensor_reduce(lim[:, 0:1], mins[:, :], AX_X, ALU.min).then_inc(lim_ready, 1)
            dve.wait_ge(lim_moved, ONE + 2)
            thr = lim2[:, 0:1]
            S0, S1 = bufs
            dve.tensor_scalar(S0[:, :], score[:, :], thr, 0.0, ALU.is_equal, ALU.add,
                              accum_out=cgt[:, 1:2]).then_inc(cgt_ready, 1)
            dve.tensor_scalar(S1[:, :], score[:, :], thr, 0.0, ALU.is_gt, ALU.add,
                              accum_out=cgt[:, 0:1]).then_inc(cgt_ready, 1)
            dve.wait_ge(cgt_ps, ONE + 2)
            dve.tensor_tensor(room[:, 0:1], lim2[:, 1:2], psD[:, 0:1], ALU.subtract).then_inc(chain, 1)
            dve.tensor_tensor(room[:, 1:2], lim2[:, 1:2], lim2[:, 1:2], ALU.subtract).then_inc(chain, 1)
            dve.wait_ge(chain, ONE + 12)
            dve.tensor_tensor(room[:, 1:2], room[:, 1:2], psD[:, 1:2], ALU.add).then_inc(chain, 1)
            dve.wait_ge(chain, ONE + 13)
            dve.wait_ge(cgt_ready, ONE + 2)
            dve.tensor_tensor_scan(S1[:, :], S0[:, :], S0[:, :], room[:, 1:2], ALU.add,
                                   ALU.bypass).then_inc(chain, 1)
            dve.wait_ge(chain, ONE + 14)
            dve.tensor_scalar(S0[:, :], S1[:, :], room[:, 0:1], None, ALU.is_le).then_inc(chain, 1)
            dve.wait_ge(chain, ONE + 15)
            dve.scalar_tensor_tensor(S1[:, :], score[:, :], thr, S0[:, :], ALU.is_ge, ALU.mult).then_inc(chain, 1)
            dve.wait_ge(chain, ONE + 16)
            dve.scalar_tensor_tensor(S0[:, :], score[:, :], thr, S1[:, :], ALU.is_gt, ALU.max).then_inc(chain, 1)
            dve.wait_ge(chain, ONE + 17)
            dve.tensor_tensor(score[:, :], score[:, :], S0[:, :], ALU.mult).then_inc(chain, 1)


def experts_phase(nc, out, xsave, par, cst, score, xH, xL, wU, wG, wD, selR, bdR, onesR):
    sems = []
    with ExitStack() as ctx:
        def sb(name, shape, dt=F32, side="left"):
            return ctx.enter_context(nc.sbuf_tensor(name, shape, dt, side=side))

        def sb2(name, shape, dt=F32):
            return [sb(f"{name}{u}", shape, dt) for u in range(2)]

        def ps2(name, shape):
            return [ctx.enter_context(nc.psum_tensor(f"{name}{u}", shape, F32)) for u in range(2)]

        def sem(name):
            sems.append(ctx.enter_context(nc.semaphore(name)))
            return sems[-1]

        def sem2(name):
            return [sem(f"{name}{u}") for u in range(2)]

        raw = sb2("raw", [P, SEQ])
        fs = sb2("fs", [P, SEQ], F32R)
        xr = [sb(f"xr{u}", [P, TT, P], side="right") for u in range(2)]
        act_u = sb2("act_u", [P, SEQ])
        gated = sb2("gated", [P, SEQ])
        hid = sb2("hid", [P, SEQ])
        hidH = [sb(f"hidH{q}", [P, SEQ], F32R) for q in range(4)]
        hidL = [sb(f"hidL{q}", [P, SEQ], F32R) for q in range(4)]
        oT = [sb(f"oT{u}", [P, SEQ], side="right") for u in range(2)]
        den = sb2("e_den", [P, TT])
        rden = sb2("e_rden", [P, TT])
        psF = ps2("psF", [P, SEQ])
        psU = ps2("psU", [P, SEQ])
        psG = ps2("psG", [P, SEQ])
        psO = ctx.enter_context(nc.psum_tensor("psO", [P, SEQ], F32))
        psT = ctx.enter_context(nc.psum_tensor("psT_e", [P, SEQ], F32))

        fs_high = sem2("fs_high")
        fs_ready = sem2("fs_ready")
        raw_in = [ctx.enter_context(nc.semaphore(f"raw_in{u}")) for u in range(2)]
        xr_in = [ctx.enter_context(nc.semaphore(f"xr_in{u}")) for u in range(2)]
        up_ps = sem2("up_ps")
        gate_ps = sem2("gate_ps")
        silu_ready = sem2("silu_ready")
        gated_ready = sem2("gated_ready")
        hid_ready = sem2("hid_ready")
        hidH_ready = [sem(f"hidH_ready{q}") for q in range(4)]
        hidL_ready = [sem(f"hidL_ready{q}") for q in range(4)]
        score_ps = sem2("score_ps")
        down_done = [sem(f"down_done{q}") for q in range(4)]
        den_ps = sem2("den_ps")
        den_done = sem2("e_den_done")
        rden_done = sem2("e_rden_done")
        oT_ready = sem2("oT_ready")
        oTT_ps = sem2("oTT_ps")
        y_ready = sem2("e_y_ready")
        y_out = sem2("y_out")

        out_t = out.rearrange("b (j p) d -> b p j d", p=P)
        QC = 2 * CH // 4
        LAG = 4
        TURN = LAG + 1
        SUMS = TURN + 3
        start_semaphores(nc, sems, raw_in + xr_in)
        block = ctx.enter_context(nc.Block())

        @block.sync
        def _(sp):
            with sp.Fori(0, HB) as i:
                for h in range(2):
                    sp.wait_ge(y_ready[h], ONE + TT * i + TT)
                    sp.dma_start(out_t[bass.ds(i + h * HB, 1)].rearrange("b p j d -> (b p) j d"),
                                 xr[h][:, :, :]).then_inc(y_out[h], 16)
            for h in range(2):
                sp.wait_ge(y_out[h], ONE + 16 * HB)

        @block.gpsimd
        def _(pool):
            with pool.Fori(0, HB) as i:
                for h in range(2):
                    pool.wait_ge(y_out[h], ONE + 16 * i)
                    for part in (0, E):
                        pool.dma_start(raw[h][part:part + E, :],
                                       score[h * E:(h + 1) * E, bass.ds(i * SEQ, SEQ)]).then_inc(raw_in[h], 16)
                    pool.dma_start(xr[h][:, :, :], xsave[:, bass.ds((i + h * HB) * TT, TT), :]).then_inc(xr_in[h], 16)
                    pool.wait_ge(raw_in[h], 32 * i + 32)
                    pool.tensor_tensor(fs[h][:, :], raw[h][:, :], cst[:, C_ONES:C_ONES + 1].broadcast_to([P, SEQ]),
                                       ALU.mult).then_inc(fs_high[h], 1)
                    pool.wait_ge(fs_high[h], ONE + i + 1)
                    pool.tensor_tensor(fs[h][E:P, :], raw[h][E:P, :], fs[h][E:P, :].bitcast(F32),
                                       ALU.subtract).then_inc(fs_ready[h], 1)
                    pool.wait_ge(fs_ready[h], ONE + i + 1)

        def run_pairs(eng, step):
            for g in range(2 * CH):
                step(0, g, True)
            with eng.Fori(1, HB) as i:
                for g in range(2 * CH):
                    step(i, g, False)

        def back(i, g, k, first=False):
            if g >= k:
                return i, g - k
            return None if first else (i - 1, 2 * CH + g - k)

        def batch_before(i, h, first):
            if h:
                return i, 0
            return None if first else (i - 1, 1)

        @block.scalar
        def _(act):
            def silu(i, g):
                p, n, c = g % 2, i * CH + g // 2, g % CH
                act.wait_ge(up_ps[p], ONE + n + 1)
                act.wait_ge(gated_ready[p], ONE + n)
                act.activation(act_u[p][:, :], psU[p][:, :], ACT.Silu,
                               bias=par[:, V_BUP + c:V_BUP + c + 1]).then_inc(silu_ready[p], 1)

            def high_part(i, g):
                p, n, q, m = g % 2, i * CH + g // 2, g % 4, i * QC + g // 4
                act.wait_ge(hid_ready[p], ONE + n + 1)
                act.wait_ge(down_done[q], ONE + m)
                act.activation(hidH[q][:, :], hid[p][:, :], ACT.Copy).then_inc(hidH_ready[q], 1)

            def store_sum(i, h):
                act.wait_ge(down_done[3], ONE + i * QC + (h + 1) * QC // 2)
                act.wait_ge(oTT_ps[h], ONE + i)
                act.activation(oT[h][:, :], psO[:, :], ACT.Copy).then_inc(oT_ready[h], 1)

            def step(i, g, first):
                h, c = g // CH, g % CH
                before = batch_before(i, h, first)
                if c == LAG and before:
                    store_sum(*before)
                silu(i, g)
                if back(i, g, 2, first):
                    high_part(*back(i, g, 2))

            run_pairs(act, step)
            for g in range(2 * CH - 2, 2 * CH):
                high_part(HB - 1, g)
            store_sum(HB - 1, 1)

        @block.tensor
        def _(pe):
            def products(i, g):
                h, c = g // CH, g % CH
                p, n = g % 2, i * CH + g // 2
                tok = bass.ds((i + h * HB) * SEQ, SEQ)
                lo, hi = c * P, (c + 1) * P
                if c == 0:
                    pe.wait_ge(fs_ready[h], ONE + i + 1)
                for w, ps, used, done in ((wU, psU, silu_ready, up_ps), (wG, psG, gated_ready, gate_ps)):
                    pe.wait_ge(used[p], ONE + n)
                    pe.matmul(ps[p][:, :], w[:, 0, lo:hi], xL[:, tok], start=True, stop=False)
                    pe.matmul(ps[p][:, :], w[:, 0, lo:hi], xH[:, tok], start=False, stop=False)
                    pe.matmul(ps[p][:, :], w[:, 1, lo:hi], xH[:, tok], start=False, stop=True).then_inc(done[p], 1)
                pe.wait_ge(hid_ready[p], ONE + n)
                pe.matmul(psF[p][:, :], selR[:, lo:hi], fs[h][:, :], start=True, stop=True).then_inc(score_ps[p], 1)

            def down(i, g):
                q, m, c = g % 4, i * QC + g // 4, g % CH
                pe.wait_ge(hidH_ready[q], ONE + m + 1)
                pe.wait_ge(hidL_ready[q], ONE + m + 1)
                pe.matmul(psO[:, :], wD[:, 1, c * P:(c + 1) * P], hidH[q][:, :], start=False, stop=False)
                pe.matmul(psO[:, :], wD[:, 0, c * P:(c + 1) * P], hidH[q][:, :], start=False, stop=False)
                pe.matmul(psO[:, :], wD[:, 0, c * P:(c + 1) * P], hidL[q][:, :], start=False,
                          stop=(c == CH - 1)).then_inc(down_done[q], 1)

            def begin(i, h):
                pe.wait_ge(oT_ready[1 - h], ONE + i + h)
                pe.matmul(psO[:, :], bdR[:, 0, :], fs[h][:, :], start=True, stop=False)
                pe.matmul(psO[:, :], bdR[:, 1, :], fs[h][:, :], start=False, stop=False)

            def score_sums(i, h):
                pe.wait_ge(y_ready[1 - h], ONE + TT * (i + h))
                for j in range(TT):
                    mm = pe.matmul(psT[:, 2 * j:2 * j + 2], fs[h][:, j * P:(j + 1) * P], onesR[:, :],
                                   start=True, stop=True)
                mm.then_inc(den_ps[h], 1)

            def turn(i, h):
                pe.wait_ge(oT_ready[h], ONE + i + 1)
                pe.wait_ge(den_done[h], ONE + i + 1)
                for j in range(TT):
                    mm = pe.transpose(psT[:, j * P:(j + 1) * P], oT[h][:, j * P:(j + 1) * P], cst[:, C_ID:C_ID + P])
                mm.then_inc(oTT_ps[h], 1)

            def step(i, g, first):
                h, c = g // CH, g % CH
                before = batch_before(i, h, first)
                products(i, g)
                if c == LAG:
                    begin(i, h)
                if back(i, g, LAG, first):
                    down(*back(i, g, LAG))
                if c == TURN and before:
                    turn(*before)
                if c == SUMS:
                    score_sums(i, h)

            run_pairs(pe, step)
            for g in range(2 * CH - LAG, 2 * CH):
                down(HB - 1, g)
            turn(HB - 1, 1)

        @block.vector
        def _(dve):
            def gate(i, g):
                p, n, c = g % 2, i * CH + g // 2, g % CH
                dve.wait_ge(gate_ps[p], ONE + n + 1)
                dve.wait_ge(silu_ready[p], ONE + n + 1)
                dve.wait_ge(hid_ready[p], ONE + n)
                dve.scalar_tensor_tensor(gated[p][:, :], psG[p][:, :], par[:, V_BGATE + c:V_BGATE + c + 1],
                                         act_u[p][:, :], ALU.add, ALU.mult).then_inc(gated_ready[p], 1)

            def weigh(i, g, first=False):
                p, n = g % 2, i * CH + g // 2
                dve.wait_ge(gated_ready[p], ONE + n + 1)
                dve.wait_ge(score_ps[p], ONE + n + 1)
                if back(i, g, 2, first):
                    j, k = back(i, g, 2)
                    dve.wait_ge(hidL_ready[k % 4], ONE + j * QC + k // 4 + 1)
                dve.tensor_tensor(hid[p][:, :], gated[p][:, :], psF[p][:, :], ALU.mult).then_inc(hid_ready[p], 1)

            def low_part(i, g):
                p, q, m = g % 2, g % 4, i * QC + g // 4
                dve.wait_ge(hidH_ready[q], ONE + m + 1)
                dve.wait_ge(down_done[q], ONE + m)
                dve.tensor_tensor(hidL[q][:, :], hid[p][:, :], hidH[q][:, :].bitcast(F32),
                                  ALU.subtract).then_inc(hidL_ready[q], 1)

            def invert(i, h):
                dve.wait_ge(den_ps[h], ONE + i + 1)
                dve.wait_ge(rden_done[h], ONE + i)
                dve.tensor_scalar(den[h][:, :], psT[:, 0:2 * TT:2], DEN_EPS, None,
                                  ALU.add).then_inc(den_done[h], 1)
                dve.wait_ge(den_done[h], ONE + i + 1)
                dve.wait_ge(y_ready[h], ONE + TT * i)
                dve.reciprocal(rden[h][:, :], den[h][:, :]).then_inc(rden_done[h], 1)

            def finish(i, h):
                dve.wait_ge(oTT_ps[h], ONE + i + 1)
                dve.wait_ge(rden_done[h], ONE + i + 1)
                dve.wait_ge(xr_in[h], 16 * i + 16)
                for j in range(TT):
                    dve.scalar_tensor_tensor(xr[h][:, j, :], psT[:, j * P:(j + 1) * P], rden[h][:, j:j + 1],
                                             xr[h][:, j, :], ALU.mult, ALU.add).then_inc(y_ready[h], 1)

            def step(i, g, first):
                h, c = g // CH, g % CH
                before = batch_before(i, h, first)
                gate(i, g)
                if back(i, g, 1, first):
                    j, k = back(i, g, 1)
                    weigh(j, k, first)
                if back(i, g, 2, first):
                    low_part(*back(i, g, 2))
                if c == TURN + 1 and before:
                    finish(*before)
                if c == SUMS + 2:
                    invert(i, h)

            run_pairs(dve, step)
            weigh(HB - 1, 2 * CH - 1)
            low_part(HB - 1, 2 * CH - 2)
            low_part(HB - 1, 2 * CH - 1)
            finish(HB - 1, 1)


def build(nc, a, out):
    with ExitStack() as ctx:
        def sb(name, shape, dt=F32):
            return ctx.enter_context(nc.sbuf_tensor(name, shape, dt))

        cst = sb("cst", [P, C_SEL])
        par = sb("par", [P, V_END + 1])
        st = sb("st", [P, NT, 6])
        score = sb("score", [P, HALF])
        xsave = nc.dram_tensor("xsave", [P, NT, P], F32).ap()
        tables_in = ctx.enter_context(nc.semaphore("tables_in"))
        eps_set = ctx.enter_context(nc.semaphore("eps_set"))
        with nc.Block() as block:
            @block.sync
            def _(sp):
                sp.dma_start(cst[:, :], a["cst"][:, 0:C_SEL]).then_inc(tables_in, 16)
                sp.dma_start(par[:, 0:V_END], a["par"]).then_inc(tables_in, 16)
                sp.wait_ge(tables_in, 32)

            @block.gpsimd
            def _(pool):
                pool.memset(par[:, V_END:V_END + 1], LN_EPS).then_inc(eps_set, 1)
                pool.wait_ge(eps_set, 1)

        with nc.sbuf_tensor("xres", [P, NT, P], F32, side="right") as xres:
            attention_phase(nc, a["x"], a["wqT"], a["wkvT"], a["wpT"], a["bp"], cst, par, xres, st)
            xH = sb("xH", [P, TOK], F32R)
            xL = sb("xL", [P, TOK], F32R)
            router_phase(nc, a["wr"], a["br"], cst, par, xres, st, xH, xL, score, xsave)
        wU = sb("wU", [P, 2, E * H], F32R)
        wG = sb("wG", [P, 2, E * H], F32R)
        wD = sb("wD", [P, 2, CH * P], F32R)
        selR = sb("selR", [P, CH * P], F32R)
        bdR = sb("bdR", [P, 2, P], F32R)
        onesR = sb("onesR", [P, 2], F32R)
        with (nc.sbuf_tensor("w_stage", [P, E * H], F32) as w_stage,
              nc.sbuf_tensor("bd_stage", [P, P], F32) as bd_stage):
            routing_phase(nc, a["wupT"], a["wgateT"], a["wdn"], a["bdn"], a["cst"][:, C_SEL:C_END], cst, score,
                                 wU, wG, wD, selR, bdR, onesR, w_stage, bd_stage)
        experts_phase(nc, out, xsave, par, cst, score, xH, xL, wU, wG, wD, selR, bdR, onesR)


def constants():
    import numpy as np
    k, m = np.arange(P)[:, None], np.arange(P)[None, :]
    c = np.zeros((P, C_END), np.float32)
    c[:, C_ID:C_ID + P] = k == m
    c[:, C_BLOCK:C_BLOCK + P] = k // HD == m // HD
    c[:, C_ONES:C_ONES + P] = 1.0
    c[:, C_PAIR:C_PAIR + P] = k % E == m % E
    c[:, C_FIRST:C_FIRST + P] = k + E == m
    c[:, C_TRI:C_TRI + E] = k < m[:, :E]
    c[:, C_HEAD:C_HEAD + HEADS] = k // HD == m[:, :HEADS]
    for n in range(CH):
        c[:, C_SEL + n * P:C_SEL + (n + 1) * P] = k % E == n * EPC + m // H
    return c


def kernel(**inputs):
    import numpy as np
    import concourse.bacc as bacc
    from concourse.bass_utils import run_bass_kernel_spmd

    v = {k: np.asarray(x) for k, x in inputs.items()}
    attn = lambda k: v["L0_attn_" + k]
    ffn = lambda k: v["L0_ffn_" + k]
    cols = lambda b: b.reshape(CH, P).T
    arrays = {
        "x": attn("x"),
        "wqT": attn("Wq").T,
        "wkvT": np.concatenate([attn("Wk").T, attn("Wv").T], axis=1),
        "wpT": attn("Wp").T,
        "bp": attn("bp").reshape(1, P),
        "wr": ffn("Wr"),
        "br": ffn("br"),
        "wupT": ffn("Wup").transpose(1, 0, 2).reshape(P, E * H),
        "wgateT": ffn("Wgate").transpose(1, 0, 2).reshape(P, E * H),
        "wdn": ffn("Wdown").reshape(CH, P, P).transpose(1, 0, 2).reshape(P, CH * P),
        "bdn": ffn("bdown"),
        "par": np.concatenate([attn("conv_w"), attn("conv_b").reshape(P, 1),
                               cols(ffn("bup")), cols(ffn("bgate"))], axis=1),
        "cst": constants(),
    }
    arrays = {k: np.ascontiguousarray(x) for k, x in arrays.items()}
    nc = bacc.Bacc("TRN2", target_bir_lowering=False, num_devices=1)
    aps = {k: nc.dram_tensor(k + "_dram", x.shape, F32, kind="ExternalInput").ap() for k, x in arrays.items()}
    out = nc.dram_tensor("out_dram", (BATCH, SEQ, P), F32, kind="ExternalOutput").ap()
    build(nc, aps, out)
    res = run_bass_kernel_spmd(nc, [{k + "_dram": x for k, x in arrays.items()}], core_ids=[0])
    return res.results[0]["out_dram"]
```

```python
from contextlib import ExitStack

import concourse.bass as bass
from concourse import mybir

F32 = mybir.dt.float32
F32R = mybir.dt.float32r
I32 = mybir.dt.int32
ALU = mybir.AluOpType
ACT = mybir.ActivationFunctionType
AX_X = mybir.AxisListType.X

P = 128
BATCH, SEQ = 16, 512
TOK = BATCH * SEQ
TT = SEQ // P
NT = TOK // P
HEADS, HD = 16, 8
E, H = 64, 32
CH = E * H // P
EPC = P // H
GROUP, KEEP = 64, 16
NG = TOK // GROUP
BUDGET = NG * KEEP
HALF = TOK // 2
HB = BATCH // 2
LN_EPS = 1e-5
DEN_EPS = 1e-6

SAMPLE = HALF // 4
LEVEL = 0x3C000000
LEVEL_BITS = range(24, 13, -1)
SPREAD = 0.025
SLACK = 20.0
ROUNDS = 2
CHUNK = 32
FOUND = HALF // CHUNK * 8
RUN = 256
WG = 2 * RUN // GROUP
ROUND = float(1 << 23)
ABOVE = 1e6

C_ID, C_BLOCK, C_ONES, C_PAIR, C_IOTA, C_TRI, C_HEAD, C_SEL = 0, 128, 256, 384, 512, 640, 704, 720
C_END = C_SEL + CH * P
V_CONV, V_CONVB, V_BUP, V_BGATE = 0, 3, 4, 4 + CH
V_END = 4 + 2 * CH


ONE = 1


def start_semaphores(nc, sems, zeros=()):
    with nc.Block() as block:
        @block.vector
        def _(dve):
            for s in zeros:
                dve.sem_clear(s)

        @block.sync
        def _(sp):
            for s in sems[0::3]:
                sp.sem_clear(s)
                sp.sem_inc(s, ONE)

        @block.scalar
        def _(act):
            for s in sems[1::3]:
                act.sem_clear(s)
                act.sem_inc(s, ONE)

        @block.tensor
        def _(pe):
            for s in sems[2::3]:
                pe.sem_clear(s)
                pe.sem_inc(s, ONE)


def fold_statistics(dve, st, tmp, mean, chain):
    dve.tensor_tensor(tmp[:, 0, :], st[:, :, 1], st[:, :, 4], ALU.add).then_inc(chain, 1)
    dve.tensor_tensor(tmp[:, 1, :], st[:, :, 1], st[:, :, 4], ALU.subtract).then_inc(chain, 1)
    dve.tensor_tensor(tmp[:, 2, :], st[:, :, 2], st[:, :, 5], ALU.add).then_inc(chain, 1)
    dve.wait_ge(chain, ONE + 3)
    dve.tensor_scalar(mean[:, :], tmp[:, 0, :], 0.5, None, ALU.mult).then_inc(chain, 1)
    dve.tensor_tensor(tmp[:, 3, :], tmp[:, 1, :], tmp[:, 1, :], ALU.mult).then_inc(chain, 1)
    dve.wait_ge(chain, ONE + 5)
    dve.scalar_tensor_tensor(tmp[:, 4, :], tmp[:, 3, :], P / 4.0, tmp[:, 2, :], ALU.mult, ALU.add).then_inc(chain, 1)


def run_slots(eng, slot):
    n = BATCH // 2
    slot((0, 0), None, None)
    slot((0, 1), (0, 0), None)
    with eng.Fori(0, n - 1) as i:
        slot((i + 1, 0), (i, 1), (i, 0))
        slot((i + 1, 1), (i + 1, 0), (i, 1))
    slot(None, (n - 1, 1), (n - 1, 0))
    slot(None, None, (n - 1, 1))


def attention_phase(nc, x, wqT, wkvT, wpT, bp, cst, par, xres, st):
    sems = []
    with ExitStack() as ctx:
        def sb(name, shape, dt=F32):
            return ctx.enter_context(nc.sbuf_tensor(name, shape, dt))

        def sb2(name, shape, dt=F32):
            return [sb(f"{name}{u}", shape, dt) for u in range(2)]

        def ps2(name, shape):
            return [ctx.enter_context(nc.psum_tensor(f"{name}{u}", shape, F32)) for u in range(2)]

        def sem(name):
            sems.append(ctx.enter_context(nc.semaphore(name)))
            return sems[-1]

        def sem2(name):
            return [sem(f"{name}{u}") for u in range(2)]

        wq_sb = sb("wq_sb", [P, P])
        wkv_sb = sb("wkv_sb", [P, 2 * P])
        wp_sb = sb("wp_sb", [P, P])
        bp_sb = sb("bp_sb", [1, SEQ])
        rstd = sb("rstd", [P, NT])
        std = sb("std", [P, NT])
        tmp = sb("tmp", [P, 5, NT])
        mean = sb("mean", [P, NT])
        x2s = sb2("x2s", [P, TT, P])
        bst = sb2("bst", [P, TT, 6])
        stat = sb2("stat", [P, 2, TT])
        xn = sb2("xn", [P, TT, P])
        xnT = sb2("xnT", [P, SEQ + 2])
        eq = sb2("eq", [P, SEQ])
        rq = sb2("rq", [P, SEQ])
        ek = sb2("ek", [P, TT, P])
        rk = sb2("rk", [P, TT, P])
        qT = sb2("qT", [P, SEQ])
        kk = sb2("kk", [P, TT, P])
        v1 = sb2("v1", [P, TT, P + 1])
        loc0 = sb2("loc0", [P, SEQ])
        loc1 = sb2("loc1", [P, SEQ])
        loc2 = sb2("loc2", [P, SEQ])
        kvs = sb2("kvs", [P, P + HEADS])
        den = sb2("den", [P, TT, HEADS])
        rden = sb2("rden", [P, TT, HEADS])
        att = sb2("att", [P, TT, P])
        yT = sb2("yT", [P, SEQ])
        psT = ps2("psT", [P, SEQ])
        psQ = ps2("psQ", [P, SEQ])
        psKV = ps2("psKV", [P, TT, 2 * P])

        x_in = [sem(f"x_in{k}") for k in range(4)]
        w_in = sem("w_in")
        staged = sem2("staged")
        bn1_done = sem2("bn1_done")
        st1_done = sem2("st1_done")
        st2_done = sem2("st2_done")
        var_done = sem("var_done")
        x2_kept = sem2("x2_kept")
        std_done = sem("std_done")
        rstd_done = sem("rstd_done")
        pads_done = sem("pads_done")
        stat_done = sem2("stat_done")
        xn_ready = sem2("xn_ready")
        xT_ps = sem2("xT_ps")
        xnT_ready = sem2("xnT_ready")
        q_ps = sem2("q_ps")
        kv_ps = sem2("kv_ps")
        q_act = sem2("q_act")
        kv_act = sem2("kv_act")
        loc0_ready = sem2("loc0_ready")
        loc1_ready = sem2("loc1_ready")
        loc2_ready = sem2("loc2_ready")
        q_ready = sem2("q_ready")
        k_ready = sem2("k_ready")
        kvs_ps = sem2("kvs_ps")
        kvs_ready = sem2("kvs_ready")
        at_ps = sem2("at_ps")
        den_done = sem2("den_done")
        rden_done = sem2("rden_done")
        at_ready = sem2("at_ready")
        aT_ps = sem2("aT_ps")
        y_ready = sem2("y_ready")
        o_ps = sem2("o_ps")
        x2_ready = sem2("x2_ready")
        bn2_done = sem2("bn2_done")

        NX = 4
        start_semaphores(nc, sems)
        block = ctx.enter_context(nc.Block())

        @block.sync
        def _(sp):
            xt = x.rearrange("b (j p) d -> p (b j) d", p=P)
            for k in range(NX):
                n = NT // NX
                sp.dma_start(xres[:, k * n:(k + 1) * n, :], xt[:, k * n:(k + 1) * n, :]).then_inc(x_in[k], 16)

        @block.gpsimd
        def _(pool):
            for u in range(2):
                pool.memset(xnT[u][:, 0:1], 0.0).then_inc(pads_done, 1)
                pool.memset(xnT[u][:, SEQ + 1:SEQ + 2], 0.0).then_inc(pads_done, 1)
                pool.memset(v1[u][:, :, P:P + 1], 1.0).then_inc(pads_done, 1)
            for k in range(NX):
                pool.wait_ge(x_in[k], ONE + 16)
                with pool.Fori(k * BATCH // NX // 2, (k + 1) * BATCH // NX // 2) as i:
                    for u in range(2):
                        pool.wait_ge(bn1_done[u], ONE + TT * i)
                        pool.tensor_copy(x2s[u][:, :, :], xres[:, bass.ds((2 * i + u) * TT, TT), :]).then_inc(staged[u], 1)
            with pool.Fori(0, BATCH // 2) as i:
                for u in range(2):
                    pool.wait_ge(x2_ready[u], ONE + i + 1)
                    pool.tensor_copy(xres[:, bass.ds((2 * i + u) * TT, TT), :], x2s[u][:, :, :]).then_inc(x2_kept[u], 1)

        @block.scalar
        def _(act):
            for dst, src in ((wq_sb[:, :], wqT), (wkv_sb[:, :], wkvT), (wp_sb[:, :], wpT), (bp_sb[:, :], bp)):
                act.dma_start(dst, src).then_inc(w_in, 16)
            act.wait_ge(var_done, ONE + 6)
            act.activation(std[:, :], tmp[:, 4, :], ACT.Sqrt, bias=par[:, V_END:V_END + 1],
                           scale=1.0 / P).then_inc(std_done, 1)
            act.wait_ge(pads_done, ONE + 6)

            def slot(ahead, front, back):
                if front:
                    i, u = front
                    act.wait_ge(xT_ps[u], ONE + i + 1)
                    act.wait_ge(loc2_ready[u], ONE + i)
                    act.activation(xnT[u][:, 1:SEQ + 1], psT[u][:, :], ACT.Copy).then_inc(xnT_ready[u], 1)
                    act.wait_ge(q_ps[u], ONE + i + 1)
                    act.wait_ge(q_ready[u], ONE + i)
                    act.activation(eq[u][:, :], psQ[u][:, :], ACT.Exp).then_inc(q_act[u], 1)
                    act.activation(rq[u][:, :], psQ[u][:, :], ACT.Relu).then_inc(q_act[u], 1)
                    act.wait_ge(kv_ps[u], ONE + i + 1)
                    act.wait_ge(k_ready[u], ONE + i)
                    act.activation(ek[u][:, :, :], psKV[u][:, :, 0:P], ACT.Exp).then_inc(kv_act[u], 1)
                    act.activation(rk[u][:, :, :], psKV[u][:, :, 0:P], ACT.Relu).then_inc(kv_act[u], 1)
                    act.wait_ge(kvs_ps[u], ONE + i)
                    act.activation(v1[u][:, :, 0:P], psKV[u][:, :, P:2 * P], ACT.Copy).then_inc(kv_act[u], 1)
                    act.wait_ge(xnT_ready[u], ONE + i + 1)
                    act.wait_ge(loc1_ready[u], ONE + i)
                    act.activation(loc0[u][:, :], xnT[u][:, 1:SEQ + 1], ACT.Identity,
                                   bias=par[:, V_CONVB:V_CONVB + 1],
                                   scale=par[:, V_CONV + 1:V_CONV + 2]).then_inc(loc0_ready[u], 1)

            run_slots(act, slot)

        @block.tensor
        def _(pe):
            pe.wait_ge(w_in, ONE + 64)

            def turn_rows(i, u):
                pe.wait_ge(xn_ready[u], ONE + TT * i + TT)
                pe.wait_ge(y_ready[u], ONE + i)
                for j in range(TT):
                    mm = pe.transpose(psT[u][:, j * P:(j + 1) * P], xn[u][:, j, :], cst[:, C_ID:C_ID + P])
                mm.then_inc(xT_ps[u], 1)

            def query(i, u):
                pe.wait_ge(xnT_ready[u], ONE + i + 1)
                pe.wait_ge(x2_ready[u], ONE + i)
                pe.matmul(psQ[u][:, :], wq_sb[:, :], xnT[u][:, 1:SEQ + 1],
                          start=True, stop=True).then_inc(q_ps[u], 1)

            def key_value(i, u):
                pe.wait_ge(at_ready[u], ONE + i)
                for j in range(TT):
                    mm = pe.matmul(psKV[u][:, j, :], xnT[u][:, 1 + j * P:1 + (j + 1) * P], wkv_sb[:, :],
                                   start=True, stop=True)
                mm.then_inc(kv_ps[u], 1)

            def states(i, u):
                pe.wait_ge(k_ready[u], ONE + i + 1)
                pe.wait_ge(kv_act[u], ONE + 3 * i + 3)
                for j in range(TT):
                    mm = pe.matmul(psKV[u][:, 0, 0:P + 1], kk[u][:, j, :], v1[u][:, j, :],
                                   start=(j == 0), stop=(j == TT - 1))
                mm.then_inc(kvs_ps[u], 1)

            def attend(i, u):
                pe.wait_ge(kvs_ready[u], ONE + 2 * i + 2)
                pe.wait_ge(q_ready[u], ONE + i + 1)
                for j in range(TT):
                    mm = pe.matmul(psKV[u][:, j, 0:P + HEADS], qT[u][:, j * P:(j + 1) * P], kvs[u][:, :],
                                   start=True, stop=True)
                mm.then_inc(at_ps[u], 1)

            def turn_attention(i, u):
                pe.wait_ge(at_ready[u], ONE + i + 1)
                for j in range(TT):
                    mm = pe.transpose(psT[u][:, j * P:(j + 1) * P], att[u][:, j, :], cst[:, C_ID:C_ID + P])
                mm.then_inc(aT_ps[u], 1)

            def project(i, u):
                pe.wait_ge(y_ready[u], ONE + i + 1)
                for j in range(TT):
                    mm = pe.matmul(psQ[u][:, j * P:(j + 1) * P], yT[u][:, j * P:(j + 1) * P], wp_sb[:, :],
                                   start=False, stop=(j == TT - 1))
                mm.then_inc(o_ps[u], 1)

            def slot(ahead, front, back):
                if front:
                    turn_rows(*front)
                if back:
                    states(*back)
                    i, u = back
                    pe.wait_ge(q_act[u], ONE + 2 * i + 2)
                    pe.matmul(psQ[u][:, :], cst[0:1, C_ONES:C_ONES + P], bp_sb[:, :], start=True, stop=False)
                if front:
                    query(*front)
                if back:
                    attend(*back)
                if front:
                    key_value(*front)
                if back:
                    turn_attention(*back)
                    project(*back)

            run_slots(pe, slot)

        @block.vector
        def _(dve):
            with dve.Fori(0, BATCH // 2) as i:
                for u in range(2):
                    dve.wait_ge(staged[u], ONE + i + 1)
                    dve.wait_ge(st1_done[u], ONE + i)
                    for j in range(TT):
                        dve.bn_stats(bst[u][:, j, :], x2s[u][:, j, :]).then_inc(bn1_done[u], 1)
                for u in range(2):
                    dve.wait_ge(bn1_done[u], ONE + TT * i + TT)
                    dve.tensor_scalar(st[:, bass.ds((2 * i + u) * TT, TT), :], bst[u][:, :, :], 1.0, None,
                                      ALU.mult).then_inc(st1_done[u], 1)
            for u in range(2):
                dve.wait_ge(st1_done[u], ONE + BATCH // 2)
            fold_statistics(dve, st, tmp, mean, var_done)
            dve.wait_ge(std_done, ONE + 1)
            dve.reciprocal(rstd[:, :], std[:, :]).then_inc(rstd_done, 1)
            dve.wait_ge(rstd_done, ONE + 1)

            def normalise(i, u):
                t0 = (2 * i + u) * TT
                dve.wait_ge(xn_ready[u], ONE + TT * i)
                dve.tensor_scalar(stat[u][:, 0, :], mean[:, bass.ds(t0, TT)], 1.0, None,
                                  ALU.mult).then_inc(stat_done[u], 1)
                dve.tensor_scalar(stat[u][:, 1, :], rstd[:, bass.ds(t0, TT)], 1.0, None,
                                  ALU.mult).then_inc(stat_done[u], 1)
                dve.wait_ge(stat_done[u], ONE + 2 * i + 2)
                dve.wait_ge(xT_ps[u], ONE + i)
                for j in range(TT):
                    dve.tensor_scalar(xn[u][:, j, :], xres[:, bass.ds(t0 + j, 1), :], stat[u][:, 0, j:j + 1],
                                      stat[u][:, 1, j:j + 1], ALU.subtract, ALU.mult).then_inc(xn_ready[u], 1)

            def feature_maps(i, u):
                dve.wait_ge(q_act[u], ONE + 2 * i + 2)
                dve.wait_ge(at_ps[u], ONE + i)
                dve.scalar_tensor_tensor(qT[u][:, :], eq[u][:, :], 1.0, rq[u][:, :],
                                         ALU.min, ALU.add).then_inc(q_ready[u], 1)
                dve.wait_ge(kv_act[u], ONE + 3 * i + 2)
                dve.wait_ge(kvs_ps[u], ONE + i)
                dve.scalar_tensor_tensor(kk[u][:, :, :], ek[u][:, :, :], 1.0, rk[u][:, :, :],
                                         ALU.min, ALU.add).then_inc(k_ready[u], 1)

            def first_tap(i, u):
                dve.wait_ge(loc0_ready[u], ONE + i + 1)
                dve.wait_ge(loc2_ready[u], ONE + i)
                dve.scalar_tensor_tensor(loc1[u][:, :], xnT[u][:, 0:SEQ], par[:, V_CONV:V_CONV + 1],
                                         loc0[u][:, :], ALU.mult, ALU.add).then_inc(loc1_ready[u], 1)

            def last_tap(i, u):
                dve.wait_ge(loc1_ready[u], ONE + i + 1)
                dve.wait_ge(y_ready[u], ONE + i)
                dve.scalar_tensor_tensor(loc2[u][:, :], xnT[u][:, 2:SEQ + 2], par[:, V_CONV + 2:V_CONV + 3],
                                         loc1[u][:, :], ALU.mult, ALU.add).then_inc(loc2_ready[u], 1)

            def mask_states(i, u):
                dve.wait_ge(kvs_ps[u], ONE + i + 1)
                dve.wait_ge(at_ps[u], ONE + i)
                dve.tensor_tensor(kvs[u][:, 0:P], psKV[u][:, 0, 0:P], cst[:, C_BLOCK:C_BLOCK + P],
                                  ALU.mult).then_inc(kvs_ready[u], 1)
                dve.tensor_scalar(kvs[u][:, P:P + HEADS], cst[:, C_HEAD:C_HEAD + HEADS],
                                  psKV[u][:, 0, P:P + 1], None, ALU.mult).then_inc(kvs_ready[u], 1)

            def divide(i, u):
                dve.wait_ge(at_ps[u], ONE + i + 1)
                dve.wait_ge(rden_done[u], ONE + i)
                dve.tensor_scalar(den[u][:, :, :], psKV[u][:, :, P:P + HEADS], 1e-6, None,
                                  ALU.max).then_inc(den_done[u], 1)
                dve.wait_ge(den_done[u], ONE + i + 1)
                dve.wait_ge(at_ready[u], ONE + i)
                dve.reciprocal(rden[u][:, :, :], den[u][:, :, :]).then_inc(rden_done[u], 1)
                dve.wait_ge(rden_done[u], ONE + i + 1)
                dve.wait_ge(aT_ps[u], ONE + i)
                dve.tensor_tensor(att[u][:, :, :].rearrange("p j (h e) -> p j h e", e=HD),
                                  psKV[u][:, :, 0:P].rearrange("p j (h e) -> p j h e", e=HD),
                                  rden[u][:, :, :].unsqueeze(3).broadcast_to([P, TT, HEADS, HD]),
                                  ALU.mult).then_inc(at_ready[u], 1)

            def add_local(i, u):
                dve.wait_ge(aT_ps[u], ONE + i + 1)
                dve.wait_ge(loc2_ready[u], ONE + i + 1)
                dve.wait_ge(o_ps[u], ONE + i)
                dve.tensor_tensor(yT[u][:, :], psT[u][:, :], loc2[u][:, :], ALU.add).then_inc(y_ready[u], 1)

            def add_residual(i, u):
                dve.wait_ge(o_ps[u], ONE + i + 1)
                dve.wait_ge(x2_kept[u], ONE + i)
                dve.tensor_tensor(x2s[u][:, :, :], psQ[u][:, :].rearrange("p (j d) -> p j d", d=P),
                                  xres[:, bass.ds((2 * i + u) * TT, TT), :], ALU.add).then_inc(x2_ready[u], 1)

            def statistics(i, u):
                dve.wait_ge(x2_ready[u], ONE + i + 1)
                dve.wait_ge(st2_done[u], ONE + i)
                for j in range(TT):
                    dve.bn_stats(bst[u][:, j, :], x2s[u][:, j, :]).then_inc(bn2_done[u], 1)
                dve.wait_ge(bn2_done[u], ONE + TT * i + TT)
                dve.tensor_scalar(st[:, bass.ds((2 * i + u) * TT, TT), :], bst[u][:, :, :], 1.0, None,
                                  ALU.mult).then_inc(st2_done[u], 1)

            def slot(ahead, front, back):
                if back:
                    mask_states(*back)
                    first_tap(*back)
                if ahead:
                    normalise(*ahead)
                if back:
                    divide(*back)
                    last_tap(*back)
                    add_local(*back)
                if front:
                    feature_maps(*front)
                if back:
                    add_residual(*back)
                    statistics(*back)

            run_slots(dve, slot)


def router_phase(nc, wr, br, cst, par, xres, st, xH, xL, score, xsave):
    sems = []
    with ExitStack() as ctx:
        def sb(name, shape, dt=F32):
            return ctx.enter_context(nc.sbuf_tensor(name, shape, dt))

        def sb2(name, shape, dt=F32):
            return [sb(f"{name}{u}", shape, dt) for u in range(2)]

        def ps2(name, shape):
            return [ctx.enter_context(nc.psum_tensor(f"{name}{u}", shape, F32)) for u in range(2)]

        def sem(name):
            sems.append(ctx.enter_context(nc.semaphore(name)))
            return sems[-1]

        def sem2(name):
            return [sem(f"{name}{u}") for u in range(2)]

        wr_sb = sb("wr_sb", [P, E])
        br_sb = sb("br_sb", [P, E])
        tmp = sb("r_tmp", [P, 5, NT])
        mean = sb("r_mean", [P, NT])
        std = sb("r_std", [P, NT])
        rstd = sb("r_rstd", [P, NT])
        stat = sb2("r_stat", [P, 2, TT])
        xn = sb2("r_xn", [P, TT, P])
        xT = sb2("r_xT", [P, SEQ])
        lg = sb2("r_lg", [P, TT, E])
        lc = sb2("r_lc", [P, TT, E])
        mx = sb2("r_mx", [P, TT])
        ex = sb2("r_ex", [P, TT, E])
        sm = sb2("r_sm", [P, TT])
        rs = sb2("r_rs", [P, TT])
        pr = sb2("r_pr", [P, TT, E])
        psT = ps2("r_psT", [P, SEQ])
        psR = ps2("r_psR", [P, TT, E])
        psS = ps2("r_psS", [P, TT // 2, P])

        w_in = sem("r_w_in")
        saved = sem("r_saved")
        var_done = sem("r_var_done")
        std_done = sem("r_std_done")
        rstd_done = sem("r_rstd_done")
        stat_done = sem2("r_stat_done")
        xn_ready = sem2("r_xn_ready")
        xT_ps = sem2("r_xT_ps")
        xT_ready = sem2("r_xT_ready")
        xH_ready = sem2("r_xH_ready")
        xL_ready = sem2("r_xL_ready")
        lg_ps = sem2("r_lg_ps")
        lg_done = sem2("r_lg_done")
        mx_done = sem2("r_mx_done")
        lc_done = sem2("r_lc_done")
        ex_done = sem2("r_ex_done")
        sm_done = sem2("r_sm_done")
        rs_done = sem2("r_rs_done")
        pr_done = sem2("r_pr_done")
        pT_ps = sem2("r_pT_ps")
        sc_done = sem2("r_sc_done")

        start_semaphores(nc, sems)
        block = ctx.enter_context(nc.Block())

        @block.sync
        def _(sp):
            sp.dma_start(wr_sb[:, :], wr).then_inc(w_in, 16)
            sp.dma_start(br_sb[:, :], br.partition_broadcast(P)).then_inc(w_in, 16)
            sp.dma_start(xsave, xres[:, :, :]).then_inc(saved, 16)
            sp.wait_ge(saved, ONE + 16)

        @block.scalar
        def _(act):
            act.wait_ge(var_done, ONE + 6)
            act.activation(std[:, :], tmp[:, 4, :], ACT.Sqrt, bias=par[:, V_END:V_END + 1],
                           scale=1.0 / P).then_inc(std_done, 1)

            def slot(ahead, front, back):
                if front:
                    i, u = front
                    act.wait_ge(xT_ps[u], ONE + i + 1)
                    act.wait_ge(lg_ps[u], ONE + i)
                    act.wait_ge(xL_ready[u], ONE + i)
                    act.activation(xT[u][:, :], psT[u][:, :], ACT.Copy).then_inc(xT_ready[u], 1)
                    act.activation(xH[:, bass.ds((i + u * HB) * SEQ, SEQ)], psT[u][:, :],
                                   ACT.Copy).then_inc(xH_ready[u], 1)
                if back:
                    i, u = back
                    act.wait_ge(lc_done[u], ONE + i + 1)
                    act.wait_ge(pr_done[u], ONE + i)
                    act.activation(ex[u][:, :, :], lc[u][:, :, :], ACT.Exp).then_inc(ex_done[u], 1)
                    act.wait_ge(pT_ps[u], ONE + i + 1)
                    dst = score[u * E:(u + 1) * E, bass.ds(i * SEQ, SEQ)].rearrange("e (a r t) -> e a r t", r=2, t=P)
                    for r in range(2):
                        act.activation(dst[:, :, r, :], psS[u][r * E:(r + 1) * E, :, :],
                                       ACT.Copy).then_inc(sc_done[u], 1)

            run_slots(act, slot)

        @block.gpsimd
        def _(pool):
            with pool.Fori(0, HB) as i:
                for u in range(2):
                    pool.wait_ge(xH_ready[u], ONE + i + 1)
                    at = bass.ds((i + u * HB) * SEQ, SEQ)
                    pool.tensor_tensor(xL[:, at], xT[u][:, :], xH[:, at].bitcast(F32),
                                       ALU.subtract).then_inc(xL_ready[u], 1)

        @block.tensor
        def _(pe):
            pe.wait_ge(w_in, ONE + 32)

            def slot(ahead, front, back):
                if front:
                    i, u = front
                    pe.wait_ge(xn_ready[u], ONE + TT * i + TT)
                    pe.wait_ge(xH_ready[u], ONE + i)
                    for j in range(TT):
                        mm = pe.transpose(psT[u][:, j * P:(j + 1) * P], xn[u][:, j, :], cst[:, C_ID:C_ID + P])
                    mm.then_inc(xT_ps[u], 1)
                    pe.wait_ge(xT_ready[u], ONE + i + 1)
                    pe.wait_ge(lg_done[u], ONE + i)
                    for j in range(TT):
                        mm = pe.matmul(psR[u][:, j, :], xT[u][:, j * P:(j + 1) * P], wr_sb[:, :],
                                       start=True, stop=True)
                    mm.then_inc(lg_ps[u], 1)
                if back:
                    i, u = back
                    pe.wait_ge(pr_done[u], ONE + i + 1)
                    pe.wait_ge(sc_done[u], ONE + 2 * i)
                    for j in range(0, TT, 2):
                        mm = pe.transpose(psS[u][:, j // 2, :], pr[u][:, j:j + 2, :].rearrange("p a e -> p (a e)"),
                                          cst[:, C_ID:C_ID + P])
                    mm.then_inc(pT_ps[u], 1)

            run_slots(pe, slot)

        @block.vector
        def _(dve):
            fold_statistics(dve, st, tmp, mean, var_done)
            dve.wait_ge(std_done, ONE + 1)
            dve.reciprocal(rstd[:, :], std[:, :]).then_inc(rstd_done, 1)
            dve.wait_ge(rstd_done, ONE + 1)
            dve.wait_ge(w_in, ONE + 32)

            def normalise(i, u):
                t0 = (i + u * HB) * TT
                dve.wait_ge(xn_ready[u], ONE + TT * i)
                dve.tensor_scalar(stat[u][:, 0, :], mean[:, bass.ds(t0, TT)], 1.0, None,
                                  ALU.mult).then_inc(stat_done[u], 1)
                dve.tensor_scalar(stat[u][:, 1, :], rstd[:, bass.ds(t0, TT)], 1.0, None,
                                  ALU.mult).then_inc(stat_done[u], 1)
                dve.wait_ge(stat_done[u], ONE + 2 * i + 2)
                dve.wait_ge(xT_ps[u], ONE + i)
                for j in range(TT):
                    dve.tensor_scalar(xn[u][:, j, :], xres[:, bass.ds(t0 + j, 1), :], stat[u][:, 0, j:j + 1],
                                      stat[u][:, 1, j:j + 1], ALU.subtract, ALU.mult).then_inc(xn_ready[u], 1)

            def shift(i, u):
                dve.wait_ge(lg_ps[u], ONE + i + 1)
                dve.wait_ge(lc_done[u], ONE + i)
                dve.tensor_tensor(lg[u][:, :, :], psR[u][:, :, :],
                                  br_sb[:, :].unsqueeze(1).broadcast_to([P, TT, E]),
                                  ALU.add).then_inc(lg_done[u], 1)
                dve.wait_ge(lg_done[u], ONE + i + 1)
                dve.tensor_reduce(mx[u][:, :], lg[u][:, :, :], AX_X, ALU.max).then_inc(mx_done[u], 1)
                dve.wait_ge(mx_done[u], ONE + i + 1)
                dve.wait_ge(ex_done[u], ONE + i)
                dve.tensor_tensor(lc[u][:, :, :], lg[u][:, :, :],
                                  mx[u][:, :].unsqueeze(2).broadcast_to([P, TT, E]),
                                  ALU.subtract).then_inc(lc_done[u], 1)

            def scale(i, u):
                dve.wait_ge(ex_done[u], ONE + i + 1)
                dve.wait_ge(rs_done[u], ONE + i)
                dve.tensor_reduce(sm[u][:, :], ex[u][:, :, :], AX_X, ALU.add).then_inc(sm_done[u], 1)
                dve.wait_ge(sm_done[u], ONE + i + 1)
                dve.wait_ge(pr_done[u], ONE + i)
                dve.reciprocal(rs[u][:, :], sm[u][:, :]).then_inc(rs_done[u], 1)
                dve.wait_ge(rs_done[u], ONE + i + 1)
                dve.wait_ge(pT_ps[u], ONE + i)
                dve.tensor_tensor(pr[u][:, :, :], ex[u][:, :, :],
                                  rs[u][:, :].unsqueeze(2).broadcast_to([P, TT, E]),
                                  ALU.mult).then_inc(pr_done[u], 1)

            def slot(ahead, front, back):
                if back:
                    shift(*back)
                if ahead:
                    normalise(*ahead)
                if back:
                    scale(*back)

            run_slots(dve, slot)


def merge_steps(first, last):
    steps = []
    block = 2 * first
    while block <= last:
        steps.append((block, 0))
        steps += halving_steps(block // 2, 1)
        block *= 2
    return steps


def halving_steps(block, down_to):
    steps = []
    while block // 2 >= down_to:
        steps.append((block, block // 2))
        block //= 2
    return steps


class Tally:

    def __init__(self):
        self.total = 0

    def one(self):
        self.total += 1
        return 1


def sort_step(dve, src, dst, step, sem, tally):
    k, d = step
    if d:
        a = src.rearrange("p (n t d) -> p n t d", t=2, d=d)
        o = dst.rearrange("p (n t d) -> p n t d", t=2, d=d)
        i0, i1, o0, o1 = a[:, :, 0], a[:, :, 1], o[:, :, 0], o[:, :, 1]
    else:
        a = src.rearrange("p (n k) -> p n k", k=k)
        o = dst.rearrange("p (n k) -> p n k", k=k)
        i0, i1 = a[:, :, 0:k // 2], a[:, :, k - 1:k // 2 - 1:-1]
        o0, o1 = o[:, :, 0:k // 2], o[:, :, k - 1:k // 2 - 1:-1]
    dve.wait_ge(sem, ONE + tally.total)
    dve.tensor_tensor(o0, i0, i1, ALU.max).then_inc(sem, tally.one())
    dve.tensor_tensor(o1, i0, i1, ALU.min).then_inc(sem, tally.one())


def routing_phase(nc, wupT, wgateT, wdn, bdn, sel, cst, score, wU, wG, wD, selR, bdR, onesR, w_stage, bd_stage):
    sems = []
    with ExitStack() as ctx:
        def sb(name, shape, dt=F32):
            return ctx.enter_context(nc.sbuf_tensor(name, shape, dt))

        def sem(name):
            sems.append(ctx.enter_context(nc.semaphore(name)))
            return sems[-1]

        bufs = [sb("sort0", [P, HALF]), sb("sort1", [P, HALF])]
        runs = [sb("runs0", [P, FOUND]), sb("runs1", [P, FOUND])]
        level = sb("level", [P, 1], I32)
        ldec = sb("ldec", [P, 1], I32)
        lcnt = sb("lcnt", [P, 1])
        limit = [sb(f"limit{n}", [P, 2]) for n in range(2 + ROUNDS)]
        ranks = [sb(f"ranks{n}", [P, 2]) for n in range(2 + ROUNDS)]
        hcnt = [sb(f"hcnt{n}", [P, 2]) for n in range(1 + ROUNDS)]
        whole = sb("whole", [P, 4])
        goal = sb("goal", [P, 2])
        must = sb("must", [P, 2])
        num = sb("num", [P, 2])
        den = sb("r_den", [P, 2])
        move = sb("move", [P, 2])
        cap = sb("cap", [P, 2])
        empty = sb("empty", [P, 1])
        first = sb("first", [P, 1])
        pads = sb("pads", [P, 1])
        padrow = sb("padrow", [P, RUN])
        missed = sb("missed", [P, 6])
        miss_all = sb("miss_all", [1, 1], I32)
        pair = [sb("pair0", [E, 2 * RUN]), sb("pair1", [E, 2 * RUN])]
        wsum = sb("wsum", [E, WG])
        wmin = sb("wmin", [E, WG])
        rel = sb("rel", [E, NG])
        at = [sb(f"at{n}", [E, NG]) for n in range(2)]
        gsum = sb("gsum", [P, NG // 2])
        gmin = sb("gmin", [P, NG // 2])
        G = sb("G", [E, NG])
        M = sb("M", [E, NG])
        cand = sb("cand", [E, 1], I32)
        dec = sb("dec", [E, 1], I32)
        cnt = sb("cnt", [E, 1])
        junk = sb("junk", [E, NG])
        gt = sb("gt", [E, NG])
        eqg = sb("eqg", [E, NG])
        left = sb("left", [E, 1])
        cum = sb("cum", [E, NG])
        pos = sb("pos", [E, NG])
        tot = sb("tot", [E, NG])
        take = sb("take", [E, NG])
        kept = sb("kept", [E, NG])
        big = sb("big", [E, NG])
        mins = sb("mins", [E, NG])
        lim = sb("lim", [E, 2])
        lim2 = sb("lim2", [P, 2])
        reach = sb("reach", [P, 2])
        excess = sb("excess", [1, 1], I32)
        same = sb("same", [P, 1])
        above = sb("above", [P, 1])
        other = sb("other", [P, 1])
        before = sb("before", [P, 1])
        room = sb("room", [P, 1])
        psC = ctx.enter_context(nc.psum_tensor("psC", [E, 1], F32))
        psA = ctx.enter_context(nc.psum_tensor("psA", [E, NG], F32))
        psB = ctx.enter_context(nc.psum_tensor("psB", [E, NG], F32))
        psS = ctx.enter_context(nc.psum_tensor("psS", [P, 1], F32))
        psK = ctx.enter_context(nc.psum_tensor("psK", [P, 2], F32))
        psQ = ctx.enter_context(nc.psum_tensor("psQ", [P, 2], F32))
        psX = ctx.enter_context(nc.psum_tensor("psX", [1, 1], F32))

        sorted_ = sem("sorted_")
        window = sem("window")
        level_ready = sem("level_ready")
        level_counted = sem("level_counted")
        level_ps = sem("level_ps")
        limits_counted = sem("limits_counted")
        limits_ps = sem("limits_ps")
        groups_ready = sem("groups_ready")
        groups_ps = sem("groups_ps")
        missed_ready = sem("missed_ready")
        missed_ps = sem("missed_ps")
        gathered = sem("gathered")
        cand_ready = sem("cand_ready")
        cnt_ready = sem("cnt_ready")
        cnt_ps = sem("cnt_ps")
        dec_ready = sem("dec_ready")
        tie_in = sem("tie_in")
        tie_ps = sem("tie_ps")
        chain = sem("chain")
        lim_ready = sem("lim_ready")
        lim_moved = sem("lim_moved")
        reach_ready = sem("reach_ready")
        reach_ps = sem("reach_ps")
        tied = sem("tied")
        w_in = [sem(f"w_in_{n}") for n in ("u", "g", "d", "s", "b")]
        w_high = sem("w_high")
        w_low = sem("w_low")
        bd_zero = sem("bd_zero")

        start_semaphores(nc, sems)
        block = ctx.enter_context(nc.Block())

        @block.sync
        def _(sp):
            sp.dma_start(w_stage[:, :], wupT).then_inc(w_in[0], 16)
            for r in range(0, P, E):
                sp.dma_start(bd_stage[r:r + E, :], bdn).then_inc(w_in[4], 16)
            sp.wait_ge(w_low, ONE + 1)
            sp.dma_start(w_stage[:, :], wgateT).then_inc(w_in[1], 16)
            sp.wait_ge(w_low, ONE + 2)
            sp.dma_start(w_stage[:, :], wdn).then_inc(w_in[2], 16)
            sp.wait_ge(w_low, ONE + 3)
            sp.dma_start(w_stage[:, :], sel).then_inc(w_in[3], 16)

        @block.gpsimd
        def _(pool):
            pool.memset(bdR[E:P, 1, :].bitcast(F32), 0.0).then_inc(bd_zero, 1)
            pool.wait_ge(bd_zero, ONE + 1)
            for n, w in enumerate((wU, wG, wD)):
                pool.wait_ge(w_high, ONE + n + 1)
                pool.tensor_tensor(w[:, 1, :], w_stage[:, :], w[:, 0, :].bitcast(F32),
                                   ALU.subtract).then_inc(w_low, 1)
            pool.wait_ge(w_high, ONE + 4)
            pool.wait_ge(w_low, ONE + 3)
            pool.tensor_tensor(bdR[0:E, 1, :], bd_stage[0:E, :], bdR[0:E, 0, :].bitcast(F32),
                               ALU.subtract).then_inc(w_low, 1)

        @block.scalar
        def _(act):
            for n, w in enumerate((wU, wG, wD)):
                act.wait_ge(w_in[n], ONE + 16)
                act.activation(w[:, 0, :], w_stage[:, :], ACT.Copy).then_inc(w_high, 1)
            act.wait_ge(w_in[4], ONE + 32)
            act.activation(bdR[:, 0, :], bd_stage[:, :], ACT.Copy).then_inc(w_high, 1)
            act.wait_ge(w_in[3], ONE + 16)
            act.activation(selR[:, :], w_stage[:, :], ACT.Copy).then_inc(w_high, 1)
            act.activation(onesR[:, :], cst[:, C_ONES:C_ONES + 2], ACT.Copy).then_inc(w_high, 1)
            act.wait_ge(lim_ready, ONE + 2)
            act.activation(lim2[0:E, :], lim[:, :], ACT.Copy).then_inc(lim_moved, 1)
            act.activation(lim2[E:P, :], lim[:, :], ACT.Copy).then_inc(lim_moved, 1)

        @block.tensor
        def _(pe):
            ones = cst[0:E, C_ONES:C_ONES + E]
            for n in range(len(LEVEL_BITS)):
                pe.wait_ge(level_counted, ONE + n + 1)
                pe.matmul(psS[:, :], cst[:, C_ONES:C_ONES + P], lcnt[:, :], start=True, stop=True).then_inc(level_ps, 1)
            for n in range(1 + ROUNDS):
                pe.wait_ge(limits_counted, ONE + 2 * n + 2)
                pe.matmul(psK[:, :], cst[:, C_PAIR:C_PAIR + P], hcnt[n][:, :],
                          start=True, stop=True).then_inc(limits_ps, 1)
                if n == 0:
                    pe.wait_ge(groups_ready, ONE + 1)
                    pe.matmul(psQ[:, :], cst[0:E, C_ONES:C_ONES + P], whole[0:E, 1:3],
                              start=True, stop=True).then_inc(groups_ps, 1)
            for n in range(6):
                pe.wait_ge(missed_ready, ONE + n + 1)
                mm = pe.matmul(psS[0:1, :], cst[:, C_ONES:C_ONES + 1], missed[:, n:n + 1], start=n == 0, stop=n == 5)
            mm.then_inc(missed_ps, 1)
            for b in range(31):
                pe.wait_ge(cnt_ready, ONE + b + 1)
                pe.matmul(psC[:, :], ones, cnt[:, :], start=True, stop=True).then_inc(cnt_ps, 1)
            pe.wait_ge(tie_in, ONE + 2)
            pe.matmul(psC[:, :], ones, cnt[:, :], start=True, stop=True).then_inc(tie_ps, 1)
            pe.matmul(psA[:, :], ones, eqg[:, :], start=True, stop=True).then_inc(tie_ps, 1)
            pe.matmul(psB[:, :], cst[0:E, C_TRI:C_TRI + E], eqg[:, :], start=True, stop=True).then_inc(tie_ps, 1)
            pe.wait_ge(reach_ready, ONE + 2)
            pe.matmul(psX[:, :], cst[:, C_ONES:C_ONES + 1], reach[:, 0:1], start=True, stop=False)
            pe.matmul(psX[:, :], cst[:, C_ONES:C_ONES + 1], reach[:, 1:2], start=False, stop=True).then_inc(reach_ps, 1)

        @block.vector
        def _(dve):
            S0, S1 = bufs
            done = Tally()
            dve.memset(level[:, :], LEVEL | 1 << LEVEL_BITS[0]).then_inc(level_ready, 1)
            for n, b in enumerate(LEVEL_BITS):
                dve.wait_ge(level_ready, ONE + n + 1)
                if n:
                    dve.wait_ge(level_ps, ONE + n)
                dve.tensor_scalar(bufs[n % 2][:, 0:SAMPLE], score[:, 0:SAMPLE], level[:, :].bitcast(F32), 0.0,
                                  ALU.is_ge, ALU.add, accum_out=lcnt[:, :]).then_inc(level_counted, 1)
                dve.wait_ge(level_ps, ONE + n + 1)
                dve.tensor_scalar(ldec[:, :], psS[:, :], float(BUDGET * GROUP * SAMPLE // HALF), float(1 << b),
                                  ALU.is_lt, ALU.mult).then_inc(window, done.one())
                dve.wait_ge(window, ONE + done.total)
                dve.scalar_tensor_tensor(level[:, :], ldec[:, :], (1 << b) >> 1, level[:, :], ALU.bitwise_or,
                                         ALU.bitwise_xor).then_inc(level_ready, 1)
            dve.wait_ge(level_ready, ONE + len(LEVEL_BITS) + 1)
            lev = level[:, :].bitcast(F32)
            dve.tensor_scalar(limit[1][:, 0:1], lev, 1.0 + SPREAD, None, ALU.mult).then_inc(window, done.one())
            dve.tensor_scalar(limit[1][:, 1:2], lev, 1.0 - SPREAD, None, ALU.mult).then_inc(window, done.one())
            dve.tensor_scalar(limit[0][:, 1:2], lev, 1.0 + SPREAD, None, ALU.mult).then_inc(window, done.one())
            dve.tensor_scalar(limit[0][:, 0:1], lev, 1.0 - SPREAD, None, ALU.mult).then_inc(window, done.one())
            for r in range(1 + ROUNDS):
                here, ago, then = limit[r + 1], limit[r], ranks[r]
                dve.wait_ge(window, ONE + done.total)
                for c in range(2):
                    dve.tensor_scalar(bufs[c][:, :], score[:, :], here[:, c:c + 1], 0.0, ALU.is_ge, ALU.add,
                                      accum_out=hcnt[r][:, c:c + 1]).then_inc(limits_counted, 1)
                dve.wait_ge(limits_ps, ONE + r + 1)
                dve.tensor_copy(ranks[r + 1][:, :], psK[:, :]).then_inc(window, done.one())
                if r == 0:
                    dve.tensor_copy(then[:, 0:1], psK[:, 1:2]).then_inc(window, done.one())
                    dve.tensor_copy(then[:, 1:2], psK[:, 0:1]).then_inc(window, done.one())
                    dve.tensor_scalar(whole[:, 0:2], psK[:, :], 1.0 / GROUP, -63.0 / 128, ALU.mult,
                                      ALU.add).then_inc(window, done.one())
                    dve.tensor_scalar(whole[:, 2:4], psK[:, :], 1.0 / GROUP, 63.0 / 128, ALU.mult,
                                      ALU.add).then_inc(window, done.one())
                    dve.wait_ge(window, ONE + done.total)
                    dve.tensor_scalar(whole[:, :], whole[:, :], ROUND, None, ALU.add).then_inc(window, done.one())
                    dve.wait_ge(window, ONE + done.total)
                    dve.tensor_scalar(whole[:, :], whole[:, :], -ROUND, None, ALU.add).then_inc(groups_ready, 1)
                    dve.wait_ge(groups_ready, ONE + 1)
                    dve.tensor_scalar(must[:, 0:1], whole[:, 0:1], float(GROUP), -1.0, ALU.mult,
                                      ALU.add).then_inc(window, done.one())
                    dve.tensor_scalar(must[:, 1:2], whole[:, 3:4], float(GROUP), None,
                                      ALU.mult).then_inc(window, done.one())
                    dve.tensor_scalar(goal[:, 0:1], whole[:, 0:1], float(GROUP), -SLACK, ALU.mult,
                                      ALU.add).then_inc(window, done.one())
                    dve.tensor_scalar(goal[:, 1:2], whole[:, 3:4], float(GROUP), SLACK, ALU.mult,
                                      ALU.add).then_inc(window, done.one())
                    dve.tensor_scalar(empty[:, :], whole[:, 0:1], 0.0, 2.0, ALU.is_equal,
                                      ALU.mult).then_inc(window, done.one())
                    dve.wait_ge(window, ONE + done.total)
                    dve.tensor_scalar(must[:, 0:1], must[:, 0:1], 0.0, None, ALU.max).then_inc(window, done.one())
                    dve.tensor_scalar(goal[:, 0:1], goal[:, 0:1], 0.0, None, ALU.max).then_inc(window, done.one())
                if r < ROUNDS:
                    dve.wait_ge(window, ONE + done.total)
                    dve.tensor_tensor(den[:, :], then[:, :], ranks[r + 1][:, :],
                                      ALU.subtract).then_inc(window, done.one())
                    dve.tensor_tensor(num[:, :], ranks[r + 1][:, :], goal[:, :],
                                      ALU.subtract).then_inc(window, done.one())
                    dve.tensor_tensor(move[:, :], here[:, :], ago[:, :], ALU.subtract).then_inc(window, done.one())
                    dve.tensor_scalar(cap[:, :], here[:, :], 0.2, None, ALU.mult).then_inc(window, done.one())
                    dve.wait_ge(window, ONE + done.total)
                    dve.scalar_tensor_tensor(den[:, :], den[:, :], 0.0, den[:, :], ALU.is_equal,
                                             ALU.add).then_inc(window, done.one())
                    dve.tensor_tensor(move[:, :], move[:, :], num[:, :], ALU.mult).then_inc(window, done.one())
                    dve.wait_ge(window, ONE + done.total)
                    dve.reciprocal(den[:, :], den[:, :]).then_inc(window, done.one())
                    dve.wait_ge(window, ONE + done.total)
                    dve.tensor_tensor(move[:, :], move[:, :], den[:, :], ALU.mult).then_inc(window, done.one())
                    dve.wait_ge(window, ONE + done.total)
                    dve.tensor_tensor(move[:, :], move[:, :], cap[:, :], ALU.min).then_inc(window, done.one())
                    dve.wait_ge(window, ONE + done.total)
                    dve.scalar_tensor_tensor(move[:, :], cap[:, :], -1.0, move[:, :], ALU.mult,
                                             ALU.max).then_inc(window, done.one())
                    dve.wait_ge(window, ONE + done.total)
                    dve.tensor_tensor(limit[r + 2][:, :], here[:, :], move[:, :], ALU.add).then_inc(window, done.one())
                if r == ROUNDS - 1:
                    dve.wait_ge(window, ONE + done.total)
                    dve.tensor_tensor(limit[r + 2][:, 0:1], limit[r + 2][:, 0:1], empty[:, :],
                                      ALU.add).then_inc(window, done.one())
            top, bottom = limit[1 + ROUNDS][:, 0:1], limit[1 + ROUNDS][:, 1:2]
            reached = ranks[1 + ROUNDS]
            dve.scalar_tensor_tensor(S0[:, :], score[:, :], top, score[:, :], ALU.is_lt,
                                     ALU.mult).then_inc(window, done.one())
            dve.tensor_scalar(first[:, :], psK[:, 0:1], 1.0 / GROUP, -63.0 / 128, ALU.mult,
                              ALU.add).then_inc(window, done.one())
            dve.wait_ge(window, ONE + done.total)
            for c in range(HALF // CHUNK):
                dve.max(runs[0][:, 8 * c:8 * c + 8], S0[:, c * CHUNK:(c + 1) * CHUNK]).then_inc(gathered, 1)
            dve.tensor_scalar(first[:, :], first[:, :], ROUND, None, ALU.add).then_inc(window, done.one())
            dve.memset(padrow[:, :], 0.0).then_inc(window, done.one())
            dve.wait_ge(window, ONE + done.total)
            dve.tensor_scalar(first[:, :], first[:, :], -ROUND, None, ALU.add).then_inc(window, done.one())
            dve.wait_ge(window, ONE + done.total)
            dve.scalar_tensor_tensor(pads[:, :], first[:, :], -float(GROUP), reached[:, 0:1], ALU.mult,
                                     ALU.add).then_inc(window, done.one())
            dve.wait_ge(window, ONE + done.total)
            dve.tensor_scalar(padrow[0:E, 0:GROUP], cst[0:E, C_IOTA:C_IOTA + GROUP], pads[0:E, :], ABOVE, ALU.is_lt,
                              ALU.mult).then_inc(window, done.one())
            dve.wait_ge(groups_ps, ONE + 1)
            dve.tensor_scalar(missed[:, 0:1], psQ[:, 1:2], float(BUDGET), None, ALU.is_gt).then_inc(missed_ready, 1)
            dve.tensor_scalar(missed[:, 1:2], psQ[:, 0:1], float(BUDGET), None, ALU.is_lt).then_inc(missed_ready, 1)
            dve.tensor_tensor(missed[:, 2:3], reached[:, 0:1], must[:, 0:1], ALU.is_gt).then_inc(missed_ready, 1)
            dve.tensor_tensor(missed[:, 3:4], reached[:, 1:2], must[:, 1:2], ALU.is_lt).then_inc(missed_ready, 1)
            dve.wait_ge(gathered, ONE + HALF // CHUNK)
            dve.tensor_scalar(S1[:, 0:HALF // CHUNK], runs[0][:, 7::8], bottom, 0.0, ALU.is_ge, ALU.add,
                              accum_out=missed[:, 4:5]).then_inc(missed_ready, 1)
            a, b = runs
            for step in merge_steps(8, RUN):
                sort_step(dve, a[:, :], b[:, :], step, window, done)
                a, b = b, a
            width = FOUND
            while width > RUN:
                w = a[:, 0:width].rearrange("p (n k) -> p n k", k=2 * RUN)
                width //= 2
                dve.wait_ge(window, ONE + done.total)
                dve.tensor_tensor(b[:, 0:width].rearrange("p (n k) -> p n k", k=RUN), w[:, :, 0:RUN],
                                  w[:, :, 2 * RUN - 1:RUN - 1:-1], ALU.max).then_inc(window, done.one())
                a, b = b, a
                for step in halving_steps(RUN, 1):
                    sort_step(dve, a[:, 0:width], b[:, 0:width], step, window, done)
                    a, b = b, a
            dve.wait_ge(window, ONE + done.total)
            dve.tensor_tensor(b[:, 0:RUN], a[:, 0:RUN], padrow[:, ::-1], ALU.max).then_inc(window, done.one())
            a, b = b, a
            for step in halving_steps(RUN, 1):
                sort_step(dve, a[:, 0:RUN], b[:, 0:RUN], step, window, done)
                a, b = b, a
            dve.wait_ge(window, ONE + done.total)
            dve.tensor_tensor(missed[:, 5:6], a[:, RUN - 1:RUN], bottom, ALU.is_ge).then_inc(missed_ready, 1)
            dve.tensor_copy(pair[0][:, 0:RUN], a[0:E, 0:RUN]).then_inc(window, done.one())
            dve.tensor_copy(pair[0][:, RUN:2 * RUN], a[E:P, 0:RUN]).then_inc(window, done.one())
            a, b = pair
            for step in [(2 * RUN, 0)] + halving_steps(RUN, GROUP):
                sort_step(dve, a[:, :], b[:, :], step, window, done)
                a, b = b, a
            dve.wait_ge(window, ONE + done.total)
            g = a[:, :].rearrange("p (g r) -> p g r", r=GROUP)
            dve.tensor_reduce(wsum[:, :], g, AX_X, ALU.add).then_inc(window, done.one())
            dve.tensor_reduce(wmin[:, :], g, AX_X, ALU.min).then_inc(window, done.one())
            dve.tensor_scalar(rel[:, :], cst[0:E, C_IOTA:C_IOTA + NG], first[0:E, :], None,
                              ALU.subtract).then_inc(window, done.one())
            dve.wait_ge(window, ONE + done.total)
            dve.tensor_scalar(G[:, :], rel[:, :], 0.0, ABOVE, ALU.is_lt, ALU.mult).then_inc(window, done.one())
            dve.tensor_scalar(M[:, :], rel[:, :], 0.0, ABOVE, ALU.is_lt, ALU.mult).then_inc(window, done.one())
            for j in range(WG):
                dve.wait_ge(window, ONE + done.total)
                dve.tensor_scalar(at[0][:, :], rel[:, :], float(j), wsum[:, j:j + 1], ALU.is_equal,
                                  ALU.mult).then_inc(window, done.one())
                dve.tensor_scalar(at[1][:, :], rel[:, :], float(j), wmin[:, j:j + 1], ALU.is_equal,
                                  ALU.mult).then_inc(window, done.one())
                dve.wait_ge(window, ONE + done.total)
                dve.tensor_tensor(G[:, :], G[:, :], at[0][:, :], ALU.add).then_inc(window, done.one())
                dve.tensor_tensor(M[:, :], M[:, :], at[1][:, :], ALU.add).then_inc(window, done.one())
            dve.wait_ge(missed_ps, ONE + 1)
            dve.tensor_copy(miss_all[:, :], psS[0:1, :]).then_inc(window, done.one())
            dve.wait_ge(window, ONE + done.total)
            useless = dve.value_load(miss_all[:, :], min_val=0, max_val=P * HALF)
            with dve.If(useless != 0):
                full = Tally()
                src, dst = score, S0
                for step in merge_steps(1, HALF):
                    sort_step(dve, src[:, :], dst[:, :], step, sorted_, full)
                    src, dst = dst, S1 if dst is S0 else S0
                dve.wait_ge(sorted_, ONE + full.total)
                dve.tensor_copy(dst[E:P, :], src[0:E, :]).then_inc(sorted_, full.one())
                dve.tensor_copy(dst[0:E, :], src[E:P, :]).then_inc(sorted_, full.one())
                dve.wait_ge(sorted_, ONE + full.total)
                dve.tensor_tensor(src[0:E, :], src[0:E, :], dst[0:E, ::-1], ALU.max).then_inc(sorted_, full.one())
                dve.tensor_tensor(src[E:P, :], src[E:P, :], dst[E:P, ::-1], ALU.min).then_inc(sorted_, full.one())
                for step in halving_steps(HALF, GROUP):
                    sort_step(dve, src[:, :], dst[:, :], step, sorted_, full)
                    src, dst = dst, src
                dve.wait_ge(sorted_, ONE + full.total)
                g = src[:, :].rearrange("p (g r) -> p g r", r=GROUP)
                dve.tensor_reduce(gsum[:, :], g, AX_X, ALU.add).then_inc(sorted_, full.one())
                dve.tensor_reduce(gmin[:, :], g, AX_X, ALU.min).then_inc(sorted_, full.one())
                dve.wait_ge(sorted_, ONE + full.total)
                for half in range(2):
                    dve.tensor_copy(G[:, half * NG // 2:(half + 1) * NG // 2],
                                    gsum[half * E:(half + 1) * E, :]).then_inc(sorted_, full.one())
                    dve.tensor_copy(M[:, half * NG // 2:(half + 1) * NG // 2],
                                    gmin[half * E:(half + 1) * E, :]).then_inc(sorted_, full.one())
                dve.wait_ge(sorted_, ONE + full.total)
            dve.memset(cand[:, :], 1 << 30).then_inc(cand_ready, 1)
            for n, b in enumerate(range(30, -1, -1)):
                dve.wait_ge(cand_ready, ONE + n + 1)
                if n:
                    dve.wait_ge(cnt_ps, ONE + n)
                dve.tensor_scalar(junk[:, :], G[:, :], cand[:, :].bitcast(F32), 0.0, ALU.is_ge, ALU.add,
                                  accum_out=cnt[:, :]).then_inc(cnt_ready, 1)
                dve.wait_ge(cnt_ps, ONE + n + 1)
                dve.tensor_scalar(dec[:, :], psC[:, :], float(BUDGET), float(1 << b), ALU.is_lt,
                                  ALU.mult).then_inc(dec_ready, 1)
                dve.wait_ge(dec_ready, ONE + n + 1)
                dve.scalar_tensor_tensor(cand[:, :], dec[:, :], (1 << b) >> 1, cand[:, :], ALU.bitwise_or,
                                         ALU.bitwise_xor).then_inc(cand_ready, 1)
            dve.wait_ge(cand_ready, ONE + 32)
            lam = cand[:, :].bitcast(F32)
            dve.tensor_scalar(gt[:, :], G[:, :], lam, 0.0, ALU.is_gt, ALU.add,
                              accum_out=cnt[:, :]).then_inc(tie_in, 1)
            dve.tensor_scalar(eqg[:, :], G[:, :], lam, None, ALU.is_equal).then_inc(tie_in, 1)
            dve.wait_ge(tie_ps, ONE + 3)
            dve.tensor_scalar(left[:, :], psC[:, :], -1.0, float(BUDGET), ALU.mult, ALU.add).then_inc(chain, 1)
            dve.tensor_copy(tot[:, :], psA[:, :]).then_inc(chain, 1)
            dve.wait_ge(chain, ONE + 2)
            dve.tensor_tensor_scan(cum[:, :], tot[:, :], tot[:, :], 0.0, ALU.add, ALU.bypass).then_inc(chain, 1)
            dve.wait_ge(chain, ONE + 3)
            dve.tensor_tensor(pos[:, :], cum[:, :], tot[:, :], ALU.subtract).then_inc(chain, 1)
            dve.wait_ge(chain, ONE + 4)
            dve.tensor_tensor(cum[:, :], psB[:, :], pos[:, :], ALU.add).then_inc(chain, 1)
            dve.wait_ge(chain, ONE + 5)
            dve.scalar_tensor_tensor(take[:, :], cum[:, :], left[:, :], eqg[:, :], ALU.is_lt,
                                     ALU.mult).then_inc(chain, 1)
            dve.wait_ge(chain, ONE + 6)
            dve.tensor_tensor(kept[:, :], take[:, :], gt[:, :], ALU.add).then_inc(chain, 1)
            dve.wait_ge(chain, ONE + 7)
            dve.tensor_scalar(big[:, :], kept[:, :], -4.0, 4.0, ALU.mult, ALU.add).then_inc(chain, 1)
            dve.tensor_reduce(cnt[:, :], kept[:, :], AX_X, ALU.add).then_inc(chain, 1)
            dve.wait_ge(chain, ONE + 9)
            dve.tensor_tensor(mins[:, :], big[:, :], M[:, :], ALU.add).then_inc(chain, 1)
            dve.tensor_scalar(lim[:, 1:2], cnt[:, :], float(GROUP), None, ALU.mult).then_inc(lim_ready, 1)
            dve.wait_ge(chain, ONE + 10)
            dve.tensor_reduce(lim[:, 0:1], mins[:, :], AX_X, ALU.min).then_inc(lim_ready, 1)
            dve.wait_ge(lim_moved, ONE + 2)
            thr = lim2[:, 0:1]
            dve.tensor_scalar(S0[:, :], score[:, :], thr, 0.0, ALU.is_ge, ALU.add,
                              accum_out=reach[:, 0:1]).then_inc(reach_ready, 1)
            dve.tensor_scalar(reach[:, 1:2], lim2[:, 1:2], -0.5, None, ALU.mult).then_inc(reach_ready, 1)
            dve.wait_ge(reach_ps, ONE + 1)
            dve.tensor_copy(excess[:, :], psX[:, :]).then_inc(chain, 1)
            dve.wait_ge(chain, ONE + 11)
            surplus = dve.value_load(excess[:, :], min_val=0, max_val=2 * E * HALF)
            with dve.If(surplus != 0):
                dve.tensor_scalar(S0[:, :], score[:, :], thr, 0.0, ALU.is_equal, ALU.add,
                                  accum_out=same[:, :]).then_inc(tied, 1)
                dve.tensor_scalar(S1[:, :], score[:, :], thr, 0.0, ALU.is_gt, ALU.add,
                                  accum_out=above[:, :]).then_inc(tied, 1)
                dve.memset(before[0:E, :], 0.0).then_inc(tied, 1)
                dve.wait_ge(tied, ONE + 3)
                dve.tensor_copy(before[E:P, :], same[0:E, :]).then_inc(tied, 1)
                dve.tensor_copy(other[E:P, :], above[0:E, :]).then_inc(tied, 1)
                dve.tensor_copy(other[0:E, :], above[E:P, :]).then_inc(tied, 1)
                dve.tensor_tensor(room[:, :], lim2[:, 1:2], above[:, :], ALU.subtract).then_inc(tied, 1)
                dve.wait_ge(tied, ONE + 7)
                dve.tensor_tensor(room[:, :], room[:, :], other[:, :], ALU.subtract).then_inc(tied, 1)
                dve.tensor_tensor_scan(S1[:, :], S0[:, :], S0[:, :], before[:, :], ALU.add,
                                       ALU.bypass).then_inc(tied, 1)
                dve.wait_ge(tied, ONE + 9)
                dve.scalar_tensor_tensor(S1[:, :], S1[:, :], room[:, :], S0[:, :], ALU.is_gt,
                                         ALU.mult).then_inc(tied, 1)
                dve.wait_ge(tied, ONE + 10)
                dve.tensor_scalar(S0[:, :], S1[:, :], -1.0, 1.0, ALU.mult, ALU.add).then_inc(tied, 1)
                dve.wait_ge(tied, ONE + 11)
                dve.tensor_tensor(score[:, :], score[:, :], S0[:, :], ALU.mult).then_inc(tied, 1)
                dve.wait_ge(tied, ONE + 12)
            dve.scalar_tensor_tensor(score[:, :], score[:, :], thr, score[:, :], ALU.is_ge, ALU.mult)


def experts_phase(nc, out, xsave, par, cst, score, xH, xL, wU, wG, wD, selR, bdR, onesR):
    sems = []
    with ExitStack() as ctx:
        def sb(name, shape, dt=F32, side="left"):
            return ctx.enter_context(nc.sbuf_tensor(name, shape, dt, side=side))

        def sb2(name, shape, dt=F32):
            return [sb(f"{name}{u}", shape, dt) for u in range(2)]

        def ps2(name, shape):
            return [ctx.enter_context(nc.psum_tensor(f"{name}{u}", shape, F32)) for u in range(2)]

        def sem(name):
            sems.append(ctx.enter_context(nc.semaphore(name)))
            return sems[-1]

        def sem2(name):
            return [sem(f"{name}{u}") for u in range(2)]

        raw = sb2("raw", [P, SEQ])
        fs = sb2("fs", [P, SEQ], F32R)
        xr = [sb(f"xr{u}", [P, TT, P], side="right") for u in range(2)]
        act_u = sb2("act_u", [P, SEQ])
        gated = sb2("gated", [P, SEQ])
        hid = sb2("hid", [P, SEQ])
        hidH = [sb(f"hidH{q}", [P, SEQ], F32R) for q in range(4)]
        hidL = [sb(f"hidL{q}", [P, SEQ], F32R) for q in range(4)]
        oT = [sb(f"oT{u}", [P, SEQ], side="right") for u in range(2)]
        den = sb2("e_den", [P, TT])
        rden = sb2("e_rden", [P, TT])
        psF = ps2("psF", [P, SEQ])
        psU = ps2("psU", [P, SEQ])
        psG = ps2("psG", [P, SEQ])
        psO = ctx.enter_context(nc.psum_tensor("psO", [P, SEQ], F32))
        psT = ctx.enter_context(nc.psum_tensor("psT_e", [P, SEQ], F32))

        fs_high = sem2("fs_high")
        fs_ready = sem2("fs_ready")
        raw_in = [ctx.enter_context(nc.semaphore(f"raw_in{u}")) for u in range(2)]
        xr_in = [ctx.enter_context(nc.semaphore(f"xr_in{u}")) for u in range(2)]
        up_ps = sem2("up_ps")
        gate_ps = sem2("gate_ps")
        silu_ready = sem2("silu_ready")
        gated_ready = sem2("gated_ready")
        hid_ready = sem2("hid_ready")
        hidH_ready = [sem(f"hidH_ready{q}") for q in range(4)]
        hidL_ready = [sem(f"hidL_ready{q}") for q in range(4)]
        score_ps = sem2("score_ps")
        down_done = [sem(f"down_done{q}") for q in range(4)]
        den_ps = sem2("den_ps")
        den_done = sem2("e_den_done")
        rden_done = sem2("e_rden_done")
        oT_ready = sem2("oT_ready")
        oTT_ps = sem2("oTT_ps")
        y_ready = sem2("e_y_ready")
        y_out = sem2("y_out")

        out_t = out.rearrange("b (j p) d -> b p j d", p=P)
        QC = 2 * CH // 4
        LAG = 4
        TURN = LAG + 1
        SUMS = TURN + 3
        start_semaphores(nc, sems, raw_in + xr_in)
        block = ctx.enter_context(nc.Block())

        @block.sync
        def _(sp):
            with sp.Fori(0, HB) as i:
                for h in range(2):
                    sp.wait_ge(y_ready[h], ONE + TT * i + TT)
                    sp.dma_start(out_t[bass.ds(i + h * HB, 1)].rearrange("b p j d -> (b p) j d"),
                                 xr[h][:, :, :]).then_inc(y_out[h], 16)
            for h in range(2):
                sp.wait_ge(y_out[h], ONE + 16 * HB)

        @block.gpsimd
        def _(pool):
            with pool.Fori(0, HB) as i:
                for h in range(2):
                    pool.wait_ge(y_out[h], ONE + 16 * i)
                    for part in (0, E):
                        pool.dma_start(raw[h][part:part + E, :],
                                       score[h * E:(h + 1) * E, bass.ds(i * SEQ, SEQ)]).then_inc(raw_in[h], 16)
                    pool.dma_start(xr[h][:, :, :], xsave[:, bass.ds((i + h * HB) * TT, TT), :]).then_inc(xr_in[h], 16)
                    pool.wait_ge(raw_in[h], 32 * i + 32)
                    pool.tensor_tensor(fs[h][:, :], raw[h][:, :], cst[:, C_ONES:C_ONES + 1].broadcast_to([P, SEQ]),
                                       ALU.mult).then_inc(fs_high[h], 1)
                    pool.wait_ge(fs_high[h], ONE + i + 1)
                    pool.tensor_tensor(fs[h][E:P, :], raw[h][E:P, :], fs[h][E:P, :].bitcast(F32),
                                       ALU.subtract).then_inc(fs_ready[h], 1)
                    pool.wait_ge(fs_ready[h], ONE + i + 1)

        def run_pairs(eng, step):
            for g in range(2 * CH):
                step(0, g, True)
            with eng.Fori(1, HB) as i:
                for g in range(2 * CH):
                    step(i, g, False)

        def back(i, g, k, first=False):
            if g >= k:
                return i, g - k
            return None if first else (i - 1, 2 * CH + g - k)

        def batch_before(i, h, first):
            if h:
                return i, 0
            return None if first else (i - 1, 1)

        @block.scalar
        def _(act):
            def silu(i, g):
                p, n, c = g % 2, i * CH + g // 2, g % CH
                act.wait_ge(up_ps[p], ONE + n + 1)
                act.wait_ge(gated_ready[p], ONE + n)
                act.activation(act_u[p][:, :], psU[p][:, :], ACT.Silu,
                               bias=par[:, V_BUP + c:V_BUP + c + 1]).then_inc(silu_ready[p], 1)

            def high_part(i, g):
                p, n, q, m = g % 2, i * CH + g // 2, g % 4, i * QC + g // 4
                act.wait_ge(hid_ready[p], ONE + n + 1)
                act.wait_ge(down_done[q], ONE + m)
                act.activation(hidH[q][:, :], hid[p][:, :], ACT.Copy).then_inc(hidH_ready[q], 1)

            def store_sum(i, h):
                act.wait_ge(down_done[3], ONE + i * QC + (h + 1) * QC // 2)
                act.wait_ge(oTT_ps[h], ONE + i)
                act.activation(oT[h][:, :], psO[:, :], ACT.Copy).then_inc(oT_ready[h], 1)

            def step(i, g, first):
                h, c = g // CH, g % CH
                before = batch_before(i, h, first)
                if c == LAG and before:
                    store_sum(*before)
                silu(i, g)
                if back(i, g, 2, first):
                    high_part(*back(i, g, 2))

            run_pairs(act, step)
            for g in range(2 * CH - 2, 2 * CH):
                high_part(HB - 1, g)
            store_sum(HB - 1, 1)

        @block.tensor
        def _(pe):
            def products(i, g):
                h, c = g // CH, g % CH
                p, n = g % 2, i * CH + g // 2
                tok = bass.ds((i + h * HB) * SEQ, SEQ)
                lo, hi = c * P, (c + 1) * P
                if c == 0:
                    pe.wait_ge(fs_ready[h], ONE + i + 1)
                for w, ps, used, done in ((wU, psU, silu_ready, up_ps), (wG, psG, gated_ready, gate_ps)):
                    pe.wait_ge(used[p], ONE + n)
                    pe.matmul(ps[p][:, :], w[:, 0, lo:hi], xL[:, tok], start=True, stop=False)
                    pe.matmul(ps[p][:, :], w[:, 0, lo:hi], xH[:, tok], start=False, stop=False)
                    pe.matmul(ps[p][:, :], w[:, 1, lo:hi], xH[:, tok], start=False, stop=True).then_inc(done[p], 1)
                pe.wait_ge(hid_ready[p], ONE + n)
                pe.matmul(psF[p][:, :], selR[:, lo:hi], fs[h][:, :], start=True, stop=True).then_inc(score_ps[p], 1)

            def down(i, g):
                q, m, c = g % 4, i * QC + g // 4, g % CH
                pe.wait_ge(hidH_ready[q], ONE + m + 1)
                pe.wait_ge(hidL_ready[q], ONE + m + 1)
                pe.matmul(psO[:, :], wD[:, 1, c * P:(c + 1) * P], hidH[q][:, :], start=False, stop=False)
                pe.matmul(psO[:, :], wD[:, 0, c * P:(c + 1) * P], hidH[q][:, :], start=False, stop=False)
                pe.matmul(psO[:, :], wD[:, 0, c * P:(c + 1) * P], hidL[q][:, :], start=False,
                          stop=(c == CH - 1)).then_inc(down_done[q], 1)

            def begin(i, h):
                pe.wait_ge(oT_ready[1 - h], ONE + i + h)
                pe.matmul(psO[:, :], bdR[:, 0, :], fs[h][:, :], start=True, stop=False)
                pe.matmul(psO[:, :], bdR[:, 1, :], fs[h][:, :], start=False, stop=False)

            def score_sums(i, h):
                pe.wait_ge(y_ready[1 - h], ONE + TT * (i + h))
                for j in range(TT):
                    mm = pe.matmul(psT[:, 2 * j:2 * j + 2], fs[h][:, j * P:(j + 1) * P], onesR[:, :],
                                   start=True, stop=True)
                mm.then_inc(den_ps[h], 1)

            def turn(i, h):
                pe.wait_ge(oT_ready[h], ONE + i + 1)
                pe.wait_ge(den_done[h], ONE + i + 1)
                for j in range(TT):
                    mm = pe.transpose(psT[:, j * P:(j + 1) * P], oT[h][:, j * P:(j + 1) * P], cst[:, C_ID:C_ID + P])
                mm.then_inc(oTT_ps[h], 1)

            def step(i, g, first):
                h, c = g // CH, g % CH
                before = batch_before(i, h, first)
                products(i, g)
                if c == LAG:
                    begin(i, h)
                if back(i, g, LAG, first):
                    down(*back(i, g, LAG))
                if c == TURN and before:
                    turn(*before)
                if c == SUMS:
                    score_sums(i, h)

            run_pairs(pe, step)
            for g in range(2 * CH - LAG, 2 * CH):
                down(HB - 1, g)
            turn(HB - 1, 1)

        @block.vector
        def _(dve):
            def gate(i, g):
                p, n, c = g % 2, i * CH + g // 2, g % CH
                dve.wait_ge(gate_ps[p], ONE + n + 1)
                dve.wait_ge(silu_ready[p], ONE + n + 1)
                dve.wait_ge(hid_ready[p], ONE + n)
                dve.scalar_tensor_tensor(gated[p][:, :], psG[p][:, :], par[:, V_BGATE + c:V_BGATE + c + 1],
                                         act_u[p][:, :], ALU.add, ALU.mult).then_inc(gated_ready[p], 1)

            def weigh(i, g, first=False):
                p, n = g % 2, i * CH + g // 2
                dve.wait_ge(gated_ready[p], ONE + n + 1)
                dve.wait_ge(score_ps[p], ONE + n + 1)
                if back(i, g, 2, first):
                    j, k = back(i, g, 2)
                    dve.wait_ge(hidL_ready[k % 4], ONE + j * QC + k // 4 + 1)
                dve.tensor_tensor(hid[p][:, :], gated[p][:, :], psF[p][:, :], ALU.mult).then_inc(hid_ready[p], 1)

            def low_part(i, g):
                p, q, m = g % 2, g % 4, i * QC + g // 4
                dve.wait_ge(hidH_ready[q], ONE + m + 1)
                dve.wait_ge(down_done[q], ONE + m)
                dve.tensor_tensor(hidL[q][:, :], hid[p][:, :], hidH[q][:, :].bitcast(F32),
                                  ALU.subtract).then_inc(hidL_ready[q], 1)

            def invert(i, h):
                dve.wait_ge(den_ps[h], ONE + i + 1)
                dve.wait_ge(rden_done[h], ONE + i)
                dve.tensor_scalar(den[h][:, :], psT[:, 0:2 * TT:2], DEN_EPS, None,
                                  ALU.add).then_inc(den_done[h], 1)
                dve.wait_ge(den_done[h], ONE + i + 1)
                dve.wait_ge(y_ready[h], ONE + TT * i)
                dve.reciprocal(rden[h][:, :], den[h][:, :]).then_inc(rden_done[h], 1)

            def finish(i, h):
                dve.wait_ge(oTT_ps[h], ONE + i + 1)
                dve.wait_ge(rden_done[h], ONE + i + 1)
                dve.wait_ge(xr_in[h], 16 * i + 16)
                for j in range(TT):
                    dve.scalar_tensor_tensor(xr[h][:, j, :], psT[:, j * P:(j + 1) * P], rden[h][:, j:j + 1],
                                             xr[h][:, j, :], ALU.mult, ALU.add).then_inc(y_ready[h], 1)

            def step(i, g, first):
                h, c = g // CH, g % CH
                before = batch_before(i, h, first)
                gate(i, g)
                if back(i, g, 1, first):
                    j, k = back(i, g, 1)
                    weigh(j, k, first)
                if back(i, g, 2, first):
                    low_part(*back(i, g, 2))
                if c == TURN + 1 and before:
                    finish(*before)
                if c == SUMS + 2:
                    invert(i, h)

            run_pairs(dve, step)
            weigh(HB - 1, 2 * CH - 1)
            low_part(HB - 1, 2 * CH - 2)
            low_part(HB - 1, 2 * CH - 1)
            finish(HB - 1, 1)


def build(nc, a, out):
    with ExitStack() as ctx:
        def sb(name, shape, dt=F32):
            return ctx.enter_context(nc.sbuf_tensor(name, shape, dt))

        cst = sb("cst", [P, C_SEL])
        par = sb("par", [P, V_END + 1])
        st = sb("st", [P, NT, 6])
        score = sb("score", [P, HALF])
        xsave = nc.dram_tensor("xsave", [P, NT, P], F32).ap()
        tables_in = ctx.enter_context(nc.semaphore("tables_in"))
        eps_set = ctx.enter_context(nc.semaphore("eps_set"))
        with nc.Block() as block:
            @block.sync
            def _(sp):
                sp.dma_start(cst[:, :], a["cst"][:, 0:C_SEL]).then_inc(tables_in, 16)
                sp.dma_start(par[:, 0:V_END], a["par"]).then_inc(tables_in, 16)
                sp.wait_ge(tables_in, 32)

            @block.gpsimd
            def _(pool):
                pool.memset(par[:, V_END:V_END + 1], LN_EPS).then_inc(eps_set, 1)
                pool.wait_ge(eps_set, 1)

        with nc.sbuf_tensor("xres", [P, NT, P], F32, side="right") as xres:
            attention_phase(nc, a["x"], a["wqT"], a["wkvT"], a["wpT"], a["bp"], cst, par, xres, st)
            xH = sb("xH", [P, TOK], F32R)
            xL = sb("xL", [P, TOK], F32R)
            router_phase(nc, a["wr"], a["br"], cst, par, xres, st, xH, xL, score, xsave)
        wU = sb("wU", [P, 2, E * H], F32R)
        wG = sb("wG", [P, 2, E * H], F32R)
        wD = sb("wD", [P, 2, CH * P], F32R)
        selR = sb("selR", [P, CH * P], F32R)
        bdR = sb("bdR", [P, 2, P], F32R)
        onesR = sb("onesR", [P, 2], F32R)
        with (nc.sbuf_tensor("w_stage", [P, E * H], F32) as w_stage,
              nc.sbuf_tensor("bd_stage", [P, P], F32) as bd_stage):
            routing_phase(nc, a["wupT"], a["wgateT"], a["wdn"], a["bdn"], a["cst"][:, C_SEL:C_END], cst, score,
                                 wU, wG, wD, selR, bdR, onesR, w_stage, bd_stage)
        experts_phase(nc, out, xsave, par, cst, score, xH, xL, wU, wG, wD, selR, bdR, onesR)


def constants():
    import numpy as np
    k, m = np.arange(P)[:, None], np.arange(P)[None, :]
    c = np.zeros((P, C_END), np.float32)
    c[:, C_ID:C_ID + P] = k == m
    c[:, C_BLOCK:C_BLOCK + P] = k // HD == m // HD
    c[:, C_ONES:C_ONES + P] = 1.0
    c[:, C_PAIR:C_PAIR + P] = k % E == m % E
    c[:, C_IOTA:C_IOTA + P] = m
    c[:, C_TRI:C_TRI + E] = k < m[:, :E]
    c[:, C_HEAD:C_HEAD + HEADS] = k // HD == m[:, :HEADS]
    for n in range(CH):
        c[:, C_SEL + n * P:C_SEL + (n + 1) * P] = k % E == n * EPC + m // H
    return c


def kernel(**inputs):
    import numpy as np
    import concourse.bacc as bacc
    from concourse.bass_utils import run_bass_kernel_spmd

    v = {k: np.asarray(x) for k, x in inputs.items()}
    attn = lambda k: v["L0_attn_" + k]
    ffn = lambda k: v["L0_ffn_" + k]
    cols = lambda b: b.reshape(CH, P).T
    arrays = {
        "x": attn("x"),
        "wqT": attn("Wq").T,
        "wkvT": np.concatenate([attn("Wk").T, attn("Wv").T], axis=1),
        "wpT": attn("Wp").T,
        "bp": np.tile(attn("bp"), TT).reshape(1, SEQ),
        "wr": ffn("Wr"),
        "br": ffn("br"),
        "wupT": ffn("Wup").transpose(1, 0, 2).reshape(P, E * H),
        "wgateT": ffn("Wgate").transpose(1, 0, 2).reshape(P, E * H),
        "wdn": ffn("Wdown").reshape(CH, P, P).transpose(1, 0, 2).reshape(P, CH * P),
        "bdn": ffn("bdown"),
        "par": np.concatenate([attn("conv_w"), attn("conv_b").reshape(P, 1),
                               cols(ffn("bup")), cols(ffn("bgate"))], axis=1),
        "cst": constants(),
    }
    arrays = {k: np.ascontiguousarray(x) for k, x in arrays.items()}
    nc = bacc.Bacc("TRN2", target_bir_lowering=False, num_devices=1)
    aps = {k: nc.dram_tensor(k + "_dram", x.shape, F32, kind="ExternalInput").ap() for k, x in arrays.items()}
    out = nc.dram_tensor("out_dram", (BATCH, SEQ, P), F32, kind="ExternalOutput").ap()
    build(nc, aps, out)
    res = run_bass_kernel_spmd(nc, [{k + "_dram": x for k, x in arrays.items()}], core_ids=[0])
    return res.results[0]["out_dram"]
```

```python
from contextlib import ExitStack

import concourse.bass as bass
from concourse import mybir

F32 = mybir.dt.float32
F32R = mybir.dt.float32r
I32 = mybir.dt.int32
ALU = mybir.AluOpType
ACT = mybir.ActivationFunctionType
AX_X = mybir.AxisListType.X

P = 128
BATCH, SEQ = 16, 512
TOK = BATCH * SEQ
TT = SEQ // P
NT = TOK // P
HEADS, HD = 16, 8
E, H = 64, 32
CH = E * H // P
EPC = P // H
GROUP, KEEP = 64, 16
NG = TOK // GROUP
BUDGET = NG * KEEP
HALF = TOK // 2
HB = BATCH // 2
LN_EPS = 1e-5
DEN_EPS = 1e-6

SAMPLE = HALF // 4
LEVELS = (1.0 / E, 1.25 / E)
LEVEL_ROUNDS = 4
SPREAD = 0.025
SLACK = 40.0
ROUNDS = 1
CHUNK = 32
FOUND = HALF // CHUNK * 8
RUN = 256
WG = 2 * RUN // GROUP
ROUND = float(1 << 23)
ABOVE = 1e6

C_ID, C_BLOCK, C_ONES, C_PAIR, C_IOTA, C_TRI, C_HEAD, C_SEL = 0, 128, 256, 384, 512, 640, 704, 720
C_END = C_SEL + CH * P
V_CONV, V_CONVB, V_BUP, V_BGATE = 0, 3, 4, 4 + CH
V_END = 4 + 2 * CH


ONE = 1


def start_semaphores(nc, sems, zeros=()):
    with nc.Block() as block:
        @block.vector
        def _(dve):
            for s in zeros:
                dve.sem_clear(s)

        @block.sync
        def _(sp):
            for s in sems[0::3]:
                sp.sem_clear(s)
                sp.sem_inc(s, ONE)

        @block.scalar
        def _(act):
            for s in sems[1::3]:
                act.sem_clear(s)
                act.sem_inc(s, ONE)

        @block.tensor
        def _(pe):
            for s in sems[2::3]:
                pe.sem_clear(s)
                pe.sem_inc(s, ONE)


def fold_statistics(dve, st, tmp, mean, chain):
    dve.tensor_tensor(tmp[:, 0, :], st[:, :, 1], st[:, :, 4], ALU.add).then_inc(chain, 1)
    dve.tensor_tensor(tmp[:, 1, :], st[:, :, 1], st[:, :, 4], ALU.subtract).then_inc(chain, 1)
    dve.tensor_tensor(tmp[:, 2, :], st[:, :, 2], st[:, :, 5], ALU.add).then_inc(chain, 1)
    dve.wait_ge(chain, ONE + 3)
    dve.tensor_scalar(mean[:, :], tmp[:, 0, :], 0.5, None, ALU.mult).then_inc(chain, 1)
    dve.tensor_tensor(tmp[:, 3, :], tmp[:, 1, :], tmp[:, 1, :], ALU.mult).then_inc(chain, 1)
    dve.wait_ge(chain, ONE + 5)
    dve.scalar_tensor_tensor(tmp[:, 4, :], tmp[:, 3, :], P / 4.0, tmp[:, 2, :], ALU.mult, ALU.add).then_inc(chain, 1)


def run_slots(eng, slot):
    n = BATCH // 2
    slot((0, 0), None, None)
    slot((0, 1), (0, 0), None)
    with eng.Fori(0, n - 1) as i:
        slot((i + 1, 0), (i, 1), (i, 0))
        slot((i + 1, 1), (i + 1, 0), (i, 1))
    slot(None, (n - 1, 1), (n - 1, 0))
    slot(None, None, (n - 1, 1))


def attention_phase(nc, x, wqT, wkvT, wpT, bp, cst, par, xres, st):
    sems = []
    with ExitStack() as ctx:
        def sb(name, shape, dt=F32):
            return ctx.enter_context(nc.sbuf_tensor(name, shape, dt))

        def sb2(name, shape, dt=F32):
            return [sb(f"{name}{u}", shape, dt) for u in range(2)]

        def ps2(name, shape):
            return [ctx.enter_context(nc.psum_tensor(f"{name}{u}", shape, F32)) for u in range(2)]

        def sem(name):
            sems.append(ctx.enter_context(nc.semaphore(name)))
            return sems[-1]

        def sem2(name):
            return [sem(f"{name}{u}") for u in range(2)]

        wq_sb = sb("wq_sb", [P, P])
        wkv_sb = sb("wkv_sb", [P, 2 * P])
        wp_sb = sb("wp_sb", [P, P])
        bp_sb = sb("bp_sb", [E, SEQ])
        bpR = sb("bpR", [E, SEQ], F32R)
        bp_ones = sb("bp_ones", [E, P], F32R)
        rstd = sb("rstd", [P, NT])
        shift = sb("shift", [P, NT])
        std = sb("std", [P, NT])
        tmp = sb("tmp", [P, 5, NT])
        mean = sb("mean", [P, NT])
        x2s = sb2("x2s", [P, TT, P])
        bst = sb2("bst", [P, TT, 6])
        stat = sb2("stat", [P, 2, TT])
        xn = sb2("xn", [P, TT, P])
        xnT = sb2("xnT", [P, SEQ + 2])
        eq = sb2("eq", [P, SEQ])
        rq = sb2("rq", [P, SEQ])
        ek = sb2("ek", [P, TT, P])
        rk = sb2("rk", [P, TT, P])
        qT = sb2("qT", [P, SEQ])
        kk = sb2("kk", [P, TT, P])
        v1 = sb2("v1", [P, TT, P + 1])
        loc0 = sb2("loc0", [P, SEQ])
        loc1 = sb2("loc1", [P, SEQ])
        loc2 = sb2("loc2", [P, SEQ])
        kvs = sb2("kvs", [P, P + HEADS])
        den = sb2("den", [P, TT, HEADS])
        rden = sb2("rden", [P, TT, HEADS])
        att = sb2("att", [P, TT, P])
        yT = sb2("yT", [P, SEQ])
        psT = ps2("psT", [P, SEQ])
        psQ = ps2("psQ", [P, SEQ])
        psKV = ps2("psKV", [P, TT, 2 * P])

        x_in = [sem(f"x_in{k}") for k in range(4)]
        w_in = sem("w_in")
        bn1_done = sem("bn1_done")
        st2_done = sem2("st2_done")
        var_done = sem("var_done")
        x2_kept = sem2("x2_kept")
        std_done = sem("std_done")
        rstd_done = sem("rstd_done")
        pads_done = sem("pads_done")
        bp_clear = sem("bp_clear")
        bp_high = sem("bp_high")
        bp_low = sem("bp_low")
        stat_done = sem2("stat_done")
        xn_ready = sem2("xn_ready")
        xT_ps = sem2("xT_ps")
        xnT_ready = sem2("xnT_ready")
        q_ps = sem2("q_ps")
        kv_ps = sem2("kv_ps")
        q_act = sem2("q_act")
        kv_act = sem2("kv_act")
        loc0_ready = sem2("loc0_ready")
        loc1_ready = sem2("loc1_ready")
        loc2_ready = sem2("loc2_ready")
        q_ready = sem2("q_ready")
        k_ready = sem2("k_ready")
        kvs_ps = sem2("kvs_ps")
        kvs_ready = sem2("kvs_ready")
        at_ps = sem2("at_ps")
        den_done = sem2("den_done")
        rden_done = sem2("rden_done")
        at_ready = sem2("at_ready")
        aT_ps = sem2("aT_ps")
        y_ready = sem2("y_ready")
        o_ps = sem2("o_ps")
        x2_ready = sem2("x2_ready")
        bn2_done = sem2("bn2_done")

        NX = 4
        start_semaphores(nc, sems)
        block = ctx.enter_context(nc.Block())

        @block.sync
        def _(sp):
            xt = x.rearrange("b (j p) d -> p (b j) d", p=P)
            for k in range(NX):
                n = NT // NX
                sp.dma_start(xres[:, k * n:(k + 1) * n, :], xt[:, k * n:(k + 1) * n, :]).then_inc(x_in[k], 16)

        @block.gpsimd
        def _(pool):
            for u in range(2):
                pool.memset(xnT[u][:, 0:1], 0.0).then_inc(pads_done, 1)
                pool.memset(xnT[u][:, SEQ + 1:SEQ + 2], 0.0).then_inc(pads_done, 1)
                pool.memset(v1[u][:, :, P:P + 1], 1.0).then_inc(pads_done, 1)
            pool.memset(bpR[:, :].bitcast(F32), 0.0).then_inc(bp_clear, 1)
            pool.wait_ge(bp_high, ONE + 3)
            pool.tensor_tensor(bpR[32:33, :], bp_sb[32:33, :], bpR[32:33, :].bitcast(F32),
                               ALU.subtract).then_inc(bp_low, 1)
            with pool.Fori(0, BATCH // 2) as i:
                for u in range(2):
                    pool.wait_ge(x2_ready[u], ONE + i + 1)
                    pool.tensor_copy(xres[:, bass.ds((2 * i + u) * TT, TT), :], x2s[u][:, :, :]).then_inc(x2_kept[u], 1)

        @block.scalar
        def _(act):
            for dst, src in ((bp_sb[0:1, :], bp), (bp_sb[32:33, :], bp), (wq_sb[:, :], wqT), (wkv_sb[:, :], wkvT),
                             (wp_sb[:, :], wpT)):
                act.dma_start(dst, src).then_inc(w_in, 16)
            act.activation(bp_ones[:, :], cst[0:E, C_ONES:C_ONES + P], ACT.Copy).then_inc(bp_high, 1)
            act.wait_ge(w_in, ONE + 80)
            act.wait_ge(bp_clear, ONE + 1)
            for r in (0, 32):
                act.activation(bpR[r:r + 1, :], bp_sb[r:r + 1, :], ACT.Copy).then_inc(bp_high, 1)
            act.wait_ge(var_done, ONE + 6)
            act.activation(std[:, :], tmp[:, 4, :], ACT.Sqrt, bias=par[:, V_END:V_END + 1],
                           scale=1.0 / P).then_inc(std_done, 1)
            act.wait_ge(pads_done, ONE + 6)

            def slot(ahead, front, back):
                if front:
                    i, u = front
                    act.wait_ge(xT_ps[u], ONE + i + 1)
                    act.wait_ge(loc2_ready[u], ONE + i)
                    act.activation(xnT[u][:, 1:SEQ + 1], psT[u][:, :], ACT.Copy).then_inc(xnT_ready[u], 1)
                    act.wait_ge(q_ps[u], ONE + i + 1)
                    act.wait_ge(q_ready[u], ONE + i)
                    act.activation(eq[u][:, :], psQ[u][:, :], ACT.Exp).then_inc(q_act[u], 1)
                    act.activation(rq[u][:, :], psQ[u][:, :], ACT.Relu).then_inc(q_act[u], 1)
                    act.wait_ge(kv_ps[u], ONE + i + 1)
                    act.wait_ge(k_ready[u], ONE + i)
                    act.activation(ek[u][:, :, :], psKV[u][:, :, 0:P], ACT.Exp).then_inc(kv_act[u], 1)
                    act.activation(rk[u][:, :, :], psKV[u][:, :, 0:P], ACT.Relu).then_inc(kv_act[u], 1)
                    act.wait_ge(kvs_ps[u], ONE + i)
                    act.activation(v1[u][:, :, 0:P], psKV[u][:, :, P:2 * P], ACT.Copy).then_inc(kv_act[u], 1)
                if ahead:
                    i, u = ahead
                    act.wait_ge(stat_done[u], ONE + 2 * i + 2)
                    act.wait_ge(xT_ps[u], ONE + i)
                    for j in range(TT):
                        act.activation(xn[u][:, j, :], xres[:, bass.ds((2 * i + u) * TT + j, 1), :], ACT.Identity,
                                       bias=stat[u][:, 1, j:j + 1], scale=stat[u][:, 0, j:j + 1]).then_inc(xn_ready[u], 1)
                if front:
                    i, u = front
                    act.wait_ge(xnT_ready[u], ONE + i + 1)
                    act.wait_ge(loc1_ready[u], ONE + i)
                    act.activation(loc0[u][:, :], xnT[u][:, 1:SEQ + 1], ACT.Identity,
                                   bias=par[:, V_CONVB:V_CONVB + 1],
                                   scale=par[:, V_CONV + 1:V_CONV + 2]).then_inc(loc0_ready[u], 1)

            run_slots(act, slot)

        @block.tensor
        def _(pe):
            pe.wait_ge(w_in, ONE + 80)
            pe.wait_ge(bp_low, ONE + 1)

            def turn_rows(i, u):
                pe.wait_ge(xn_ready[u], ONE + TT * i + TT)
                pe.wait_ge(y_ready[u], ONE + i)
                for j in range(TT):
                    mm = pe.transpose(psT[u][:, j * P:(j + 1) * P], xn[u][:, j, :], cst[:, C_ID:C_ID + P])
                mm.then_inc(xT_ps[u], 1)

            def query(i, u):
                pe.wait_ge(xnT_ready[u], ONE + i + 1)
                pe.wait_ge(x2_ready[u], ONE + i)
                pe.matmul(psQ[u][:, :], wq_sb[:, :], xnT[u][:, 1:SEQ + 1],
                          start=True, stop=True).then_inc(q_ps[u], 1)

            def key_value(i, u):
                pe.wait_ge(at_ready[u], ONE + i)
                for j in range(TT):
                    mm = pe.matmul(psKV[u][:, j, :], xnT[u][:, 1 + j * P:1 + (j + 1) * P], wkv_sb[:, :],
                                   start=True, stop=True)
                mm.then_inc(kv_ps[u], 1)

            def states(i, u):
                pe.wait_ge(k_ready[u], ONE + i + 1)
                pe.wait_ge(kv_act[u], ONE + 3 * i + 3)
                for j in range(TT):
                    mm = pe.matmul(psKV[u][:, 0, 0:P + 1], kk[u][:, j, :], v1[u][:, j, :],
                                   start=(j == 0), stop=(j == TT - 1))
                mm.then_inc(kvs_ps[u], 1)

            def attend(i, u):
                pe.wait_ge(kvs_ready[u], ONE + 2 * i + 2)
                pe.wait_ge(q_ready[u], ONE + i + 1)
                for j in range(TT):
                    mm = pe.matmul(psKV[u][:, j, 0:P + HEADS], qT[u][:, j * P:(j + 1) * P], kvs[u][:, :],
                                   start=True, stop=True)
                mm.then_inc(at_ps[u], 1)

            def turn_attention(i, u):
                pe.wait_ge(at_ready[u], ONE + i + 1)
                for j in range(TT):
                    mm = pe.transpose(psT[u][:, j * P:(j + 1) * P], att[u][:, j, :], cst[:, C_ID:C_ID + P])
                mm.then_inc(aT_ps[u], 1)

            def project(i, u):
                pe.wait_ge(y_ready[u], ONE + i + 1)
                for j in range(TT):
                    mm = pe.matmul(psQ[u][:, j * P:(j + 1) * P], yT[u][:, j * P:(j + 1) * P], wp_sb[:, :],
                                   start=False, stop=(j == TT - 1))
                mm.then_inc(o_ps[u], 1)

            def slot(ahead, front, back):
                if front:
                    turn_rows(*front)
                if back:
                    attend(*back)
                    i, u = back
                    pe.wait_ge(q_act[u], ONE + 2 * i + 2)
                    pe.matmul(psQ[u][:, :], bp_ones[:, :], bpR[:, :], start=True, stop=False)
                if front:
                    query(*front)
                    key_value(*front)
                if back:
                    turn_attention(*back)
                    project(*back)
                if front:
                    states(*front)

            run_slots(pe, slot)

        @block.vector
        def _(dve):
            for k in range(NX):
                dve.wait_ge(x_in[k], ONE + 16)
                for t in range(k * NT // NX, (k + 1) * NT // NX):
                    dve.bn_stats(st[:, t, :], xres[:, t, :]).then_inc(bn1_done, 1)
            dve.wait_ge(bn1_done, ONE + NT)
            fold_statistics(dve, st, tmp, mean, var_done)
            dve.wait_ge(std_done, ONE + 1)
            dve.reciprocal(rstd[:, :], std[:, :]).then_inc(rstd_done, 1)
            dve.wait_ge(rstd_done, ONE + 1)
            dve.scalar_tensor_tensor(shift[:, :], mean[:, :], -1.0, rstd[:, :], ALU.mult,
                                     ALU.mult).then_inc(rstd_done, 1)
            dve.wait_ge(rstd_done, ONE + 2)

            def place_statistics(i, u):
                t0 = (2 * i + u) * TT
                dve.wait_ge(xn_ready[u], ONE + TT * i)
                dve.tensor_scalar(stat[u][:, 0, :], rstd[:, bass.ds(t0, TT)], 1.0, None,
                                  ALU.mult).then_inc(stat_done[u], 1)
                dve.tensor_scalar(stat[u][:, 1, :], shift[:, bass.ds(t0, TT)], 1.0, None,
                                  ALU.mult).then_inc(stat_done[u], 1)

            def query_map(i, u):
                dve.wait_ge(q_act[u], ONE + 2 * i + 2)
                dve.wait_ge(at_ps[u], ONE + i)
                dve.scalar_tensor_tensor(qT[u][:, :], eq[u][:, :], 1.0, rq[u][:, :],
                                         ALU.min, ALU.add).then_inc(q_ready[u], 1)

            def key_map(i, u):
                dve.wait_ge(kv_act[u], ONE + 3 * i + 2)
                dve.wait_ge(kvs_ps[u], ONE + i)
                dve.scalar_tensor_tensor(kk[u][:, :, :], ek[u][:, :, :], 1.0, rk[u][:, :, :],
                                         ALU.min, ALU.add).then_inc(k_ready[u], 1)

            def first_tap(i, u):
                dve.wait_ge(loc0_ready[u], ONE + i + 1)
                dve.wait_ge(loc2_ready[u], ONE + i)
                dve.scalar_tensor_tensor(loc1[u][:, :], xnT[u][:, 0:SEQ], par[:, V_CONV:V_CONV + 1],
                                         loc0[u][:, :], ALU.mult, ALU.add).then_inc(loc1_ready[u], 1)

            def last_tap(i, u):
                dve.wait_ge(loc1_ready[u], ONE + i + 1)
                dve.wait_ge(y_ready[u], ONE + i)
                dve.scalar_tensor_tensor(loc2[u][:, :], xnT[u][:, 2:SEQ + 2], par[:, V_CONV + 2:V_CONV + 3],
                                         loc1[u][:, :], ALU.mult, ALU.add).then_inc(loc2_ready[u], 1)

            def mask_states(i, u):
                dve.wait_ge(kvs_ps[u], ONE + i + 1)
                dve.wait_ge(at_ps[u], ONE + i)
                dve.tensor_tensor(kvs[u][:, 0:P], psKV[u][:, 0, 0:P], cst[:, C_BLOCK:C_BLOCK + P],
                                  ALU.mult).then_inc(kvs_ready[u], 1)
                dve.tensor_scalar(kvs[u][:, P:P + HEADS], cst[:, C_HEAD:C_HEAD + HEADS],
                                  psKV[u][:, 0, P:P + 1], None, ALU.mult).then_inc(kvs_ready[u], 1)

            def divide(i, u):
                dve.wait_ge(at_ps[u], ONE + i + 1)
                dve.wait_ge(rden_done[u], ONE + i)
                dve.tensor_scalar(den[u][:, :, :], psKV[u][:, :, P:P + HEADS], 1e-6, None,
                                  ALU.max).then_inc(den_done[u], 1)
                dve.wait_ge(den_done[u], ONE + i + 1)
                dve.wait_ge(at_ready[u], ONE + i)
                dve.reciprocal(rden[u][:, :, :], den[u][:, :, :]).then_inc(rden_done[u], 1)
                dve.wait_ge(rden_done[u], ONE + i + 1)
                dve.wait_ge(aT_ps[u], ONE + i)
                dve.tensor_tensor(att[u][:, :, :].rearrange("p j (h e) -> p j h e", e=HD),
                                  psKV[u][:, :, 0:P].rearrange("p j (h e) -> p j h e", e=HD),
                                  rden[u][:, :, :].unsqueeze(3).broadcast_to([P, TT, HEADS, HD]),
                                  ALU.mult).then_inc(at_ready[u], 1)

            def add_local(i, u):
                dve.wait_ge(aT_ps[u], ONE + i + 1)
                dve.wait_ge(loc2_ready[u], ONE + i + 1)
                dve.wait_ge(o_ps[u], ONE + i)
                dve.tensor_tensor(yT[u][:, :], psT[u][:, :], loc2[u][:, :], ALU.add).then_inc(y_ready[u], 1)

            def add_residual(i, u):
                dve.wait_ge(o_ps[u], ONE + i + 1)
                dve.wait_ge(x2_kept[u], ONE + i)
                dve.tensor_tensor(x2s[u][:, :, :], psQ[u][:, :].rearrange("p (j d) -> p j d", d=P),
                                  xres[:, bass.ds((2 * i + u) * TT, TT), :], ALU.add).then_inc(x2_ready[u], 1)

            def statistics(i, u):
                dve.wait_ge(x2_ready[u], ONE + i + 1)
                dve.wait_ge(st2_done[u], ONE + i)
                for j in range(TT):
                    dve.bn_stats(bst[u][:, j, :], x2s[u][:, j, :]).then_inc(bn2_done[u], 1)
                dve.wait_ge(bn2_done[u], ONE + TT * i + TT)
                dve.tensor_scalar(st[:, bass.ds((2 * i + u) * TT, TT), :], bst[u][:, :, :], 1.0, None,
                                  ALU.mult).then_inc(st2_done[u], 1)

            def slot(ahead, front, back):
                if ahead:
                    place_statistics(*ahead)
                if back:
                    first_tap(*back)
                    divide(*back)
                    last_tap(*back)
                if front:
                    query_map(*front)
                if back:
                    add_local(*back)
                if front:
                    key_map(*front)
                if back:
                    add_residual(*back)
                if front:
                    mask_states(*front)
                if back:
                    statistics(*back)

            run_slots(dve, slot)


def router_phase(nc, wr, br, cst, par, xres, st, xH, xL, score, xsave):
    sems = []
    with ExitStack() as ctx:
        def sb(name, shape, dt=F32):
            return ctx.enter_context(nc.sbuf_tensor(name, shape, dt))

        def sb2(name, shape, dt=F32):
            return [sb(f"{name}{u}", shape, dt) for u in range(2)]

        def ps2(name, shape):
            return [ctx.enter_context(nc.psum_tensor(f"{name}{u}", shape, F32)) for u in range(2)]

        def sem(name):
            sems.append(ctx.enter_context(nc.semaphore(name)))
            return sems[-1]

        def sem2(name):
            return [sem(f"{name}{u}") for u in range(2)]

        wr_sb = sb("wr_sb", [P, E])
        br_sb = sb("br_sb", [P, E])
        tmp = sb("r_tmp", [P, 5, NT])
        mean = sb("r_mean", [P, NT])
        std = sb("r_std", [P, NT])
        rstd = sb("r_rstd", [P, NT])
        stat = sb2("r_stat", [P, 2, TT])
        xn = sb2("r_xn", [P, TT, P])
        xT = sb2("r_xT", [P, SEQ])
        lg = sb2("r_lg", [P, TT, E])
        lc = sb2("r_lc", [P, TT, E])
        mx = sb2("r_mx", [P, TT])
        ex = sb2("r_ex", [P, TT, E])
        sm = sb2("r_sm", [P, TT])
        rs = sb2("r_rs", [P, TT])
        pr = sb2("r_pr", [P, TT, E])
        psT = ps2("r_psT", [P, SEQ])
        psR = ps2("r_psR", [P, TT, E])
        psS = ps2("r_psS", [P, TT // 2, P])

        w_in = sem("r_w_in")
        saved = sem("r_saved")
        var_done = sem("r_var_done")
        std_done = sem("r_std_done")
        rstd_done = sem("r_rstd_done")
        stat_done = sem2("r_stat_done")
        xn_ready = sem2("r_xn_ready")
        xT_ps = sem2("r_xT_ps")
        xT_ready = sem2("r_xT_ready")
        xH_ready = sem2("r_xH_ready")
        xL_ready = sem2("r_xL_ready")
        lg_ps = sem2("r_lg_ps")
        lg_done = sem2("r_lg_done")
        mx_done = sem2("r_mx_done")
        lc_done = sem2("r_lc_done")
        ex_done = sem2("r_ex_done")
        sm_done = sem2("r_sm_done")
        rs_done = sem2("r_rs_done")
        pr_done = sem2("r_pr_done")
        pT_ps = sem2("r_pT_ps")
        sc_done = sem2("r_sc_done")

        start_semaphores(nc, sems)
        block = ctx.enter_context(nc.Block())

        @block.sync
        def _(sp):
            sp.dma_start(wr_sb[:, :], wr).then_inc(w_in, 16)
            sp.dma_start(br_sb[:, :], br.partition_broadcast(P)).then_inc(w_in, 16)
            sp.dma_start(xsave, xres[:, :, :]).then_inc(saved, 16)
            sp.wait_ge(saved, ONE + 16)

        @block.scalar
        def _(act):
            act.wait_ge(var_done, ONE + 6)
            act.activation(std[:, :], tmp[:, 4, :], ACT.Sqrt, bias=par[:, V_END:V_END + 1],
                           scale=1.0 / P).then_inc(std_done, 1)

            def slot(ahead, front, back):
                if back:
                    i, u = back
                    act.wait_ge(lc_done[u], ONE + i + 1)
                    act.wait_ge(pr_done[u], ONE + i)
                    act.activation(ex[u][:, :, :], lc[u][:, :, :], ACT.Exp).then_inc(ex_done[u], 1)
                if ahead:
                    i, u = ahead
                    act.wait_ge(xT_ps[u], ONE + i + 1)
                    act.wait_ge(lg_ps[u], ONE + i)
                    act.wait_ge(xL_ready[u], ONE + i)
                    act.activation(xT[u][:, :], psT[u][:, :], ACT.Copy).then_inc(xT_ready[u], 1)
                    act.activation(xH[:, bass.ds((i + u * HB) * SEQ, SEQ)], psT[u][:, :],
                                   ACT.Copy).then_inc(xH_ready[u], 1)
                if back:
                    i, u = back
                    act.wait_ge(pT_ps[u], ONE + i + 1)
                    dst = score[u * E:(u + 1) * E, bass.ds(i * SEQ, SEQ)].rearrange("e (a r t) -> e a r t", r=2, t=P)
                    for r in range(2):
                        act.activation(dst[:, :, r, :], psS[u][r * E:(r + 1) * E, :, :],
                                       ACT.Copy).then_inc(sc_done[u], 1)

            run_slots(act, slot)

        @block.gpsimd
        def _(pool):
            with pool.Fori(0, HB) as i:
                for u in range(2):
                    pool.wait_ge(xH_ready[u], ONE + i + 1)
                    at = bass.ds((i + u * HB) * SEQ, SEQ)
                    pool.tensor_tensor(xL[:, at], xT[u][:, :], xH[:, at].bitcast(F32),
                                       ALU.subtract).then_inc(xL_ready[u], 1)

        @block.tensor
        def _(pe):
            pe.wait_ge(w_in, ONE + 32)

            def slot(ahead, front, back):
                if front:
                    i, u = front
                    pe.wait_ge(xT_ready[u], ONE + i + 1)
                    pe.wait_ge(lg_done[u], ONE + i)
                    for j in range(TT):
                        mm = pe.matmul(psR[u][:, j, :], xT[u][:, j * P:(j + 1) * P], wr_sb[:, :],
                                       start=True, stop=True)
                    mm.then_inc(lg_ps[u], 1)
                if ahead:
                    i, u = ahead
                    pe.wait_ge(xn_ready[u], ONE + TT * i + TT)
                    pe.wait_ge(xH_ready[u], ONE + i)
                    for j in range(TT):
                        mm = pe.transpose(psT[u][:, j * P:(j + 1) * P], xn[u][:, j, :], cst[:, C_ID:C_ID + P])
                    mm.then_inc(xT_ps[u], 1)
                if back:
                    i, u = back
                    pe.wait_ge(pr_done[u], ONE + i + 1)
                    pe.wait_ge(sc_done[u], ONE + 2 * i)
                    for j in range(0, TT, 2):
                        mm = pe.transpose(psS[u][:, j // 2, :], pr[u][:, j:j + 2, :].rearrange("p a e -> p (a e)"),
                                          cst[:, C_ID:C_ID + P])
                    mm.then_inc(pT_ps[u], 1)

            run_slots(pe, slot)

        @block.vector
        def _(dve):
            fold_statistics(dve, st, tmp, mean, var_done)
            dve.wait_ge(std_done, ONE + 1)
            dve.reciprocal(rstd[:, :], std[:, :]).then_inc(rstd_done, 1)
            dve.wait_ge(rstd_done, ONE + 1)
            dve.wait_ge(w_in, ONE + 32)

            def normalise(i, u):
                t0 = (i + u * HB) * TT
                dve.wait_ge(xn_ready[u], ONE + TT * i)
                dve.tensor_scalar(stat[u][:, 0, :], mean[:, bass.ds(t0, TT)], 1.0, None,
                                  ALU.mult).then_inc(stat_done[u], 1)
                dve.tensor_scalar(stat[u][:, 1, :], rstd[:, bass.ds(t0, TT)], 1.0, None,
                                  ALU.mult).then_inc(stat_done[u], 1)
                dve.wait_ge(stat_done[u], ONE + 2 * i + 2)
                dve.wait_ge(xT_ps[u], ONE + i)
                for j in range(TT):
                    dve.tensor_scalar(xn[u][:, j, :], xres[:, bass.ds(t0 + j, 1), :], stat[u][:, 0, j:j + 1],
                                      stat[u][:, 1, j:j + 1], ALU.subtract, ALU.mult).then_inc(xn_ready[u], 1)

            def shift(i, u):
                dve.wait_ge(lg_ps[u], ONE + i + 1)
                dve.wait_ge(lc_done[u], ONE + i)
                dve.tensor_tensor(lg[u][:, :, :], psR[u][:, :, :],
                                  br_sb[:, :].unsqueeze(1).broadcast_to([P, TT, E]),
                                  ALU.add).then_inc(lg_done[u], 1)
                dve.wait_ge(lg_done[u], ONE + i + 1)
                dve.tensor_reduce(mx[u][:, :], lg[u][:, :, :], AX_X, ALU.max).then_inc(mx_done[u], 1)
                dve.wait_ge(mx_done[u], ONE + i + 1)
                dve.wait_ge(ex_done[u], ONE + i)
                dve.tensor_tensor(lc[u][:, :, :], lg[u][:, :, :],
                                  mx[u][:, :].unsqueeze(2).broadcast_to([P, TT, E]),
                                  ALU.subtract).then_inc(lc_done[u], 1)

            def scale(i, u):
                dve.wait_ge(ex_done[u], ONE + i + 1)
                dve.wait_ge(rs_done[u], ONE + i)
                dve.tensor_reduce(sm[u][:, :], ex[u][:, :, :], AX_X, ALU.add).then_inc(sm_done[u], 1)
                dve.wait_ge(sm_done[u], ONE + i + 1)
                dve.wait_ge(pr_done[u], ONE + i)
                dve.reciprocal(rs[u][:, :], sm[u][:, :]).then_inc(rs_done[u], 1)
                dve.wait_ge(rs_done[u], ONE + i + 1)
                dve.wait_ge(pT_ps[u], ONE + i)
                dve.tensor_tensor(pr[u][:, :, :], ex[u][:, :, :],
                                  rs[u][:, :].unsqueeze(2).broadcast_to([P, TT, E]),
                                  ALU.mult).then_inc(pr_done[u], 1)

            def slot(ahead, front, back):
                if back:
                    shift(*back)
                if ahead:
                    normalise(*ahead)
                if back:
                    scale(*back)

            run_slots(dve, slot)


def merge_steps(first, last):
    steps = []
    block = 2 * first
    while block <= last:
        steps.append((block, 0))
        steps += halving_steps(block // 2, 1)
        block *= 2
    return steps


def halving_steps(block, down_to):
    steps = []
    while block // 2 >= down_to:
        steps.append((block, block // 2))
        block //= 2
    return steps


def approach(dve, out, here, ago, count, count_ago, goal, tmp, sem, tally):
    num, den, move, cap = tmp
    dve.wait_ge(sem, ONE + tally.total)
    dve.tensor_tensor(den, count_ago, count, ALU.subtract).then_inc(sem, tally.one())
    if isinstance(goal, float):
        dve.tensor_scalar(num, count, goal, None, ALU.subtract).then_inc(sem, tally.one())
    else:
        dve.tensor_tensor(num, count, goal, ALU.subtract).then_inc(sem, tally.one())
    dve.tensor_tensor(move, here, ago, ALU.subtract).then_inc(sem, tally.one())
    dve.tensor_scalar(cap, here, 0.2, None, ALU.mult).then_inc(sem, tally.one())
    dve.wait_ge(sem, ONE + tally.total)
    dve.scalar_tensor_tensor(den, den, 0.0, den, ALU.is_equal, ALU.add).then_inc(sem, tally.one())
    dve.tensor_tensor(move, move, num, ALU.mult).then_inc(sem, tally.one())
    dve.wait_ge(sem, ONE + tally.total)
    dve.reciprocal(den, den).then_inc(sem, tally.one())
    dve.wait_ge(sem, ONE + tally.total)
    dve.tensor_tensor(move, move, den, ALU.mult).then_inc(sem, tally.one())
    dve.wait_ge(sem, ONE + tally.total)
    dve.tensor_tensor(move, move, cap, ALU.min).then_inc(sem, tally.one())
    dve.wait_ge(sem, ONE + tally.total)
    dve.scalar_tensor_tensor(move, cap, -1.0, move, ALU.mult, ALU.max).then_inc(sem, tally.one())
    dve.wait_ge(sem, ONE + tally.total)
    dve.tensor_tensor(out, here, move, ALU.add).then_inc(sem, tally.one())


class Tally:

    def __init__(self):
        self.total = 0

    def one(self):
        self.total += 1
        return 1


def sort_step(dve, src, dst, step, sem, tally):
    k, d = step
    if d:
        a = src.rearrange("p (n t d) -> p n t d", t=2, d=d)
        o = dst.rearrange("p (n t d) -> p n t d", t=2, d=d)
        i0, i1, o0, o1 = a[:, :, 0], a[:, :, 1], o[:, :, 0], o[:, :, 1]
    else:
        a = src.rearrange("p (n k) -> p n k", k=k)
        o = dst.rearrange("p (n k) -> p n k", k=k)
        i0, i1 = a[:, :, 0:k // 2], a[:, :, k - 1:k // 2 - 1:-1]
        o0, o1 = o[:, :, 0:k // 2], o[:, :, k - 1:k // 2 - 1:-1]
    dve.wait_ge(sem, ONE + tally.total)
    dve.tensor_tensor(o0, i0, i1, ALU.max).then_inc(sem, tally.one())
    dve.tensor_tensor(o1, i0, i1, ALU.min).then_inc(sem, tally.one())


def routing_phase(nc, wupT, wgateT, wdn, bdn, sel, cst, score, wU, wG, wD, selR, bdR, onesR, w_stage, bd_stage):
    sems = []
    with ExitStack() as ctx:
        def sb(name, shape, dt=F32):
            return ctx.enter_context(nc.sbuf_tensor(name, shape, dt))

        def sem(name):
            sems.append(ctx.enter_context(nc.semaphore(name)))
            return sems[-1]

        bufs = [sb("sort0", [P, HALF]), sb("sort1", [P, HALF])]
        runs = [sb("runs0", [P, FOUND]), sb("runs1", [P, FOUND])]
        level = sb("level", [P, LEVEL_ROUNDS])
        inv_level = sb("inv_level", [P, LEVEL_ROUNDS + 1])
        lcnt = sb("lcnt", [P, LEVEL_ROUNDS])
        lall = sb("lall", [P, LEVEL_ROUNDS])
        limit = [None] + [sb(f"limit{n}", [P, 2]) for n in range(1 + ROUNDS)]
        inv = [sb(f"inv{n}", [P, 2]) for n in range(2 + ROUNDS)]
        ranks = [sb(f"ranks{n}", [P, 2]) for n in range(2 + ROUNDS)]
        hcnt = [sb(f"hcnt{n}", [P, 2]) for n in range(1 + ROUNDS)]
        whole = sb("whole", [P, 4])
        goal = sb("goal", [P, 2])
        must = sb("must", [P, 2])
        num = sb("num", [P, 2])
        den = sb("r_den", [P, 2])
        move = sb("move", [P, 2])
        cap = sb("cap", [P, 2])
        empty = sb("empty", [P, 1])
        first = sb("first", [P, 1])
        inside = sb("inside", [P, 1])
        seen = sb("seen", [P, 1])
        pads = sb("pads", [P, 1])
        padrow = sb("padrow", [P, RUN])
        missed = sb("missed", [P, 6])
        miss_all = sb("miss_all", [1, 1], I32)
        pair = [sb("pair0", [E, 2 * RUN]), sb("pair1", [E, 2 * RUN])]
        wsum = sb("wsum", [E, WG])
        wmin = sb("wmin", [E, WG])
        spread_out = bufs[1][0:E, 0:E * WG].rearrange("p (e g) -> p e g", g=WG)
        beats = [bufs[0][:, n * E * WG:(n + 1) * E * WG] for n in range(WG // 2)]
        own = sb("own", [P, WG // 2])
        higher = sb("higher", [P, WG // 2])
        need = sb("need", [P, 1])
        least = sb("least", [P, 1])
        least_at = sb("least_at", [P, P])
        lam = sb("lam", [P, 1])
        wkept = sb("wkept", [E, WG])
        wout = sb("wout", [E, WG])
        nkept = sb("nkept", [E, 1])
        wrong = sb("wrong", [1, 1])
        gsum = sb("gsum", [P, NG // 2])
        gmin = sb("gmin", [P, NG // 2])
        G = sb("G", [E, NG])
        M = sb("M", [E, NG])
        cand = sb("cand", [E, 1], I32)
        dec = sb("dec", [E, 1], I32)
        cnt = sb("cnt", [E, 1])
        junk = sb("junk", [E, NG])
        gt = sb("gt", [E, NG])
        eqg = sb("eqg", [E, NG])
        left = sb("left", [E, 1])
        cum = sb("cum", [E, NG])
        pos = sb("pos", [E, NG])
        tot = sb("tot", [E, NG])
        take = sb("take", [E, NG])
        kept = sb("kept", [E, NG])
        big = sb("big", [E, NG])
        mins = sb("mins", [E, NG])
        lim = sb("lim", [E, 2])
        lim2 = sb("lim2", [P, 2])
        reach = sb("reach", [P, 2])
        excess = sb("excess", [1, 1], I32)
        same = sb("same", [P, 1])
        above = sb("above", [P, 1])
        other = sb("other", [P, 1])
        before = sb("before", [P, 1])
        room = sb("room", [P, 1])
        psC = ctx.enter_context(nc.psum_tensor("psC", [E, 1], F32))
        psA = ctx.enter_context(nc.psum_tensor("psA", [E, NG], F32))
        psB = ctx.enter_context(nc.psum_tensor("psB", [E, NG], F32))
        psS = ctx.enter_context(nc.psum_tensor("psS", [P, LEVEL_ROUNDS], F32))
        psK = ctx.enter_context(nc.psum_tensor("psK", [P, 2], F32))
        psQ = ctx.enter_context(nc.psum_tensor("psQ", [P, 2], F32))
        psW = ctx.enter_context(nc.psum_tensor("psW", [P, E * WG], F32))
        psX = ctx.enter_context(nc.psum_tensor("psX", [1, 1], F32))

        sorted_ = sem("sorted_")
        window = sem("window")
        level_counted = sem("level_counted")
        level_ps = sem("level_ps")
        limits_counted = sem("limits_counted")
        limits_ps = sem("limits_ps")
        groups_ready = sem("groups_ready")
        groups_ps = sem("groups_ps")
        missed_ready = sem("missed_ready")
        missed_ps = sem("missed_ps")
        gathered = sem("gathered")
        spread_ready = sem("spread_ready")
        spread_ps = sem("spread_ps")
        least_ready = sem("least_ready")
        least_ps = sem("least_ps")
        nkept_ready = sem("nkept_ready")
        nkept_ps = sem("nkept_ps")
        flag_ready = sem("flag_ready")
        full_lim = sem("full_lim")
        cand_ready = sem("cand_ready")
        cnt_ready = sem("cnt_ready")
        cnt_ps = sem("cnt_ps")
        dec_ready = sem("dec_ready")
        tie_in = sem("tie_in")
        tie_ps = sem("tie_ps")
        chain = sem("chain")
        lim_ready = sem("lim_ready")
        lim_moved = sem("lim_moved")
        reach_ready = sem("reach_ready")
        reach_ps = sem("reach_ps")
        excess_ready = sem("excess_ready")
        tied = sem("tied")
        w_in = [sem(f"w_in_{n}") for n in ("u", "g", "d", "s", "b")]
        w_high = sem("w_high")
        w_low = sem("w_low")
        bd_zero = sem("bd_zero")

        start_semaphores(nc, sems)
        block = ctx.enter_context(nc.Block())

        @block.sync
        def _(sp):
            sp.dma_start(w_stage[:, :], wupT).then_inc(w_in[0], 16)
            for r in range(0, P, E):
                sp.dma_start(bd_stage[r:r + E, :], bdn).then_inc(w_in[4], 16)
            sp.wait_ge(w_low, ONE + 1)
            sp.dma_start(w_stage[:, :], wgateT).then_inc(w_in[1], 16)
            sp.wait_ge(w_low, ONE + 2)
            sp.dma_start(w_stage[:, :], wdn).then_inc(w_in[2], 16)
            sp.wait_ge(w_low, ONE + 3)
            sp.dma_start(w_stage[:, :], sel).then_inc(w_in[3], 16)

        @block.gpsimd
        def _(pool):
            pool.memset(bdR[E:P, 1, :].bitcast(F32), 0.0).then_inc(bd_zero, 1)
            pool.wait_ge(bd_zero, ONE + 1)
            for n, w in enumerate((wU, wG, wD)):
                pool.wait_ge(w_high, ONE + n + 1)
                pool.tensor_tensor(w[:, 1, :], w_stage[:, :], w[:, 0, :].bitcast(F32),
                                   ALU.subtract).then_inc(w_low, 1)
            pool.wait_ge(w_high, ONE + 4)
            pool.wait_ge(w_low, ONE + 3)
            pool.tensor_tensor(bdR[0:E, 1, :], bd_stage[0:E, :], bdR[0:E, 0, :].bitcast(F32),
                               ALU.subtract).then_inc(w_low, 1)

        @block.scalar
        def _(act):
            for n, w in enumerate((wU, wG, wD)):
                act.wait_ge(w_in[n], ONE + 16)
                act.activation(w[:, 0, :], w_stage[:, :], ACT.Copy).then_inc(w_high, 1)
            act.wait_ge(w_in[4], ONE + 32)
            act.activation(bdR[:, 0, :], bd_stage[:, :], ACT.Copy).then_inc(w_high, 1)
            act.wait_ge(w_in[3], ONE + 16)
            act.activation(selR[:, :], w_stage[:, :], ACT.Copy).then_inc(w_high, 1)
            act.activation(onesR[:, :], cst[:, C_ONES:C_ONES + 2], ACT.Copy).then_inc(w_high, 1)
            act.wait_ge(lim_ready, ONE + 1)
            act.activation(lim2[0:E, :], lim[:, :], ACT.Copy).then_inc(lim_moved, 1)
            act.activation(lim2[E:P, :], lim[:, :], ACT.Copy).then_inc(lim_moved, 1)

        @block.tensor
        def _(pe):
            ones = cst[0:E, C_ONES:C_ONES + E]
            for n in range(LEVEL_ROUNDS):
                pe.wait_ge(level_counted, ONE + n + 1)
                pe.matmul(psS[:, n:n + 1], cst[:, C_ONES:C_ONES + P], lcnt[:, n:n + 1],
                          start=True, stop=True).then_inc(level_ps, 1)
            for n in range(1 + ROUNDS):
                pe.wait_ge(limits_counted, ONE + 2 * n + 2)
                pe.matmul(psK[:, :], cst[:, C_PAIR:C_PAIR + P], hcnt[n][:, :],
                          start=True, stop=True).then_inc(limits_ps, 1)
                if n == 0:
                    pe.wait_ge(groups_ready, ONE + 1)
                    pe.matmul(psQ[:, :], cst[0:E, C_ONES:C_ONES + P], whole[0:E, 1:3],
                              start=True, stop=True).then_inc(groups_ps, 1)
            pe.wait_ge(spread_ready, ONE + 1)
            pe.matmul(psW[:, :], cst[0:E, C_ONES:C_ONES + P], bufs[1][0:E, 0:E * WG],
                      start=True, stop=True)
            pe.matmul(psQ[:, 0:1], cst[0:E, C_ONES:C_ONES + P], first[0:E, :], start=True, stop=True).then_inc(spread_ps, 1)
            for n in range(6):
                pe.wait_ge(missed_ready, ONE + n + 1)
                pe.matmul(psS[0:1, 0:1], cst[:, C_ONES:C_ONES + 1], missed[:, n:n + 1], start=n == 0, stop=n == 5)
            pe.wait_ge(least_ready, ONE + 1)
            pe.matmul(psW[:, 0:P], cst[:, C_ONES:C_ONES + P], least_at[:, :], start=True, stop=True).then_inc(least_ps, 1)
            pe.wait_ge(nkept_ready, ONE + 1)
            pe.matmul(psQ[0:1, 1:2], cst[0:E, C_ONES:C_ONES + 1], nkept[:, :], start=True, stop=True).then_inc(nkept_ps, 1)
            pe.wait_ge(flag_ready, ONE + 1)
            useless = pe.value_load(miss_all[:, :], min_val=0, max_val=P * HALF)
            with pe.If(useless != 0):
                for b in range(31):
                    pe.wait_ge(cnt_ready, ONE + b + 1)
                    pe.matmul(psC[:, :], ones, cnt[:, :], start=True, stop=True).then_inc(cnt_ps, 1)
                pe.wait_ge(tie_in, ONE + 2)
                pe.matmul(psC[:, :], ones, cnt[:, :], start=True, stop=True).then_inc(tie_ps, 1)
                pe.matmul(psA[:, :], ones, eqg[:, :], start=True, stop=True).then_inc(tie_ps, 1)
                pe.matmul(psB[:, :], cst[0:E, C_TRI:C_TRI + E], eqg[:, :], start=True, stop=True).then_inc(tie_ps, 1)
            pe.wait_ge(reach_ready, ONE + 2)
            pe.matmul(psX[:, :], cst[:, C_ONES:C_ONES + 1], reach[:, 0:1], start=True, stop=False)
            pe.matmul(psX[:, :], cst[:, C_ONES:C_ONES + 1], reach[:, 1:2], start=False, stop=True).then_inc(reach_ps, 1)

        @block.vector
        def _(dve):
            S0, S1 = bufs
            done = Tally()
            for n, guess in enumerate(LEVELS):
                dve.memset(level[:, n:n + 1], guess).then_inc(window, done.one())
                dve.memset(inv_level[:, n:n + 1], 1.0 / guess).then_inc(window, done.one())
            tmp1 = [t[:, 0:1] for t in (num, den, move, cap)]
            for n in range(LEVEL_ROUNDS):
                dve.wait_ge(window, ONE + done.total)
                dve.tensor_scalar(bufs[n % 2][:, 0:SAMPLE], score[:, 0:SAMPLE], level[:, n:n + 1], 0.0,
                                  ALU.is_ge, ALU.add, accum_out=lcnt[:, n:n + 1]).then_inc(level_counted, 1)
                if n:
                    dve.wait_ge(level_ps, ONE + n + 1)
                    dve.tensor_copy(lall[:, n - 1:n + 1], psS[:, n - 1:n + 1]).then_inc(window, done.one())
                    approach(dve, inv_level[:, n + 1:n + 2], inv_level[:, n:n + 1], inv_level[:, n - 1:n],
                             lall[:, n:n + 1], lall[:, n - 1:n], float(BUDGET * GROUP * SAMPLE // HALF),
                             tmp1, window, done)
                    if n + 1 < LEVEL_ROUNDS:
                        dve.wait_ge(window, ONE + done.total)
                        dve.reciprocal(level[:, n + 1:n + 2], inv_level[:, n + 1:n + 2]).then_inc(window, done.one())
            dve.wait_ge(window, ONE + done.total)
            il = inv_level[:, LEVEL_ROUNDS:LEVEL_ROUNDS + 1]
            for side in range(2):
                dve.tensor_scalar(inv[side][:, 1 - side:2 - side], il, 1.0 / (1.0 + SPREAD), None,
                                  ALU.mult).then_inc(window, done.one())
                dve.tensor_scalar(inv[side][:, side:side + 1], il, 1.0 / (1.0 - SPREAD), None,
                                  ALU.mult).then_inc(window, done.one())
            dve.wait_ge(window, ONE + done.total)
            dve.reciprocal(limit[1][:, :], inv[1][:, :]).then_inc(window, done.one())
            for r in range(1 + ROUNDS):
                here, then = limit[r + 1], ranks[r]
                dve.wait_ge(window, ONE + done.total)
                for c in range(2):
                    dve.tensor_scalar(bufs[c][:, :], score[:, :], here[:, c:c + 1], 0.0, ALU.is_ge, ALU.add,
                                      accum_out=hcnt[r][:, c:c + 1]).then_inc(limits_counted, 1)
                dve.wait_ge(limits_ps, ONE + r + 1)
                dve.tensor_copy(ranks[r + 1][:, :], psK[:, :]).then_inc(window, done.one())
                if r == 0:
                    dve.tensor_copy(then[:, 0:1], psK[:, 1:2]).then_inc(window, done.one())
                    dve.tensor_copy(then[:, 1:2], psK[:, 0:1]).then_inc(window, done.one())
                    dve.tensor_scalar(whole[:, 0:2], psK[:, :], 1.0 / GROUP, -63.0 / 128, ALU.mult,
                                      ALU.add).then_inc(window, done.one())
                    dve.tensor_scalar(whole[:, 2:4], psK[:, :], 1.0 / GROUP, 63.0 / 128, ALU.mult,
                                      ALU.add).then_inc(window, done.one())
                    dve.wait_ge(window, ONE + done.total)
                    dve.tensor_scalar(whole[:, :], whole[:, :], ROUND, None, ALU.add).then_inc(window, done.one())
                    dve.wait_ge(window, ONE + done.total)
                    dve.tensor_scalar(whole[:, :], whole[:, :], -ROUND, None, ALU.add).then_inc(groups_ready, 1)
                    dve.wait_ge(groups_ready, ONE + 1)
                    dve.tensor_scalar(must[:, 0:1], whole[:, 0:1], float(GROUP), -1.0, ALU.mult,
                                      ALU.add).then_inc(window, done.one())
                    dve.tensor_scalar(must[:, 1:2], whole[:, 3:4], float(GROUP), None,
                                      ALU.mult).then_inc(window, done.one())
                    dve.tensor_scalar(goal[:, 0:1], whole[:, 0:1], float(GROUP), -SLACK, ALU.mult,
                                      ALU.add).then_inc(window, done.one())
                    dve.tensor_scalar(goal[:, 1:2], whole[:, 3:4], float(GROUP), SLACK, ALU.mult,
                                      ALU.add).then_inc(window, done.one())
                    dve.tensor_scalar(empty[:, :], whole[:, 0:1], 0.0, 2.0, ALU.is_equal,
                                      ALU.mult).then_inc(window, done.one())
                    dve.wait_ge(window, ONE + done.total)
                    dve.tensor_scalar(must[:, 0:1], must[:, 0:1], 0.0, None, ALU.max).then_inc(window, done.one())
                    dve.tensor_scalar(goal[:, 0:1], goal[:, 0:1], 0.0, None, ALU.max).then_inc(window, done.one())
                if r < ROUNDS:
                    approach(dve, inv[r + 2][:, :], inv[r + 1][:, :], inv[r][:, :], ranks[r + 1][:, :], then[:, :],
                             goal[:, :], [t[:, :] for t in (num, den, move, cap)], window, done)
                    dve.wait_ge(window, ONE + done.total)
                    dve.reciprocal(limit[r + 2][:, :], inv[r + 2][:, :]).then_inc(window, done.one())
                if r == ROUNDS - 1:
                    dve.wait_ge(window, ONE + done.total)
                    dve.tensor_tensor(limit[r + 2][:, 0:1], limit[r + 2][:, 0:1], empty[:, :],
                                      ALU.add).then_inc(window, done.one())
            top, bottom = limit[1 + ROUNDS][:, 0:1], limit[1 + ROUNDS][:, 1:2]
            reached = ranks[1 + ROUNDS]
            dve.scalar_tensor_tensor(S0[:, :], score[:, :], top, score[:, :], ALU.is_lt,
                                     ALU.mult).then_inc(window, done.one())
            dve.tensor_scalar(first[:, :], psK[:, 0:1], 1.0 / GROUP, -63.0 / 128, ALU.mult,
                              ALU.add).then_inc(window, done.one())
            dve.wait_ge(window, ONE + done.total)
            for c in range(HALF // CHUNK):
                dve.max(runs[0][:, 8 * c:8 * c + 8], S0[:, c * CHUNK:(c + 1) * CHUNK]).then_inc(gathered, 1)
            dve.tensor_scalar(first[:, :], first[:, :], ROUND, None, ALU.add).then_inc(window, done.one())
            dve.memset(padrow[:, :], 0.0).then_inc(window, done.one())
            dve.wait_ge(window, ONE + done.total)
            dve.tensor_scalar(first[:, :], first[:, :], -ROUND, None, ALU.add).then_inc(window, done.one())
            dve.wait_ge(window, ONE + done.total)
            dve.scalar_tensor_tensor(pads[:, :], first[:, :], -float(GROUP), reached[:, 0:1], ALU.mult,
                                     ALU.add).then_inc(window, done.one())
            dve.wait_ge(window, ONE + done.total)
            dve.tensor_scalar(padrow[0:E, 0:GROUP], cst[0:E, C_IOTA:C_IOTA + GROUP], pads[0:E, :], ABOVE, ALU.is_lt,
                              ALU.mult).then_inc(window, done.one())
            dve.wait_ge(groups_ps, ONE + 1)
            dve.tensor_scalar(missed[:, 0:1], psQ[:, 1:2], float(BUDGET), None, ALU.is_gt).then_inc(missed_ready, 1)
            dve.tensor_scalar(missed[:, 1:2], psQ[:, 0:1], float(BUDGET), None, ALU.is_lt).then_inc(missed_ready, 1)
            dve.tensor_tensor(missed[:, 2:3], reached[:, 0:1], must[:, 0:1], ALU.is_gt).then_inc(missed_ready, 1)
            dve.tensor_tensor(missed[:, 3:4], reached[:, 1:2], must[:, 1:2], ALU.is_lt).then_inc(missed_ready, 1)
            dve.tensor_tensor(inside[:, :], hcnt[ROUNDS][:, 1:2], hcnt[ROUNDS][:, 0:1],
                              ALU.subtract).then_inc(window, done.one())
            dve.wait_ge(gathered, ONE + HALF // CHUNK)
            a, b = runs
            width, run = FOUND, 8
            for longest in (32, 128):
                for step in merge_steps(run, longest):
                    sort_step(dve, a[:, 0:width], b[:, 0:width], step, window, done)
                    a, b = b, a
                w = a[:, 0:width].rearrange("p (n k) -> p n k", k=2 * longest)
                width, run = width // 2, longest
                dve.wait_ge(window, ONE + done.total)
                dve.tensor_tensor(b[:, 0:width].rearrange("p (n k) -> p n k", k=run), w[:, :, 0:run],
                                  w[:, :, 2 * run - 1:run - 1:-1], ALU.max).then_inc(window, done.one())
                a, b = b, a
                for step in halving_steps(run, 1):
                    sort_step(dve, a[:, 0:width], b[:, 0:width], step, window, done)
                    a, b = b, a
            for step in merge_steps(run, RUN):
                sort_step(dve, a[:, 0:width], b[:, 0:width], step, window, done)
                a, b = b, a
            dve.wait_ge(window, ONE + done.total)
            dve.tensor_scalar(b[:, RUN:2 * RUN], a[:, 0:RUN], bottom, 0.0, ALU.is_ge, ALU.add,
                              accum_out=seen[:, :]).then_inc(window, done.one())
            dve.tensor_tensor(b[:, 0:RUN], a[:, 0:RUN], padrow[:, ::-1], ALU.max).then_inc(window, done.one())
            a, b = b, a
            for step in halving_steps(RUN, 1):
                sort_step(dve, a[:, 0:RUN], b[:, 0:RUN], step, window, done)
                a, b = b, a
            dve.wait_ge(window, ONE + done.total)
            dve.tensor_tensor(missed[:, 4:5], seen[:, :], inside[:, :], ALU.is_lt).then_inc(missed_ready, 1)
            dve.tensor_tensor(missed[:, 5:6], a[:, RUN - 1:RUN], bottom, ALU.is_ge).then_inc(missed_ready, 1)
            dve.tensor_copy(pair[0][:, 0:RUN], a[0:E, 0:RUN]).then_inc(window, done.one())
            dve.tensor_copy(pair[0][:, RUN:2 * RUN], a[E:P, 0:RUN]).then_inc(window, done.one())
            a, b = pair
            for step in [(2 * RUN, 0)] + halving_steps(RUN, GROUP):
                sort_step(dve, a[:, :], b[:, :], step, window, done)
                a, b = b, a
            dve.wait_ge(window, ONE + done.total)
            g = a[:, :].rearrange("p (g r) -> p g r", r=GROUP)
            dve.tensor_reduce(wsum[:, :], g, AX_X, ALU.add).then_inc(window, done.one())
            dve.tensor_reduce(wmin[:, :], g, AX_X, ALU.min).then_inc(window, done.one())
            dve.wait_ge(window, ONE + done.total)
            dve.tensor_tensor(spread_out, wsum[:, :].unsqueeze(1).broadcast_to([E, E, WG]),
                              cst[0:E, C_ID:C_ID + E].unsqueeze(2).broadcast_to([E, E, WG]),
                              ALU.mult).then_inc(spread_ready, 1)
            dve.tensor_copy(own[0:E, :], wsum[:, 0:WG // 2]).then_inc(window, done.one())
            dve.tensor_copy(own[E:P, :], wsum[:, WG // 2:WG]).then_inc(window, done.one())
            dve.wait_ge(window, ONE + done.total)
            dve.wait_ge(spread_ps, ONE + 1)
            dve.tensor_scalar(need[:, :], psQ[:, 0:1], -1.0, float(BUDGET), ALU.mult,
                              ALU.add).then_inc(window, done.one())
            for j in range(WG // 2):
                dve.tensor_scalar(beats[j], psW[:, :], own[:, j:j + 1], 0.0, ALU.is_gt, ALU.add,
                                  accum_out=higher[:, j:j + 1]).then_inc(window, done.one())
            dve.wait_ge(window, ONE + done.total)
            dve.tensor_scalar(higher[:, :], higher[:, :], need[:, :], 100.0 * ABOVE, ALU.is_ge,
                              ALU.mult).then_inc(window, done.one())
            dve.wait_ge(window, ONE + done.total)
            dve.tensor_tensor(higher[:, :], higher[:, :], own[:, :], ALU.add).then_inc(window, done.one())
            dve.wait_ge(window, ONE + done.total)
            dve.tensor_reduce(least[:, :], higher[:, :], AX_X, ALU.min).then_inc(window, done.one())
            dve.wait_ge(window, ONE + done.total)
            dve.tensor_scalar(least_at[:, :], cst[:, C_ID:C_ID + P], least[:, :], None,
                              ALU.mult).then_inc(least_ready, 1)
            dve.wait_ge(least_ps, ONE + 1)
            dve.tensor_reduce(lam[:, :], psW[:, 0:P], AX_X, ALU.min).then_inc(window, done.one())
            dve.wait_ge(window, ONE + done.total)
            dve.tensor_scalar(wkept[:, :], wsum[:, :], lam[0:E, :], 0.0, ALU.is_ge, ALU.add,
                              accum_out=nkept[:, :]).then_inc(window, done.one())
            dve.tensor_scalar(wout[:, :], wsum[:, :], lam[0:E, :], 4.0, ALU.is_lt, ALU.mult).then_inc(window, done.one())
            dve.wait_ge(window, ONE + done.total)
            dve.tensor_tensor(nkept[:, :], nkept[:, :], first[0:E, :], ALU.add).then_inc(nkept_ready, 1)
            dve.tensor_tensor(wout[:, :], wout[:, :], wmin[:, :], ALU.add).then_inc(window, done.one())
            dve.wait_ge(window, ONE + done.total)
            dve.wait_ge(nkept_ready, ONE + 1)
            dve.tensor_reduce(lim[:, 0:1], wout[:, :], AX_X, ALU.min).then_inc(window, done.one())
            dve.tensor_scalar(lim[:, 1:2], nkept[:, :], float(GROUP), None, ALU.mult).then_inc(window, done.one())
            dve.wait_ge(nkept_ps, ONE + 1)
            dve.tensor_scalar(wrong[:, :], psQ[0:1, 1:2], float(BUDGET), -1.0, ALU.is_equal,
                              ALU.mult).then_inc(window, done.one())
            dve.wait_ge(window, ONE + done.total)
            dve.scalar_tensor_tensor(miss_all[:, :], wrong[:, :], 1.0, psS[0:1, 0:1], ALU.add,
                                     ALU.add).then_inc(flag_ready, 1)
            dve.wait_ge(flag_ready, ONE + 1)
            useless = dve.value_load(miss_all[:, :], min_val=0, max_val=P * HALF)
            with dve.If(useless != 0):
                full = Tally()
                src, dst = score, S0
                for step in merge_steps(1, HALF):
                    sort_step(dve, src[:, :], dst[:, :], step, sorted_, full)
                    src, dst = dst, S1 if dst is S0 else S0
                dve.wait_ge(sorted_, ONE + full.total)
                dve.tensor_copy(dst[E:P, :], src[0:E, :]).then_inc(sorted_, full.one())
                dve.tensor_copy(dst[0:E, :], src[E:P, :]).then_inc(sorted_, full.one())
                dve.wait_ge(sorted_, ONE + full.total)
                dve.tensor_tensor(src[0:E, :], src[0:E, :], dst[0:E, ::-1], ALU.max).then_inc(sorted_, full.one())
                dve.tensor_tensor(src[E:P, :], src[E:P, :], dst[E:P, ::-1], ALU.min).then_inc(sorted_, full.one())
                for step in halving_steps(HALF, GROUP):
                    sort_step(dve, src[:, :], dst[:, :], step, sorted_, full)
                    src, dst = dst, src
                dve.wait_ge(sorted_, ONE + full.total)
                g = src[:, :].rearrange("p (g r) -> p g r", r=GROUP)
                dve.tensor_reduce(gsum[:, :], g, AX_X, ALU.add).then_inc(sorted_, full.one())
                dve.tensor_reduce(gmin[:, :], g, AX_X, ALU.min).then_inc(sorted_, full.one())
                dve.wait_ge(sorted_, ONE + full.total)
                for half in range(2):
                    dve.tensor_copy(G[:, half * NG // 2:(half + 1) * NG // 2],
                                    gsum[half * E:(half + 1) * E, :]).then_inc(sorted_, full.one())
                    dve.tensor_copy(M[:, half * NG // 2:(half + 1) * NG // 2],
                                    gmin[half * E:(half + 1) * E, :]).then_inc(sorted_, full.one())
                dve.wait_ge(sorted_, ONE + full.total)
                dve.memset(cand[:, :], 1 << 30).then_inc(cand_ready, 1)
                for n, b in enumerate(range(30, -1, -1)):
                    dve.wait_ge(cand_ready, ONE + n + 1)
                    if n:
                        dve.wait_ge(cnt_ps, ONE + n)
                    dve.tensor_scalar(junk[:, :], G[:, :], cand[:, :].bitcast(F32), 0.0, ALU.is_ge, ALU.add,
                                      accum_out=cnt[:, :]).then_inc(cnt_ready, 1)
                    dve.wait_ge(cnt_ps, ONE + n + 1)
                    dve.tensor_scalar(dec[:, :], psC[:, :], float(BUDGET), float(1 << b), ALU.is_lt,
                                      ALU.mult).then_inc(dec_ready, 1)
                    dve.wait_ge(dec_ready, ONE + n + 1)
                    dve.scalar_tensor_tensor(cand[:, :], dec[:, :], (1 << b) >> 1, cand[:, :], ALU.bitwise_or,
                                             ALU.bitwise_xor).then_inc(cand_ready, 1)
                dve.wait_ge(cand_ready, ONE + 32)
                last = cand[:, :].bitcast(F32)
                dve.tensor_scalar(gt[:, :], G[:, :], last, 0.0, ALU.is_gt, ALU.add,
                                  accum_out=cnt[:, :]).then_inc(tie_in, 1)
                dve.tensor_scalar(eqg[:, :], G[:, :], last, None, ALU.is_equal).then_inc(tie_in, 1)
                dve.wait_ge(tie_ps, ONE + 3)
                dve.tensor_scalar(left[:, :], psC[:, :], -1.0, float(BUDGET), ALU.mult, ALU.add).then_inc(chain, 1)
                dve.tensor_copy(tot[:, :], psA[:, :]).then_inc(chain, 1)
                dve.wait_ge(chain, ONE + 2)
                dve.tensor_tensor_scan(cum[:, :], tot[:, :], tot[:, :], 0.0, ALU.add, ALU.bypass).then_inc(chain, 1)
                dve.wait_ge(chain, ONE + 3)
                dve.tensor_tensor(pos[:, :], cum[:, :], tot[:, :], ALU.subtract).then_inc(chain, 1)
                dve.wait_ge(chain, ONE + 4)
                dve.tensor_tensor(cum[:, :], psB[:, :], pos[:, :], ALU.add).then_inc(chain, 1)
                dve.wait_ge(chain, ONE + 5)
                dve.scalar_tensor_tensor(take[:, :], cum[:, :], left[:, :], eqg[:, :], ALU.is_lt,
                                         ALU.mult).then_inc(chain, 1)
                dve.wait_ge(chain, ONE + 6)
                dve.tensor_tensor(kept[:, :], take[:, :], gt[:, :], ALU.add).then_inc(chain, 1)
                dve.wait_ge(chain, ONE + 7)
                dve.tensor_scalar(big[:, :], kept[:, :], -4.0, 4.0, ALU.mult, ALU.add).then_inc(chain, 1)
                dve.tensor_reduce(cnt[:, :], kept[:, :], AX_X, ALU.add).then_inc(chain, 1)
                dve.wait_ge(chain, ONE + 9)
                dve.tensor_tensor(mins[:, :], big[:, :], M[:, :], ALU.add).then_inc(chain, 1)
                dve.tensor_scalar(lim[:, 1:2], cnt[:, :], float(GROUP), None, ALU.mult).then_inc(full_lim, 1)
                dve.wait_ge(chain, ONE + 10)
                dve.tensor_reduce(lim[:, 0:1], mins[:, :], AX_X, ALU.min).then_inc(full_lim, 1)
                dve.wait_ge(full_lim, ONE + 2)
            dve.sem_inc(lim_ready, 1)
            dve.wait_ge(lim_moved, ONE + 2)
            thr = lim2[:, 0:1]
            dve.tensor_scalar(S0[:, :], score[:, :], thr, 0.0, ALU.is_ge, ALU.add,
                              accum_out=reach[:, 0:1]).then_inc(reach_ready, 1)
            dve.tensor_scalar(reach[:, 1:2], lim2[:, 1:2], -0.5, None, ALU.mult).then_inc(reach_ready, 1)
            dve.wait_ge(reach_ps, ONE + 1)
            dve.tensor_copy(excess[:, :], psX[:, :]).then_inc(excess_ready, 1)
            dve.wait_ge(excess_ready, ONE + 1)
            surplus = dve.value_load(excess[:, :], min_val=0, max_val=2 * E * HALF)
            with dve.If(surplus != 0):
                dve.tensor_scalar(S0[:, :], score[:, :], thr, 0.0, ALU.is_equal, ALU.add,
                                  accum_out=same[:, :]).then_inc(tied, 1)
                dve.tensor_scalar(S1[:, :], score[:, :], thr, 0.0, ALU.is_gt, ALU.add,
                                  accum_out=above[:, :]).then_inc(tied, 1)
                dve.memset(before[0:E, :], 0.0).then_inc(tied, 1)
                dve.wait_ge(tied, ONE + 3)
                dve.tensor_copy(before[E:P, :], same[0:E, :]).then_inc(tied, 1)
                dve.tensor_copy(other[E:P, :], above[0:E, :]).then_inc(tied, 1)
                dve.tensor_copy(other[0:E, :], above[E:P, :]).then_inc(tied, 1)
                dve.tensor_tensor(room[:, :], lim2[:, 1:2], above[:, :], ALU.subtract).then_inc(tied, 1)
                dve.wait_ge(tied, ONE + 7)
                dve.tensor_tensor(room[:, :], room[:, :], other[:, :], ALU.subtract).then_inc(tied, 1)
                dve.tensor_tensor_scan(S1[:, :], S0[:, :], S0[:, :], before[:, :], ALU.add,
                                       ALU.bypass).then_inc(tied, 1)
                dve.wait_ge(tied, ONE + 9)
                dve.scalar_tensor_tensor(S1[:, :], S1[:, :], room[:, :], S0[:, :], ALU.is_gt,
                                         ALU.mult).then_inc(tied, 1)
                dve.wait_ge(tied, ONE + 10)
                dve.tensor_scalar(S0[:, :], S1[:, :], -1.0, 1.0, ALU.mult, ALU.add).then_inc(tied, 1)
                dve.wait_ge(tied, ONE + 11)
                dve.tensor_tensor(score[:, :], score[:, :], S0[:, :], ALU.mult).then_inc(tied, 1)
                dve.wait_ge(tied, ONE + 12)
            dve.scalar_tensor_tensor(score[:, :], score[:, :], thr, score[:, :], ALU.is_ge, ALU.mult)


def experts_phase(nc, out, xsave, par, cst, score, xH, xL, wU, wG, wD, selR, bdR, onesR):
    sems = []
    with ExitStack() as ctx:
        def sb(name, shape, dt=F32, side="left"):
            return ctx.enter_context(nc.sbuf_tensor(name, shape, dt, side=side))

        def sb2(name, shape, dt=F32):
            return [sb(f"{name}{u}", shape, dt) for u in range(2)]

        def ps2(name, shape):
            return [ctx.enter_context(nc.psum_tensor(f"{name}{u}", shape, F32)) for u in range(2)]

        def sem(name):
            sems.append(ctx.enter_context(nc.semaphore(name)))
            return sems[-1]

        def sem2(name):
            return [sem(f"{name}{u}") for u in range(2)]

        raw = sb2("raw", [P, SEQ])
        fs = sb2("fs", [P, SEQ], F32R)
        xr = [sb(f"xr{u}", [P, TT, P], side="right") for u in range(2)]
        act_u = sb2("act_u", [P, SEQ])
        gated = sb2("gated", [P, SEQ])
        hid = sb2("hid", [P, SEQ])
        hidH = [sb(f"hidH{q}", [P, SEQ], F32R) for q in range(4)]
        hidL = [sb(f"hidL{q}", [P, SEQ], F32R) for q in range(4)]
        oT = [sb(f"oT{u}", [P, SEQ], side="right") for u in range(2)]
        den = sb2("e_den", [P, TT])
        rden = sb2("e_rden", [P, TT])
        psF = ps2("psF", [P, SEQ])
        psU = ps2("psU", [P, SEQ])
        psG = ps2("psG", [P, SEQ])
        psO = ctx.enter_context(nc.psum_tensor("psO", [P, SEQ], F32))
        psT = ctx.enter_context(nc.psum_tensor("psT_e", [P, SEQ], F32))

        fs_high = sem2("fs_high")
        fs_ready = sem2("fs_ready")
        raw_in = [ctx.enter_context(nc.semaphore(f"raw_in{u}")) for u in range(2)]
        xr_in = [ctx.enter_context(nc.semaphore(f"xr_in{u}")) for u in range(2)]
        up_ps = sem2("up_ps")
        gate_ps = sem2("gate_ps")
        silu_ready = sem2("silu_ready")
        gated_ready = sem2("gated_ready")
        hid_ready = sem2("hid_ready")
        hidH_ready = [sem(f"hidH_ready{q}") for q in range(4)]
        hidL_ready = [sem(f"hidL_ready{q}") for q in range(4)]
        score_ps = sem2("score_ps")
        down_done = [sem(f"down_done{q}") for q in range(4)]
        den_ps = sem2("den_ps")
        den_done = sem2("e_den_done")
        rden_done = sem2("e_rden_done")
        oT_ready = sem2("oT_ready")
        oTT_ps = sem2("oTT_ps")
        y_ready = sem2("e_y_ready")
        y_out = sem2("y_out")

        out_t = out.rearrange("b (j p) d -> b p j d", p=P)
        QC = 2 * CH // 4
        LAG = 4
        TURN = LAG + 1
        SUMS = TURN + 3
        start_semaphores(nc, sems, raw_in + xr_in)
        block = ctx.enter_context(nc.Block())

        @block.sync
        def _(sp):
            with sp.Fori(0, HB) as i:
                for h in range(2):
                    sp.wait_ge(y_ready[h], ONE + TT * i + TT)
                    sp.dma_start(out_t[bass.ds(i + h * HB, 1)].rearrange("b p j d -> (b p) j d"),
                                 xr[h][:, :, :]).then_inc(y_out[h], 16)
            for h in range(2):
                sp.wait_ge(y_out[h], ONE + 16 * HB)

        @block.gpsimd
        def _(pool):
            with pool.Fori(0, HB) as i:
                for h in range(2):
                    pool.wait_ge(y_out[h], ONE + 16 * i)
                    for part in (0, E):
                        pool.dma_start(raw[h][part:part + E, :],
                                       score[h * E:(h + 1) * E, bass.ds(i * SEQ, SEQ)]).then_inc(raw_in[h], 16)
                    pool.dma_start(xr[h][:, :, :], xsave[:, bass.ds((i + h * HB) * TT, TT), :]).then_inc(xr_in[h], 16)
                    pool.wait_ge(raw_in[h], 32 * i + 32)
                    pool.tensor_tensor(fs[h][:, :], raw[h][:, :], cst[:, C_ONES:C_ONES + 1].broadcast_to([P, SEQ]),
                                       ALU.mult).then_inc(fs_high[h], 1)
                    pool.wait_ge(fs_high[h], ONE + i + 1)
                    pool.tensor_tensor(fs[h][E:P, :], raw[h][E:P, :], fs[h][E:P, :].bitcast(F32),
                                       ALU.subtract).then_inc(fs_ready[h], 1)
                    pool.wait_ge(fs_ready[h], ONE + i + 1)

        def run_pairs(eng, step):
            for g in range(2 * CH):
                step(0, g, True)
            with eng.Fori(1, HB) as i:
                for g in range(2 * CH):
                    step(i, g, False)

        def back(i, g, k, first=False):
            if g >= k:
                return i, g - k
            return None if first else (i - 1, 2 * CH + g - k)

        def batch_before(i, h, first):
            if h:
                return i, 0
            return None if first else (i - 1, 1)

        @block.scalar
        def _(act):
            def silu(i, g):
                p, n, c = g % 2, i * CH + g // 2, g % CH
                act.wait_ge(up_ps[p], ONE + n + 1)
                act.wait_ge(gated_ready[p], ONE + n)
                act.activation(act_u[p][:, :], psU[p][:, :], ACT.Silu,
                               bias=par[:, V_BUP + c:V_BUP + c + 1]).then_inc(silu_ready[p], 1)

            def high_part(i, g):
                p, n, q, m = g % 2, i * CH + g // 2, g % 4, i * QC + g // 4
                act.wait_ge(hid_ready[p], ONE + n + 1)
                act.wait_ge(down_done[q], ONE + m)
                act.activation(hidH[q][:, :], hid[p][:, :], ACT.Copy).then_inc(hidH_ready[q], 1)

            def store_sum(i, h):
                act.wait_ge(down_done[3], ONE + i * QC + (h + 1) * QC // 2)
                act.wait_ge(oTT_ps[h], ONE + i)
                act.activation(oT[h][:, :], psO[:, :], ACT.Copy).then_inc(oT_ready[h], 1)

            def step(i, g, first):
                h, c = g // CH, g % CH
                before = batch_before(i, h, first)
                if c == LAG and before:
                    store_sum(*before)
                silu(i, g)
                if back(i, g, 2, first):
                    high_part(*back(i, g, 2))

            run_pairs(act, step)
            for g in range(2 * CH - 2, 2 * CH):
                high_part(HB - 1, g)
            store_sum(HB - 1, 1)

        @block.tensor
        def _(pe):
            def products(i, g):
                h, c = g // CH, g % CH
                p, n = g % 2, i * CH + g // 2
                tok = bass.ds((i + h * HB) * SEQ, SEQ)
                lo, hi = c * P, (c + 1) * P
                if c == 0:
                    pe.wait_ge(fs_ready[h], ONE + i + 1)
                for w, ps, used, done in ((wU, psU, silu_ready, up_ps), (wG, psG, gated_ready, gate_ps)):
                    pe.wait_ge(used[p], ONE + n)
                    pe.matmul(ps[p][:, :], w[:, 0, lo:hi], xL[:, tok], start=True, stop=False)
                    pe.matmul(ps[p][:, :], w[:, 0, lo:hi], xH[:, tok], start=False, stop=False)
                    pe.matmul(ps[p][:, :], w[:, 1, lo:hi], xH[:, tok], start=False, stop=True).then_inc(done[p], 1)
                pe.wait_ge(hid_ready[p], ONE + n)
                pe.matmul(psF[p][:, :], selR[:, lo:hi], fs[h][:, :], start=True, stop=True).then_inc(score_ps[p], 1)

            def down(i, g):
                q, m, c = g % 4, i * QC + g // 4, g % CH
                pe.wait_ge(hidH_ready[q], ONE + m + 1)
                pe.wait_ge(hidL_ready[q], ONE + m + 1)
                pe.matmul(psO[:, :], wD[:, 1, c * P:(c + 1) * P], hidH[q][:, :], start=False, stop=False)
                pe.matmul(psO[:, :], wD[:, 0, c * P:(c + 1) * P], hidH[q][:, :], start=False, stop=False)
                pe.matmul(psO[:, :], wD[:, 0, c * P:(c + 1) * P], hidL[q][:, :], start=False,
                          stop=(c == CH - 1)).then_inc(down_done[q], 1)

            def begin(i, h):
                pe.wait_ge(oT_ready[1 - h], ONE + i + h)
                pe.matmul(psO[:, :], bdR[:, 0, :], fs[h][:, :], start=True, stop=False)
                pe.matmul(psO[:, :], bdR[:, 1, :], fs[h][:, :], start=False, stop=False)

            def score_sums(i, h):
                pe.wait_ge(y_ready[1 - h], ONE + TT * (i + h))
                for j in range(TT):
                    mm = pe.matmul(psT[:, 2 * j:2 * j + 2], fs[h][:, j * P:(j + 1) * P], onesR[:, :],
                                   start=True, stop=True)
                mm.then_inc(den_ps[h], 1)

            def turn(i, h):
                pe.wait_ge(oT_ready[h], ONE + i + 1)
                pe.wait_ge(den_done[h], ONE + i + 1)
                for j in range(TT):
                    mm = pe.transpose(psT[:, j * P:(j + 1) * P], oT[h][:, j * P:(j + 1) * P], cst[:, C_ID:C_ID + P])
                mm.then_inc(oTT_ps[h], 1)

            def step(i, g, first):
                h, c = g // CH, g % CH
                before = batch_before(i, h, first)
                products(i, g)
                if c == LAG:
                    begin(i, h)
                if back(i, g, LAG, first):
                    down(*back(i, g, LAG))
                if c == TURN and before:
                    turn(*before)
                if c == SUMS:
                    score_sums(i, h)

            run_pairs(pe, step)
            for g in range(2 * CH - LAG, 2 * CH):
                down(HB - 1, g)
            turn(HB - 1, 1)

        @block.vector
        def _(dve):
            def gate(i, g):
                p, n, c = g % 2, i * CH + g // 2, g % CH
                dve.wait_ge(gate_ps[p], ONE + n + 1)
                dve.wait_ge(silu_ready[p], ONE + n + 1)
                dve.wait_ge(hid_ready[p], ONE + n)
                dve.scalar_tensor_tensor(gated[p][:, :], psG[p][:, :], par[:, V_BGATE + c:V_BGATE + c + 1],
                                         act_u[p][:, :], ALU.add, ALU.mult).then_inc(gated_ready[p], 1)

            def weigh(i, g, first=False):
                p, n = g % 2, i * CH + g // 2
                dve.wait_ge(gated_ready[p], ONE + n + 1)
                dve.wait_ge(score_ps[p], ONE + n + 1)
                if back(i, g, 2, first):
                    j, k = back(i, g, 2)
                    dve.wait_ge(hidL_ready[k % 4], ONE + j * QC + k // 4 + 1)
                dve.tensor_tensor(hid[p][:, :], gated[p][:, :], psF[p][:, :], ALU.mult).then_inc(hid_ready[p], 1)

            def low_part(i, g):
                p, q, m = g % 2, g % 4, i * QC + g // 4
                dve.wait_ge(hidH_ready[q], ONE + m + 1)
                dve.wait_ge(down_done[q], ONE + m)
                dve.tensor_tensor(hidL[q][:, :], hid[p][:, :], hidH[q][:, :].bitcast(F32),
                                  ALU.subtract).then_inc(hidL_ready[q], 1)

            def invert(i, h):
                dve.wait_ge(den_ps[h], ONE + i + 1)
                dve.wait_ge(rden_done[h], ONE + i)
                dve.tensor_scalar(den[h][:, :], psT[:, 0:2 * TT:2], DEN_EPS, None,
                                  ALU.add).then_inc(den_done[h], 1)
                dve.wait_ge(den_done[h], ONE + i + 1)
                dve.wait_ge(y_ready[h], ONE + TT * i)
                dve.reciprocal(rden[h][:, :], den[h][:, :]).then_inc(rden_done[h], 1)

            def finish(i, h):
                dve.wait_ge(oTT_ps[h], ONE + i + 1)
                dve.wait_ge(rden_done[h], ONE + i + 1)
                dve.wait_ge(xr_in[h], 16 * i + 16)
                for j in range(TT):
                    dve.scalar_tensor_tensor(xr[h][:, j, :], psT[:, j * P:(j + 1) * P], rden[h][:, j:j + 1],
                                             xr[h][:, j, :], ALU.mult, ALU.add).then_inc(y_ready[h], 1)

            def step(i, g, first):
                h, c = g // CH, g % CH
                before = batch_before(i, h, first)
                gate(i, g)
                if back(i, g, 1, first):
                    j, k = back(i, g, 1)
                    weigh(j, k, first)
                if back(i, g, 2, first):
                    low_part(*back(i, g, 2))
                if c == TURN + 1 and before:
                    finish(*before)
                if c == SUMS + 2:
                    invert(i, h)

            run_pairs(dve, step)
            weigh(HB - 1, 2 * CH - 1)
            low_part(HB - 1, 2 * CH - 2)
            low_part(HB - 1, 2 * CH - 1)
            finish(HB - 1, 1)


def build(nc, a, out):
    with ExitStack() as ctx:
        def sb(name, shape, dt=F32):
            return ctx.enter_context(nc.sbuf_tensor(name, shape, dt))

        cst = sb("cst", [P, C_SEL])
        par = sb("par", [P, V_END + 1])
        st = sb("st", [P, NT, 6])
        score = sb("score", [P, HALF])
        xsave = nc.dram_tensor("xsave", [P, NT, P], F32).ap()
        tables_in = ctx.enter_context(nc.semaphore("tables_in"))
        eps_set = ctx.enter_context(nc.semaphore("eps_set"))
        with nc.Block() as block:
            @block.sync
            def _(sp):
                sp.dma_start(cst[:, :], a["cst"][:, 0:C_SEL]).then_inc(tables_in, 16)
                sp.dma_start(par[:, 0:V_END], a["par"]).then_inc(tables_in, 16)
                sp.wait_ge(tables_in, 32)

            @block.gpsimd
            def _(pool):
                pool.memset(par[:, V_END:V_END + 1], LN_EPS).then_inc(eps_set, 1)
                pool.wait_ge(eps_set, 1)

        with nc.sbuf_tensor("xres", [P, NT, P], F32, side="right") as xres:
            attention_phase(nc, a["x"], a["wqT"], a["wkvT"], a["wpT"], a["bp"], cst, par, xres, st)
            xH = sb("xH", [P, TOK], F32R)
            xL = sb("xL", [P, TOK], F32R)
            router_phase(nc, a["wr"], a["br"], cst, par, xres, st, xH, xL, score, xsave)
        wU = sb("wU", [P, 2, E * H], F32R)
        wG = sb("wG", [P, 2, E * H], F32R)
        wD = sb("wD", [P, 2, CH * P], F32R)
        selR = sb("selR", [P, CH * P], F32R)
        bdR = sb("bdR", [P, 2, P], F32R)
        onesR = sb("onesR", [P, 2], F32R)
        with (nc.sbuf_tensor("w_stage", [P, E * H], F32) as w_stage,
              nc.sbuf_tensor("bd_stage", [P, P], F32) as bd_stage):
            routing_phase(nc, a["wupT"], a["wgateT"], a["wdn"], a["bdn"], a["cst"][:, C_SEL:C_END], cst, score,
                                 wU, wG, wD, selR, bdR, onesR, w_stage, bd_stage)
        experts_phase(nc, out, xsave, par, cst, score, xH, xL, wU, wG, wD, selR, bdR, onesR)


def constants():
    import numpy as np
    k, m = np.arange(P)[:, None], np.arange(P)[None, :]
    c = np.zeros((P, C_END), np.float32)
    c[:, C_ID:C_ID + P] = k == m
    c[:, C_BLOCK:C_BLOCK + P] = k // HD == m // HD
    c[:, C_ONES:C_ONES + P] = 1.0
    c[:, C_PAIR:C_PAIR + P] = k % E == m % E
    c[:, C_IOTA:C_IOTA + P] = m
    c[:, C_TRI:C_TRI + E] = k < m[:, :E]
    c[:, C_HEAD:C_HEAD + HEADS] = k // HD == m[:, :HEADS]
    for n in range(CH):
        c[:, C_SEL + n * P:C_SEL + (n + 1) * P] = k % E == n * EPC + m // H
    return c


def kernel(**inputs):
    import numpy as np
    import concourse.bacc as bacc
    from concourse.bass_utils import run_bass_kernel_spmd

    v = {k: np.asarray(x) for k, x in inputs.items()}
    attn = lambda k: v["L0_attn_" + k]
    ffn = lambda k: v["L0_ffn_" + k]
    cols = lambda b: b.reshape(CH, P).T
    arrays = {
        "x": attn("x"),
        "wqT": attn("Wq").T,
        "wkvT": np.concatenate([attn("Wk").T, attn("Wv").T], axis=1),
        "wpT": attn("Wp").T,
        "bp": np.tile(attn("bp"), TT).reshape(1, SEQ),
        "wr": ffn("Wr"),
        "br": ffn("br"),
        "wupT": ffn("Wup").transpose(1, 0, 2).reshape(P, E * H),
        "wgateT": ffn("Wgate").transpose(1, 0, 2).reshape(P, E * H),
        "wdn": ffn("Wdown").reshape(CH, P, P).transpose(1, 0, 2).reshape(P, CH * P),
        "bdn": ffn("bdown"),
        "par": np.concatenate([attn("conv_w"), attn("conv_b").reshape(P, 1),
                               cols(ffn("bup")), cols(ffn("bgate"))], axis=1),
        "cst": constants(),
    }
    arrays = {k: np.ascontiguousarray(x) for k, x in arrays.items()}
    nc = bacc.Bacc("TRN2", target_bir_lowering=False, num_devices=1)
    aps = {k: nc.dram_tensor(k + "_dram", x.shape, F32, kind="ExternalInput").ap() for k, x in arrays.items()}
    out = nc.dram_tensor("out_dram", (BATCH, SEQ, P), F32, kind="ExternalOutput").ap()
    build(nc, aps, out)
    res = run_bass_kernel_spmd(nc, [{k + "_dram": x for k, x in arrays.items()}], core_ids=[0])
    return res.results[0]["out_dram"]
```
